# Optimizing a Trainium2 kernel written in Bass

```python
import numpy as np
import jax
import jax.numpy as jnp

def _softmax(x, axis=-1):
    return jax.nn.softmax(x, axis=axis)

def _gelu(x):
    return jax.nn.gelu(x, approximate=True)

def _silu(x):
    return jax.nn.silu(x)

def _sigmoid(x):
    return jax.nn.sigmoid(x)

def _layernorm(x, axis=-1, eps=1e-05):
    m = jnp.mean(x, axis=axis, keepdims=True)
    v = jnp.var(x, axis=axis, keepdims=True)
    return (x - m) / jnp.sqrt(v + eps)

def _scatter_add(tgt, idx, src, axis=0):
    return tgt.at[idx].add(src)

def _segment_sum(src, seg, n):
    return jax.ops.segment_sum(src, seg, n)
kernel_name = 'mk_xattn_ffn_d1_seqx_r8_3c3926'

def setup_inputs(seed: int=0):
    np.random.seed(seed)
    _w = jnp.asarray

    def _rec_inputs():
        import jax
        import jax.numpy as jnp
        _rk = jax.random.key(seed)
        x = -0.0003929 + 0.9999 * jax.random.normal(jax.random.fold_in(_rk, 1), (32, 64, 512), jnp.float32)
        _lenS = 64 - jax.random.randint(jax.random.fold_in(_rk, 7), (32,), 0, max(1, 64 // 4) + 1, jnp.int32)
        _lenS2 = 64 - jax.random.randint(jax.random.fold_in(_rk, 8), (32,), 0, max(1, 64 // 4) + 1, jnp.int32)
        _ctx_4096P = jax.random.normal(jax.random.fold_in(_rk, 11), (32, 16, 512), jnp.float32)
        _ctx_4096c = jax.random.dirichlet(jax.random.fold_in(_rk, 511), 0.3 * jnp.ones((16,), jnp.float32), (32, 64))
        _ctx_4096t = jnp.einsum('bsk,bkd->bsd', _ctx_4096c, _ctx_4096P)
        _ctx_4096t = _ctx_4096t * jax.lax.rsqrt(jnp.mean(jnp.square(_ctx_4096t)) + 1e-12) * 0.953939
        ctx_4096 = 2.81802e-05 + 1.00001 * (_ctx_4096t + 0.3 * jax.random.normal(jax.random.fold_in(_rk, 611), (32, 64, 512), jnp.float32))
        pos_BxS2 = jnp.broadcast_to(jnp.arange(64, dtype=jnp.int32), (32, 64))
        _validS = jnp.arange(64)[None, :] < _lenS[:, None]
        _validS2 = jnp.arange(64)[None, :] < _lenS2[:, None]
        _causal = jnp.tril(jnp.ones((64, 64), dtype=bool))
        mask_BxSxS2_ik0 = jnp.where(jnp.broadcast_to(_validS2[:, None, :], (32, 64, 64)), 0, 1).astype(jnp.int32)
        return (x, ctx_4096, pos_BxS2, mask_BxSxS2_ik0)
    x, ctx_4096, pos_BxS2, mask_BxSxS2_ik0 = _rec_inputs()

    def _L0_xattn_setup():
        import jax, jax.numpy as jnp
        import numpy as np
        B, S, E = (2, 256, 512)
        H, KVH, D = (32, 8, 128)
        GROUPS = H // KVH
        MAX_POS = 512
        ROPE_THETA = 10000.0

        def _rope_tables(max_pos, dim, theta):
            inv_freq = 1.0 / theta ** (jnp.arange(0, dim, 2, dtype=jnp.float32) / dim)
            t = jnp.arange(max_pos, dtype=jnp.float32)
            freqs = jnp.einsum('i,j->ij', t, inv_freq)
            emb = jnp.concatenate([freqs, freqs], axis=-1)
            return (jnp.cos(emb), jnp.sin(emb))

        def _rotate_half(x):
            x1, x2 = (x[..., :x.shape[-1] // 2], x[..., x.shape[-1] // 2:])
            return jnp.concatenate([-x2, x1], axis=-1)
        key = jax.random.key(seed)
        ks = jax.random.split(key, 8)
        scale_w = 1.0 / np.sqrt(E)
        query = jax.random.normal(ks[0], (B, S, E), dtype=jnp.float32)
        k_in = jax.random.normal(ks[1], (B, S, E), dtype=jnp.float32)
        v_in = jax.random.normal(ks[2], (B, S, E), dtype=jnp.float32)
        position_ids = jnp.broadcast_to(jnp.arange(S, dtype=jnp.int64), (B, S))
        src_mask = jnp.tril(jnp.ones((S, S), dtype=jnp.int32))
        src_mask = jnp.broadcast_to(src_mask, (B, S, S))
        Wq = jax.random.normal(ks[3], (E, H * D), dtype=jnp.float32) * scale_w
        Wk = jax.random.normal(ks[4], (E, KVH * D), dtype=jnp.float32) * scale_w
        Wv = jax.random.normal(ks[5], (E, KVH * D), dtype=jnp.float32) * scale_w
        Wo = jax.random.normal(ks[6], (H * D, E), dtype=jnp.float32) * scale_w
        return {'query': query, 'key': k_in, 'value': v_in, 'position_ids': position_ids, 'src_mask': src_mask, 'Wq': Wq, 'Wk': Wk, 'Wv': Wv, 'Wo': Wo}
    _L0_xattn_all = _L0_xattn_setup()
    _L0_xattn_in = {k: v for k, v in _L0_xattn_all.items() if k in ('Wq', 'Wk', 'Wv', 'Wo')}
    del _L0_xattn_all

    def _L0_ffn_setup():
        import jax, jax.numpy as jnp
        import numpy as np
        _TRIPLES = [(1, 2, 3), (1, 4, 5), (1, 7, 6), (2, 4, 6), (2, 5, 7), (3, 4, 7), (3, 6, 5)]

        def _oct_struct():
            S = np.zeros((8, 8, 8), np.float32)
            S[0, 0, 0] = 1.0
            for i in range(1, 8):
                S[0, i, i] = 1.0
                S[i, 0, i] = 1.0
                S[i, i, 0] = -1.0
            for a, b, c in _TRIPLES:
                for x, y, z in ((a, b, c), (b, c, a), (c, a, b)):
                    S[x, y, z] = 1.0
                    S[y, x, z] = -1.0
            return jnp.asarray(S)
        S_OCT = _oct_struct()
        N_EMBD = 512
        HIDDEN = 1366

        def ternary_dequant(W):
            scale = jnp.mean(jnp.abs(W))
            Wq = scale * jnp.clip(jnp.round(W / scale), -1.0, 1.0)
            return W + jax.lax.stop_gradient(Wq - W)

        def oct_ternary_linear(xp, W):
            Wq = ternary_dequant(W)
            M = jnp.einsum('jik,jod->koid', S_OCT, Wq)
            return jnp.einsum('...id,koid->...ko', xp, M)
        key = jax.random.key(seed)
        k1, k2, k3, k4 = jax.random.split(key, 4)
        B, T = (2, 256)
        d8, h8 = (N_EMBD // 8, HIDDEN // 8)
        std_in = 1.0 / np.sqrt(N_EMBD)
        std_h = 1.0 / np.sqrt(HIDDEN)
        return {'x': jax.random.normal(k1, (B, T, N_EMBD), jnp.float32), 'w_gate': jax.random.normal(k2, (8, h8, d8), jnp.float32) * std_in, 'w_up': jax.random.normal(k3, (8, h8, d8), jnp.float32) * std_in, 'w_down': jax.random.normal(k4, (8, d8, h8), jnp.float32) * std_h}
    _L0_ffn_all = _L0_ffn_setup()
    _L0_ffn_in = {k: v for k, v in _L0_ffn_all.items() if k in ('w_gate', 'w_up', 'w_down')}
    del _L0_ffn_all
    return {'x': x, 'ctx_4096': ctx_4096, 'pos_BxS2': pos_BxS2, 'mask_BxSxS2_ik0': mask_BxSxS2_ik0, 'L0_xattn_Wq': _L0_xattn_in['Wq'], 'L0_xattn_Wk': _L0_xattn_in['Wk'], 'L0_xattn_Wv': _L0_xattn_in['Wv'], 'L0_xattn_Wo': _L0_xattn_in['Wo'], 'L0_ffn_w_gate': _L0_ffn_in['w_gate'], 'L0_ffn_w_up': _L0_ffn_in['w_up'], 'L0_ffn_w_down': _L0_ffn_in['w_down']}

def reference(x, ctx_4096, pos_BxS2, mask_BxSxS2_ik0, L0_xattn_Wq, L0_xattn_Wk, L0_xattn_Wv, L0_xattn_Wo, L0_ffn_w_gate, L0_ffn_w_up, L0_ffn_w_down):
    import jax
    import jax.numpy as jnp

    def _L0_xattn_ref(query, key, value, position_ids, src_mask, Wq, Wk, Wv, Wo):
        import jax, jax.numpy as jnp
        import numpy as np
        B, S, E = (2, 256, 512)
        H, KVH, D = (32, 8, 128)
        GROUPS = H // KVH
        MAX_POS = 512
        ROPE_THETA = 10000.0

        def _rope_tables(max_pos, dim, theta):
            inv_freq = 1.0 / theta ** (jnp.arange(0, dim, 2, dtype=jnp.float32) / dim)
            t = jnp.arange(max_pos, dtype=jnp.float32)
            freqs = jnp.einsum('i,j->ij', t, inv_freq)
            emb = jnp.concatenate([freqs, freqs], axis=-1)
            return (jnp.cos(emb), jnp.sin(emb))

        def _rotate_half(x):
            x1, x2 = (x[..., :x.shape[-1] // 2], x[..., x.shape[-1] // 2:])
            return jnp.concatenate([-x2, x1], axis=-1)
        nb, q_len, _ = query.shape
        q = (query @ Wq).reshape(nb, q_len, H, D).transpose(0, 2, 1, 3)
        k = (key @ Wk).reshape(nb, q_len, KVH, D).transpose(0, 2, 1, 3)
        v = (value @ Wv).reshape(nb, q_len, KVH, D).transpose(0, 2, 1, 3)
        cos_t, sin_t = _rope_tables(MAX_POS, D, ROPE_THETA)
        cos = cos_t[position_ids][:, None]
        sin = sin_t[position_ids][:, None]
        q = q * cos + _rotate_half(q) * sin
        k = k * cos + _rotate_half(k) * sin
        k = jnp.repeat(k, GROUPS, axis=1)
        v = jnp.repeat(v, GROUPS, axis=1)
        scores = jnp.einsum('bhqd,bhkd->bhqk', q, k) / jnp.sqrt(jnp.float32(D))
        mask = src_mask[:, None]
        scores = jnp.where(mask == 0, jnp.float32(-1000000000.0), scores)
        attn = jax.nn.softmax(scores, axis=-1)
        x = jnp.einsum('bhqk,bhkd->bhqd', attn, v)
        x = x.transpose(0, 2, 1, 3).reshape(nb, q_len, H * D)
        return x @ Wo

    def _L0_ffn_ref(x, w_gate, w_up, w_down):
        import jax, jax.numpy as jnp
        import numpy as np
        _TRIPLES = [(1, 2, 3), (1, 4, 5), (1, 7, 6), (2, 4, 6), (2, 5, 7), (3, 4, 7), (3, 6, 5)]

        def _oct_struct():
            S = np.zeros((8, 8, 8), np.float32)
            S[0, 0, 0] = 1.0
            for i in range(1, 8):
                S[0, i, i] = 1.0
                S[i, 0, i] = 1.0
                S[i, i, 0] = -1.0
            for a, b, c in _TRIPLES:
                for x, y, z in ((a, b, c), (b, c, a), (c, a, b)):
                    S[x, y, z] = 1.0
                    S[y, x, z] = -1.0
            return jnp.asarray(S)
        S_OCT = _oct_struct()
        N_EMBD = 512
        HIDDEN = 1366

        def ternary_dequant(W):
            scale = jnp.mean(jnp.abs(W))
            Wq = scale * jnp.clip(jnp.round(W / scale), -1.0, 1.0)
            return W + jax.lax.stop_gradient(Wq - W)

        def oct_ternary_linear(xp, W):
            Wq = ternary_dequant(W)
            M = jnp.einsum('jik,jod->koid', S_OCT, Wq)
            return jnp.einsum('...id,koid->...ko', xp, M)
        B, T, D = x.shape
        xp = x.reshape(B, T, 8, D // 8)
        gate = oct_ternary_linear(xp, w_gate).reshape(B, T, -1)
        up = oct_ternary_linear(xp, w_up).reshape(B, T, -1)
        h = jax.nn.silu(gate) * up
        hp = h.reshape(B, T, 8, h.shape[-1] // 8)
        out = oct_ternary_linear(hp, w_down).reshape(B, T, D)
        return out
    x = x + _L0_xattn_ref(_layernorm(x, axis=-1), ctx_4096, ctx_4096, pos_BxS2, mask_BxSxS2_ik0, L0_xattn_Wq, L0_xattn_Wk, L0_xattn_Wv, L0_xattn_Wo)
    x = x + _L0_ffn_ref(_layernorm(x, axis=-1), L0_ffn_w_gate, L0_ffn_w_up, L0_ffn_w_down)
    return x

_drawn_inputs = setup_inputs


def setup_inputs(seed=0):
    import zlib

    import numpy as np

    out = dict(_drawn_inputs(seed))
    spreads = {}
    factors = {}
    for name, (base, spread) in spreads.items():
        noise = np.random.default_rng([zlib.crc32(name.encode()), seed]).standard_normal(out[name].shape)
        drawn = base * np.exp(spread * noise) if base else spread * noise
        out[name] = jnp.asarray(drawn.astype(out[name].dtype))
    for name, factor in factors.items():
        out[name] = (out[name] * factor).astype(out[name].dtype)
    return out
```

```python
from contextlib import ExitStack

import concourse.bass as bass
from concourse import mybir

F32 = mybir.dt.float32
F16 = mybir.dt.float16
I32 = mybir.dt.int32
U8 = mybir.dt.uint8
ALU = mybir.AluOpType
ACT = mybir.ActivationFunctionType
AX = mybir.AxisListType
REDUCE = bass.bass_isa.ReduceOp

P = 128
BATCH, SEQ, EMB = 32, 64, 512
TOKENS = BATCH * SEQ
HEADS, KV_HEADS, HEAD_DIM = 32, 8, 128
GROUP = HEADS // KV_HEADS
MAX_POS, THETA = 512, 10000.0
EPS = 1e-5
KT = EMB // P
TILES = TOKENS // P
SPAN = 512
SPANS = TOKENS // SPAN
SPAN_TILES = SPAN // P
SPAN_BATCHES = SPAN // SEQ
GCOLS = GROUP * HEAD_DIM

OCT = 8
HID8, EMB8 = 170, EMB // OCT
HIDDEN = OCT * HID8
HCHUNKS = -(-HIDDEN // P)
HLAST = HIDDEN - (HCHUNKS - 1) * P
FFN_COUNT = float(OCT * HID8 * EMB8)

MASKED = -1.0e9
XN_SCALE = 128.0
TOP = 2.0 ** 11
V_SCALE = 2.0 ** -18
H_SCALE = 2.0 ** -4
TINY = 1e-30
EXP_BITS = 0x7F800000

_TRIPLES = [(1, 2, 3), (1, 4, 5), (1, 7, 6), (2, 4, 6), (2, 5, 7), (3, 4, 7), (3, 6, 5)]


def octonion_signs():
    s = {(0, 0): (0, 1)}
    for i in range(1, OCT):
        s[(0, i)] = (i, 1)
        s[(i, 0)] = (i, 1)
        s[(i, i)] = (0, -1)
    for a, b, c in _TRIPLES:
        for x, y, z in ((a, b, c), (b, c, a), (c, a, b)):
            s[(x, y)] = (z, 1)
            s[(y, x)] = (z, -1)
    sign = [[0] * OCT for _ in range(OCT)]
    for (j, i), (k, v) in s.items():
        assert j == i ^ k
        sign[i][k] = v
    return sign


SIGN = octonion_signs()


def at_least(eng, sem, value):
    if isinstance(value, int) and value <= 0:
        return
    eng.wait_ge(sem, value)


class Chain:

    def __init__(self, eng, sem):
        self.eng, self.sem, self.base, self.n = eng, sem, 0, 0

    def step(self, ins):
        ins.then_inc(self.sem, 1)
        self.n += 1
        self.eng.wait_ge(self.sem, self.base + self.n)


class Net:
    pass


def prepare(nc, N):
    with ExitStack() as ctx:
        def sb(name, shape, dt):
            return ctx.enter_context(nc.sbuf_tensor(name, shape, dt))

        def sem(name):
            return N.sems.enter_context(nc.semaphore(name))

        ctx_both = sb("ctx_both", [P, 2, SPAN_TILES, EMB], F32)
        ctx_raw = [ctx_both[:, s, :, :] for s in range(2)]
        normed = [sb(f"normed{j}", [P, EMB], F32) for j in range(2)]
        stats = sb("stats", [P, SPAN_TILES, 6], F32)
        mean_var = sb("mean_var", [P, SPAN_TILES, 2], F32)
        std = sb("std", [P, SPAN_TILES], F32)
        rstd = sb("rstd", [P, SPAN_TILES], F32)
        cmax = sb("cmax", [P, 1], F32)
        cmax_all = sb("cmax_all", [P, 1], F32)
        cpow = sb("cpow", [P, 1], F32)
        pos = sb("pos", [P, TILES], I32)
        pos_wrap = sb("pos_wrap", [P, TILES], I32)
        rope_rows = [sb(f"rope_rows{s}", [P, 2 * HEAD_DIM], F32) for s in range(4)]
        mask_raw = sb("mask_raw", [P, BATCH, SEQ], I32)
        w_nat = [sb(f"w_nat{w}", [P, HCHUNKS, EMB8], F32) for w in range(2)]
        wd_nat = sb("wd_nat", [P, OCT, HID8], F32)
        low = sb("low", [P, OCT * HID8], F16)
        tern = [sb(f"tern{w}", [P, HCHUNKS, 2, EMB8], F16) for w in range(2)]
        tern_t = [sb(f"tern_t{w}", [P, HCHUNKS * P], F16) for w in range(2)]
        ternd = sb("ternd", [P, OCT, HID8], F16)
        m_in = sb("m_in", [P, KT, HIDDEN], F16)
        down_rows = sb("down_rows", [P, 4, HIDDEN], F16)
        wsum = sb("wsum", [P, 3], F32)
        wsum_all = sb("wsum_all", [P, 3], F32)
        half = sb("half", [P, 3], F32)
        nhalf = sb("nhalf", [P, 3], F32)
        spow = sb("spow", [P, 3], F32)
        ident16 = sb("ident16", [P, P], F16)

        turn = [ctx.enter_context(nc.psum_tensor(f"turn{i}", [P, KT, P], F32)) for i in range(4)]
        rope_ps = [ctx.enter_context(nc.psum_tensor(f"rope_ps{i}", [P, 2, P], F32)) for i in range(2)]
        tern_ps = [ctx.enter_context(nc.psum_tensor(f"tern_ps{i}", [P, 8 * P], F16)) for i in range(2)]

        ident_zero, ident_in, ident16_in = sem("ident_zero"), sem("ident_in"), sem("ident16_in")
        pos_in, mask_in, wffn_in = sem("pos_in"), sem("mask_in"), sem("wffn_in")
        ctx_in = [sem(f"ctx_in{s}") for s in range(2)]
        x_in = [sem(f"x_in{s}") for s in range(2)]
        pad_zero = sem("pad_zero")
        dve_step = sem("p_dve_step")
        pos_ready, rows_in, rows_turned, rows_out = sem("pos_ready"), [sem(f"rows_in{s}") for s in range(4)], sem("rows_turned"), sem("rows_out")
        pred_ready = sem("pred_ready")
        cmax_ready, cmax_reduced, cscale_ready = sem("cmax_ready"), sem("cmax_reduced"), sem("cscale_ready")
        var_ready, std_ready, normed_ready = sem("var_ready"), sem("std_ready"), sem("normed_ready")
        turned, hi_ready, lo_ready = sem("turned"), sem("p_hi_ready"), sem("p_lo_ready")
        wsum_ready, wsum_reduced = sem("wsum_ready"), sem("wsum_reduced")
        tern_ready, tern_turned, tern_out = sem("tern_ready"), sem("tern_turned"), sem("tern_out")
        m_part, m_stored = sem("m_part"), sem("m_stored")
        down_ready, down_turned, down_out, down_stored = sem("down_ready"), sem("down_turned"), sem("down_out"), sem("down_stored")
        m_down = ctx_both[:, :, :, :].rearrange("p s a b -> p (s a b)").bitcast(F16)

        def expand_in(eng, w, hf):
            rows = slice(EMB8 * hf, EMB8 * hf + EMB8)
            for kt in range(KT):
                i = 2 * kt + hf
                for k in range(OCT):
                    j = i ^ k
                    ins = eng.tensor_scalar(m_in[rows, kt, k * HID8:(k + 1) * HID8],
                                            tern_t[w][rows, j * HID8:(j + 1) * HID8],
                                            float(SIGN[i][k]), None, ALU.mult)
            return ins

        def ternary(dve, chain):
            dve.wait_ge(wffn_in, 16 * 6)
            for w in range(2):
                dve.tensor_reduce(wsum[:, w:w + 1], w_nat[w][:, :, :], AX.XY, ALU.add, apply_absolute_value=True)
            dve.tensor_reduce(wsum[:, 2:3], wd_nat[:, :, :], AX.XY, ALU.add, apply_absolute_value=True).then_inc(wsum_ready, 1)
            dve.wait_ge(wsum_reduced, 1)
            chain.step(dve.tensor_scalar(N.ffn_scale[:, 0:2], wsum_all[:, 0:2], 1.0 / FFN_COUNT, None, ALU.mult))
            chain.step(dve.tensor_scalar(N.ffn_scale[:, 2:3], wsum_all[:, 2:3], 0.5 / FFN_COUNT, None, ALU.mult))
            dve.tensor_scalar(half[:, :], N.ffn_scale[:, :], 0.5, None, ALU.mult)
            chain.step(dve.tensor_scalar(nhalf[:, :], N.ffn_scale[:, :], -0.5, None, ALU.mult))
            for w in range(2):
                a = low[:, 0:HCHUNKS * EMB8].rearrange("p (c d) -> p c d", c=HCHUNKS) if HCHUNKS * EMB8 <= OCT * HID8 else None
                chain.step(dve.tensor_scalar(a, w_nat[w][:, :, :], nhalf[:, w:w + 1], None, ALU.is_lt))
                for copy in range(2):
                    ins = dve.scalar_tensor_tensor(out=tern[w][:, :, copy, :], in0=w_nat[w][:, :, :], scalar=half[:, w:w + 1],
                                                   in1=a, op0=ALU.is_gt, op1=ALU.subtract)
                chain.step(ins)
                dve.tensor_copy(cpow[:, :], half[:, 0:1]).then_inc(tern_ready, 1)
            b = low[:, :].rearrange("p (j d) -> p j d", j=OCT)
            chain.step(dve.tensor_scalar(b, wd_nat[:, :, :], nhalf[:, 2:3], None, ALU.is_lt))
            chain.step(dve.scalar_tensor_tensor(out=ternd[:, :, :], in0=wd_nat[:, :, :], scalar=half[:, 2:3], in1=b,
                                                op0=ALU.is_gt, op1=ALU.subtract))
            chain.step(dve.tensor_scalar(spow[:, 0:1], N.ffn_scale[:, 0:1], TINY, None, ALU.max))
            chain.step(dve.tensor_scalar(spow[:, 1:2].bitcast(I32), spow[:, 0:1].bitcast(I32), EXP_BITS, None, ALU.bitwise_and))
            chain.step(dve.reciprocal(spow[:, 2:3], spow[:, 1:2]))
            chain.step(dve.tensor_scalar(N.ffn_factor[:, 0:1], N.ffn_scale[:, 0:1], 1.0 / XN_SCALE, None, ALU.mult))
            chain.step(dve.tensor_scalar(N.ffn_factor[:, 1:2], spow[:, 2:3], H_SCALE / XN_SCALE, None, ALU.mult))
            chain.step(dve.tensor_tensor(spow[:, 0:1], spow[:, 1:2], N.ffn_scale[:, 1:2], ALU.mult))
            chain.step(dve.tensor_scalar(N.ffn_factor[:, 2:3], spow[:, 0:1], N.ffn_scale[:, 2:3], 1.0 / H_SCALE, ALU.mult, ALU.mult))

        block = ctx.enter_context(nc.Block())

        @block.sync
        def _(sp):
            sp.dma_start(pos[:, :], N.pos.rearrange("b s -> (b s)").rearrange("(i p) -> p i", p=P),
                         allow_slow_non_contiguous=True).then_inc(pos_in, 16)

            def load_tokens(s, half_index):
                if s == 0 and isinstance(half_index, int):
                    pass
                rows = (half_index * 2 + s) * SPAN
                sp.dma_start(ctx_raw[s][:, :, :], N.ctx[bass.ds(rows, SPAN), :].rearrange("(j p) e -> p j e", p=P)).then_inc(ctx_in[s], 16)
                sp.dma_start(N.acc[:, bass.ds((half_index * 2 + s) * SPAN_TILES, SPAN_TILES), :],
                             N.x[bass.ds(rows, SPAN), :].rearrange("(j p) e -> p j e", p=P)).then_inc(x_in[s], 16)

            load_tokens(0, 0)
            load_tokens(1, 0)
            sp.wait_ge(pad_zero, 1)
            full = (HCHUNKS - 1) * P
            for w, dram in enumerate((N.w_gate, N.w_up)):
                rows = dram.rearrange("j o d -> (j o) d")
                sp.dma_start(w_nat[w][:, 0:HCHUNKS - 1, :], rows[0:full, :].rearrange("(c p) d -> p c d", p=P)).then_inc(wffn_in, 16)
                sp.dma_start(w_nat[w][0:HLAST, HCHUNKS - 1, :], rows[full:HIDDEN, :]).then_inc(wffn_in, 16)
            for half_rows in range(2):
                sp.dma_start(wd_nat[64 * half_rows:64 * half_rows + 64, :, :], N.w_down.rearrange("j o d -> o j d")).then_inc(wffn_in, 16)
            for half_rows in range(2):
                sp.dma_start(mask_raw[64 * half_rows:64 * half_rows + 64, :, :], N.mask.rearrange("b q k -> q b k")).then_inc(mask_in, 16)
            for s in range(2):
                sp.wait_ge(lo_ready, 8 * (s + 1))
                load_tokens(s, 1)
            for w in range(2):
                sp.wait_ge(m_part, 2 * (w + 1))
                sp.dma_start(N.m_dram[w], m_in[:, :, :].rearrange("p k h -> p (k h)")).then_inc(m_stored, 16)
            sp.wait_ge(down_out, HCHUNKS)
            sp.dma_start(N.m_dram[2][:, 0:HCHUNKS * EMB], m_down[:, 0:HCHUNKS * EMB]).then_inc(down_stored, 16)
            sp.wait_ge(m_stored, 32)
            sp.wait_ge(down_stored, 16)

        @block.gpsimd
        def _(pool):
            pool.memset(N.ident[:, :], 0.0).then_inc(ident_zero, 1)
            pool.wait_ge(ident_zero, 1)
            pool.affine_select(out=N.ident[:, :], in_=N.ident[:, :], compare_op=ALU.not_equal, fill=1.0,
                               base=0, pattern=[[-1, P]], channel_multiplier=1).then_inc(ident_in, 1)
            pool.wait_ge(pos_ready, 1)
            for i in range(TILES):
                if i >= 4:
                    pool.wait_ge(rows_turned, i - 3)
                pool.indirect_dma_start(rope_rows[i % 4][:, :], None, N.rope_table,
                                        bass.IndirectOffsetOnAxis(pos[:, i:i + 1], 0)).then_inc(rows_in[i % 4], 16)
                if i == 11:
                    pool.wait_ge(wsum_ready, 1)
                    pool.partition_all_reduce(wsum_all[:, :], wsum[:, :], P, REDUCE.add).then_inc(wsum_reduced, 1)
                if i % SPAN_TILES == SPAN_TILES - 1:
                    pool.wait_ge(cmax_ready, i // SPAN_TILES + 1)
                    pool.partition_all_reduce(cmax_all[:, :], cmax[:, :], P, REDUCE.max).then_inc(cmax_reduced, 1)
            for w in range(2):
                pool.wait_ge(tern_out, 2 * w + 2)
                if w:
                    pool.wait_ge(m_stored, 16)
                expand_in(pool, w, 1).then_inc(m_part, 1)

        @block.scalar
        def _(act):
            def deviation(t):
                act.wait_ge(var_ready, t + 1)
                act.activation(std[:, :], mean_var[:, :, 1], ACT.Sqrt, scale=XN_SCALE ** -2,
                               bias=N.eps_tile[:, 0:1]).then_inc(std_ready, 1)

            def high(m, out, scale):
                act.wait_ge(turned, m + 1)
                act.activation(out, turn[m % 4][:, :, :], ACT.Copy, scale=scale).then_inc(hi_ready, 1)

            act.wait_ge(N.consts_ready, 1)
            for t in range(SPANS):
                deviation(t)
                act.wait_ge(cscale_ready, t + 1)
                for j in range(SPAN_TILES):
                    tile = SPAN_TILES * t + j
                    high(8 * t + j, N.c_hi[:, :, tile * P:(tile + 1) * P], N.c_scale[:, t:t + 1])
                for j in range(SPAN_TILES):
                    tile = SPAN_TILES * t + j
                    high(8 * t + 4 + j, N.x_hi[:, :, tile * P:(tile + 1) * P], 1.0)
                for i in range(SPAN_TILES * t, SPAN_TILES * (t + 1)):
                    act.wait_ge(rows_turned, i + 1)
                    act.activation(N.cos_t[:, i * P:(i + 1) * P], rope_ps[i % 2][:, 0, :], ACT.Copy)
                    act.activation(N.sin_t[:, i * P:(i + 1) * P], rope_ps[i % 2][:, 1, :], ACT.Copy).then_inc(rows_out, 1)
            for w in range(2):
                for part, (a, b) in enumerate(((0, 8), (8, HCHUNKS))):
                    act.wait_ge(tern_turned, 2 * w + part + 1)
                    act.activation(tern_t[w][:, a * P:b * P], tern_ps[part][:, 0:(b - a) * P], ACT.Copy).then_inc(tern_out, 1)
            for c in range(HCHUNKS):
                act.wait_ge(down_turned, c + 1)
                act.activation(m_down[:, c * EMB:(c + 1) * EMB], tern_ps[c % 2][:, 0:EMB], ACT.Copy).then_inc(down_out, 1)

        @block.vector
        def _(dve):
            chain = Chain(dve, dve_step)
            for w in range(2):
                last = dve.memset(w_nat[w][:, HCHUNKS - 1, :], 0.0)
            last.then_inc(pad_zero, 1)
            dve.memset(N.fill[:, :], MASKED)
            dve.memset(N.eps_tile[:, :], EPS / XN_SCALE ** 2).then_inc(N.consts_ready, 1)
            dve.wait_ge(pos_in, 16)
            chain.step(dve.tensor_scalar(pos_wrap[:, :], pos[:, :], 0.0, float(MAX_POS), ALU.is_lt, ALU.mult))
            chain.step(dve.tensor_tensor(pos_wrap[:, :], pos_wrap[:, :], pos[:, :], ALU.add))
            dve.tensor_scalar(pos[:, :], pos_wrap[:, :], 0.0, float(MAX_POS - 1), ALU.max, ALU.min).then_inc(pos_ready, 1)
            dve.wait_ge(ident_in, 1)
            dve.tensor_copy(ident16[:, :], N.ident[:, :]).then_inc(ident16_in, 1)

            def low_part(m, out, hi, scale):
                dve.wait_ge(hi_ready, m + 1)
                dve.scalar_tensor_tensor(out=out, in0=turn[m % 4][:, :, :], scalar=scale, in1=hi,
                                         op0=ALU.mult, op1=ALU.subtract).then_inc(lo_ready, 1)

            for t in range(SPANS):
                s = t % 2
                dve.wait_ge(ctx_in[s], 16 * (t // 2 + 1))
                if t:
                    dve.wait_ge(cmax_reduced, t)
                dve.tensor_reduce(cmax[:, :], ctx_raw[s][:, :, :], AX.XY, ALU.max,
                                  apply_absolute_value=True).then_inc(cmax_ready, 1)
                dve.wait_ge(x_in[s], 16 * (t // 2 + 1))
                for j in range(SPAN_TILES):
                    ins = dve.bn_stats(stats[:, j, :], N.acc[:, SPAN_TILES * t + j, :])
                chain.step(ins)
                if t:
                    dve.wait_ge(std_ready, t)
                for j in range(SPAN_TILES):
                    ins = dve.bn_aggr(mean_var[:, j, :], stats[:, j, :])
                ins.then_inc(var_ready, 1)
                dve.wait_ge(cmax_reduced, t + 1)
                pow2_scale(dve, chain, cmax_all[:, :], cpow[:, :], N.c_scale[:, t:t + 1], N.c_inv[:, t:t + 1], cscale_ready)
                dve.wait_ge(std_ready, t + 1)
                chain.step(dve.reciprocal(rstd[:, :], std[:, :]))
                for j in range(SPAN_TILES):
                    tile = SPAN_TILES * t + j
                    m = 8 * t + 4 + j
                    k = 8 * t + 4 + j - 2 if j >= 2 else 8 * (t - 1) + 4 + j + 2
                    if k > 0:
                        dve.wait_ge(turned, k + 1)
                    dve.tensor_scalar(normed[j % 2][:, :], N.acc[:, tile, :], mean_var[:, j, 0:1], rstd[:, j:j + 1],
                                      ALU.subtract, ALU.mult).then_inc(normed_ready, 1)
                    if j == 1:
                        for jj in range(SPAN_TILES):
                            ct = SPAN_TILES * t + jj
                            low_part(8 * t + jj, N.c_lo[:, :, ct * P:(ct + 1) * P], N.c_hi[:, :, ct * P:(ct + 1) * P],
                                     N.c_scale[:, t:t + 1])
                for j in range(SPAN_TILES):
                    tile = SPAN_TILES * t + j
                    low_part(8 * t + 4 + j, N.x_lo[:, :, tile * P:(tile + 1) * P], N.x_hi[:, :, tile * P:(tile + 1) * P], 1.0)
                if t == 1:
                    ternary(dve, chain)
            dve.wait_ge(mask_in, 32)
            dve.tensor_scalar(N.pred[:, :, :], mask_raw[:, :, :], 0.0, None, ALU.is_equal).then_inc(pred_ready, 1)
            for kp in range(4):
                for hf in range(2):
                    rows = slice(64 * hf, 64 * hf + 64)
                    k = 2 * kp + hf
                    for i in range(OCT):
                        ins = dve.tensor_scalar(down_rows[rows, kp, i * HID8:(i + 1) * HID8], ternd[rows, i ^ k, :],
                                                float(SIGN[i][k]), None, ALU.mult)
            ins.then_inc(down_ready, 1)
            for w in range(2):
                dve.wait_ge(tern_out, 2 * w + 2)
                if w:
                    dve.wait_ge(m_stored, 16)
                expand_in(dve, w, 0).then_inc(m_part, 1)

        @block.tensor
        def _(pe):
            pe.wait_ge(ident_in, 1)

            def turn_tile(m, src):
                if m >= 4:
                    pe.wait_ge(lo_ready, m - 3)
                for kt in range(KT):
                    ins = pe.transpose(turn[m % 4][:, kt, :], src[:, kt * P:(kt + 1) * P], N.ident[:, :])
                ins.then_inc(turned, 1)

            for t in range(SPANS):
                pe.wait_ge(ctx_in[t % 2], 16 * (t // 2 + 1))
                for j in range(SPAN_TILES):
                    turn_tile(8 * t + j, ctx_raw[t % 2][:, j, :])
                for j in range(SPAN_TILES):
                    pe.wait_ge(normed_ready, SPAN_TILES * t + j + 1)
                    turn_tile(8 * t + 4 + j, normed[j % 2])
                for i in range(SPAN_TILES * t, SPAN_TILES * (t + 1)):
                    pe.wait_ge(rows_in[i % 4], 16 * (i // 4 + 1))
                    if i >= 2:
                        pe.wait_ge(rows_out, i - 1)
                    for c in range(2):
                        ins = pe.transpose(rope_ps[i % 2][:, c, :], rope_rows[i % 4][:, c * P:(c + 1) * P], N.ident[:, :])
                    ins.then_inc(rows_turned, 1)
            pe.wait_ge(ident16_in, 1)
            for w in range(2):
                pe.wait_ge(tern_ready, w + 1)
                for part, (a, b) in enumerate(((0, 8), (8, HCHUNKS))):
                    if w:
                        pe.wait_ge(tern_out, part + 1)
                    for c in range(a, b):
                        ins = pe.transpose(tern_ps[part][:, (c - a) * P:(c - a + 1) * P],
                                           tern[w][:, c, :, :].rearrange("p a d -> p (a d)"), ident16[:, :])
                    ins.then_inc(tern_turned, 1)
            pe.wait_ge(down_ready, 1)
            for c in range(HCHUNKS):
                pe.wait_ge(tern_out, 4)
                if c >= 2:
                    pe.wait_ge(down_out, c - 1)
                rows = P if c < HCHUNKS - 1 else HLAST
                for kp in range(4):
                    ins = pe.transpose(tern_ps[c % 2][0:rows, kp * P:(kp + 1) * P],
                                       down_rows[:, kp, c * P:c * P + rows], ident16[:, :])
                ins.then_inc(down_turned, 1)


def pow2_scale(dve, chain, amax, tmp, scale, inverse, ready):
    chain.step(dve.tensor_scalar(tmp, amax, TINY, None, ALU.max))
    chain.step(dve.tensor_scalar(amax.bitcast(I32), tmp.bitcast(I32), EXP_BITS, None, ALU.bitwise_and))
    chain.step(dve.tensor_scalar(inverse, amax, 1.0 / TOP, None, ALU.mult))
    ins = dve.reciprocal(scale, inverse)
    if ready is None:
        chain.step(ins)
    else:
        ins.then_inc(ready, 1)


def attend(nc, N):
    with ExitStack() as ctx:
        def sb(name, shape, dt):
            return ctx.enter_context(nc.sbuf_tensor(name, shape, dt))

        def sem(name):
            return N.sems.enter_context(nc.semaphore(name))

        w_raw = sb("w_raw", [P, KT, GCOLS], F32)
        wk_raw = sb("wk_raw", [P, KT, HEAD_DIM], F32)
        wv_raw = sb("wv_raw", [P, KT, HEAD_DIM], F32)
        wq_hi, wq_lo = sb("wq_hi", [P, KT, GCOLS], F16), sb("wq_lo", [P, KT, GCOLS], F16)
        wk_hi, wk_lo = sb("wk_hi", [P, KT, HEAD_DIM], F16), sb("wk_lo", [P, KT, HEAD_DIM], F16)
        wv_hi, wv_lo = sb("wv_hi", [P, KT, HEAD_DIM], F16), sb("wv_lo", [P, KT, HEAD_DIM], F16)
        wo_hi, wo_lo = sb("wo_hi", [P, 2, GROUP, EMB], F16), sb("wo_lo", [P, 2, GROUP, EMB], F16)
        wmax, wmax_all = sb("wmax", [P, 4], F32), sb("wmax_all", [P, 4], F32)
        wtmp = sb("wtmp", [P, 4], F32)
        w_scale, w_inv = sb("w_scale", [P, 4], F32), sb("w_inv", [P, 4], F32)
        inv_q = sb("inv_q", [P, 2, 1], F32)
        inv_k = sb("inv_k", [P, 2, SPANS], F32)
        inv_y = sb("inv_y", [P, 2, SPANS], F32)
        k_sb = [sb(f"k_sb{i}", [P, SPAN], F32) for i in range(2)]
        v_sb = [sb(f"v_sb{i}", [P, SPAN_TILES, HEAD_DIM], F32) for i in range(2)]
        q_sb = [sb(f"q_sb{i}", [P, SPAN_BATCHES, 2, SEQ], F32) for i in range(2)]
        by_cos = [sb(f"by_cos{j}", [P, SPAN], F32) for j in range(2)]
        by_sin = [sb(f"by_sin{j}", [P, SPAN], F32) for j in range(2)]
        probs = [sb(f"probs{i}", [P, SPAN_BATCHES, SEQ], F32) for i in range(2)]
        probs_t = [sb(f"probs_t{i}", [P, SPAN_TILES, P], F32) for i in range(2)]
        neg_max = [sb(f"neg_max{i}", [P, SPAN_BATCHES], F32) for i in range(2)]
        row_sum = [sb(f"row_sum{i}", [P, SPAN_BATCHES], F32) for i in range(2)]
        row_inv = [sb(f"row_inv{i}", [P, SPAN_BATCHES], F32) for i in range(2)]
        o_hi = [sb(f"o_hi{i}", [P, GROUP, SPAN], F16) for i in range(2)]
        o_lo = [sb(f"o_lo{i}", [P, GROUP, SPAN], F16) for i in range(2)]

        def bank(name):
            return ctx.enter_context(nc.psum_tensor(name, [P, SPAN], F32))

        q_ps = [bank("q_ps0"), bank("q_ps1")]
        kv_ps = bank("kv_ps")
        s_ps = bank("s_ps")
        pair_ps = [bank("pair_ps0"), bank("pair_ps1")]
        y_ps = [bank("y_ps0"), bank("y_ps1")]

        raw_in, kv_in = sem("raw_in"), sem("kv_in")
        omax_ready, omax_reduced, oscale_ready = sem("omax_ready"), sem("omax_reduced"), sem("oscale_ready")
        qmax_ready, qmax_reduced, qscale_ready = sem("qmax_ready"), sem("qmax_reduced"), sem("qscale_ready")
        wo_hi_ready, wo_ready = sem("wo_hi_ready"), sem("wo_ready")
        wk_hi_ready, wk_ready = sem("wk_hi_ready"), sem("wk_ready")
        wv_hi_ready, wv_ready = sem("wv_hi_ready"), sem("wv_ready")
        wq_hi_ready, wq_ready = sem("wq_hi_ready"), sem("wq_ready")
        q_done, q_free = [sem("q_done0"), sem("q_done1")], [sem("q_free0"), sem("q_free1")]
        q_roped = sem("q_roped")
        k_done, k_free, k_roped = sem("k_done"), sem("k_free"), sem("k_roped")
        v_done, v_ready = sem("v_done"), sem("v_ready")
        s_done, filled, max_ready, exp_done, inv_ready, p_ready = (
            sem("s_done"), sem("filled"), sem("max_ready"), sem("exp_done"), sem("inv_ready"), sem("p_ready"))
        t_done, pt_ready = sem("t_done"), sem("pt_ready")
        pv_done, o_hi_ready, o_ready = sem("pv_done"), sem("o_hi_ready"), sem("o_ready")
        y_done, y_added = sem("y_done"), sem("y_added")
        dve_step = sem("a_dve_step")
        STEPS = 24

        wq_dram = N.wq.rearrange("(k p) n -> p k n", p=P)
        wk_dram = N.wk.rearrange("(k p) n -> p k n", p=P)
        wv_dram = N.wv.rearrange("(k p) n -> p k n", p=P)
        wo_dram = N.wo.rearrange("(h p) n -> p h n", p=P)

        block = ctx.enter_context(nc.Block())
        SLOTS = [(t, u) for t in range(SPANS) for u in range(2)]

        def groups(eng, body):
            body(0)
            with eng.Fori(1, KV_HEADS - 1) as g:
                body(g)
            body(KV_HEADS - 1)

        def is_last(g):
            return isinstance(g, int) and g == KV_HEADS - 1

        def o_view(buf, u, e):
            return buf[:, 2 * u:2 * u + 2, :].rearrange("p h (b e q) -> p e b h q", e=2, q=SEQ)[:, e, :, :, :]

        def o_psum(e):
            return pair_ps[1 - e][:, :].rearrange("p (b h q) -> p b h q", b=4, h=2)

        @block.sync
        def _(sp):
            def load(g):
                if not isinstance(g, int) or g:
                    sp.wait_ge(wq_ready, 2 * g)
                sp.dma_start(w_raw[:, :, :], wo_dram[:, bass.ds(g * GROUP, GROUP), :]).then_inc(raw_in, 16)
                if not isinstance(g, int) or g:
                    sp.wait_ge(wk_ready, g)
                    sp.wait_ge(wv_ready, g)
                sp.dma_start(wk_raw[:, :, :], wk_dram[:, :, bass.ds(g * HEAD_DIM, HEAD_DIM)]).then_inc(kv_in, 16)
                sp.dma_start(wv_raw[:, :, :], wv_dram[:, :, bass.ds(g * HEAD_DIM, HEAD_DIM)]).then_inc(kv_in, 16)
                sp.wait_ge(wo_ready, g + 1)
                sp.dma_start(w_raw[:, :, :], wq_dram[:, :, bass.ds(g * GCOLS, GCOLS)]).then_inc(raw_in, 16)

            load(0)
            with sp.Fori(1, KV_HEADS) as g:
                load(g)

        @block.gpsimd
        def _(pool):
            def reduce_o(g):
                pool.partition_all_reduce(wmax_all[:, 3:4], wmax[:, 3:4], P, REDUCE.max).then_inc(omax_reduced, 1)

            def reduce_qkv(g):
                pool.partition_all_reduce(wmax_all[:, 0:3], wmax[:, 0:3], P, REDUCE.max).then_inc(qmax_reduced, 1)

            def rotate_q(n):
                par = n[1]
                n = n[0]
                at_least(pool, s_done, n - 1)
                for j in range(2):
                    pool.wait_ge(q_free[j], n + 1)
                    pool.tensor_tensor(q_sb[par][:, :, j, :], by_cos[j][:, :].rearrange("p (b q) -> p b q", q=SEQ),
                                       by_sin[j][:, :].rearrange("p (b q) -> p b q", q=SEQ), ALU.add).then_inc(q_roped, 1)

            def rotate_k(tau, par):
                at_least(pool, s_done, 2 * (tau - 1))
                pool.wait_ge(k_free, tau + 1)
                pool.tensor_tensor(k_sb[par][:, :], by_cos[0][:, :], by_sin[0][:, :], ALU.add).then_inc(k_roped, 1)

            def normalize(n, u, maxima=None, count=None):
                if maxima is not None:
                    pool.wait_ge(maxima, count)
                pool.wait_ge(inv_ready, n + 1)
                pool.tensor_tensor(probs[u][:, :, :], probs[u][:, :, :],
                                   row_inv[u][:, :].unsqueeze(2).to_broadcast([P, SPAN_BATCHES, SEQ]),
                                   ALU.mult).then_inc(p_ready, 1)

            pool.wait_ge(omax_ready, 1)
            reduce_o(0)
            pool.wait_ge(qmax_ready, 1)
            reduce_qkv(0)
            rotate_k(0, 0)
            rotate_q((0, 0))

            def body(g):
                for slot, (t, u) in enumerate(SLOTS):
                    tau = 4 * g + t
                    n = 2 * tau + u
                    more = not is_last(g) or slot < 7
                    if more:
                        rotate_q((n + 1, 1 - u))
                    if u == 0 and not (is_last(g) and t == SPANS - 1):
                        rotate_k(tau + 1, (t + 1) % 2)
                    if is_last(g) or slot not in (2, 5):
                        normalize(n, u)
                    elif slot == 2:
                        normalize(n, u, omax_ready, g + 2)
                        reduce_o(g + 1)
                    else:
                        normalize(n, u, qmax_ready, g + 2)
                        reduce_qkv(g + 1)

            groups(pool, body)

        @block.scalar
        def _(act):
            def split_hi(out, raw, col, ready):
                act.activation(out, raw, ACT.Copy, scale=w_scale[:, col:col + 1]).then_inc(ready, 1)

            def o_weights(g):
                act.wait_ge(oscale_ready, g + 1)
                at_least(act, y_done, 16 * g - 16)
                split_hi(wo_hi[:, g & 1, :, :], w_raw[:, :, :], 3, wo_hi_ready)

            def k_weights(g):
                act.wait_ge(qscale_ready, g + 1)
                at_least(act, k_done, 4 * g)
                split_hi(wk_hi[:, :, :], wk_raw[:, :, :], 1, wk_hi_ready)

            def v_weights(g):
                at_least(act, v_done, 4 * g)
                split_hi(wv_hi[:, :, :], wv_raw[:, :, :], 2, wv_hi_ready)

            def q_weights(g, hp):
                at_least(act, q_done[1], 8 * g - 1 + hp if not (isinstance(g, int) and g == 0) else 0)
                cols = slice(hp * 256, hp * 256 + 256)
                split_hi(wq_hi[:, :, cols], w_raw[:, :, cols], 0, wq_hi_ready)

            def turned_probs(n, u):
                act.wait_ge(t_done, n + 1)
                act.activation(probs_t[u][:, :, :].rearrange("p a b -> p (a b)"), pair_ps[0][:, :], ACT.Copy).then_inc(pt_ready, 1)

            def exponentials(n, u):
                act.wait_ge(max_ready, n + 1)
                at_least(act, t_done, n - 1)
                for b in range(SPAN_BATCHES):
                    ins = act.activation(probs[u][:, b, :], s_ps[:, b * SEQ:(b + 1) * SEQ], ACT.Exp,
                                         bias=neg_max[u][:, b:b + 1], accum_out=row_sum[u][:, b:b + 1])
                ins.then_inc(exp_done, 1)

            def values(tau, par):
                act.wait_ge(v_done, tau + 1)
                at_least(act, pv_done, 4 * (tau - 1))
                act.activation(v_sb[par][:, :, :].rearrange("p a b -> p (a b)"), kv_ps[:, :], ACT.Copy,
                               scale=V_SCALE).then_inc(v_ready, 1)

            def outputs_hi(n, tau, par, u):
                at_least(act, y_done, 4 * tau - 4)
                for hf in (0, 1):
                    act.wait_ge(pv_done, 2 * n + hf + 1)
                    act.activation(o_view(o_hi[par], u, hf), o_psum(hf), ACT.Copy).then_inc(o_hi_ready, 1)

            o_weights(0)
            k_weights(0)
            v_weights(0)
            q_weights(0, 0)
            q_weights(0, 1)
            values(0, 0)

            def body(g):
                first = isinstance(g, int) and g == 0
                for slot, (t, u) in enumerate(SLOTS):
                    tau = 4 * g + t
                    n = 2 * tau + u
                    prev = not (first and slot == 0)
                    if prev:
                        turned_probs(n - 1, 1 - u)
                    exponentials(n, u)
                    if u == 1 and not (is_last(g) and t == SPANS - 1):
                        values(tau + 1, (t + 1) % 2)
                    if prev:
                        pt, pp = (tau, t % 2) if u else (tau - 1, (t + 1) % 2)
                        outputs_hi(n - 1, pt, pp, 1 - u)
                    if not is_last(g):
                        if slot == 3:
                            o_weights(g + 1)
                        if slot == 5:
                            k_weights(g + 1)
                        if slot == 6:
                            v_weights(g + 1)
                            q_weights(g + 1, 0)
                        if slot == 7:
                            q_weights(g + 1, 1)

            groups(act, body)
            last = 2 * SPANS * KV_HEADS - 1
            turned_probs(last, 1)
            outputs_hi(last, SPANS * KV_HEADS - 1, 1, 1)

        @block.vector
        def _(dve):
            chain = Chain(dve, dve_step)

            def max_o(g):
                dve.wait_ge(raw_in, 32 * g + 16)
                dve.tensor_reduce(wmax[:, 3:4], w_raw[:, :, :], AX.XY, ALU.max, apply_absolute_value=True).then_inc(omax_ready, 1)

            def scale_o(g):
                dve.wait_ge(omax_reduced, g + 1)
                pow2_scale(dve, chain, wmax_all[:, 3:4], wtmp[:, 3:4], w_scale[:, 3:4], w_inv[:, 3:4], oscale_ready)

            def max_qkv(g):
                dve.wait_ge(raw_in, 32 * g + 32)
                dve.wait_ge(kv_in, 32 * g + 32)
                dve.tensor_reduce(wmax[:, 0:1], w_raw[:, :, :], AX.XY, ALU.max, apply_absolute_value=True)
                dve.tensor_reduce(wmax[:, 1:2], wk_raw[:, :, :], AX.XY, ALU.max, apply_absolute_value=True)
                dve.tensor_reduce(wmax[:, 2:3], wv_raw[:, :, :], AX.XY, ALU.max, apply_absolute_value=True).then_inc(qmax_ready, 1)

            def scale_qkv(g):
                dve.wait_ge(qmax_reduced, g + 1)
                pow2_scale(dve, chain, wmax_all[:, 0:3], wtmp[:, 0:3], w_scale[:, 0:3], w_inv[:, 0:3], qscale_ready)
                chain.step(dve.tensor_scalar(inv_q[:, g & 1, :], w_inv[:, 0:1], 1.0 / (XN_SCALE * float(HEAD_DIM) ** 0.5), None, ALU.mult))
                chain.step(dve.tensor_scalar(inv_k[:, g & 1, :], N.c_inv[:, :], w_inv[:, 1:2], None, ALU.mult))
                chain.step(dve.tensor_scalar(wtmp[:, 0:1], w_inv[:, 2:3], w_inv[:, 3:4], 1.0 / V_SCALE, ALU.mult, ALU.mult))
                chain.step(dve.tensor_scalar(inv_y[:, g & 1, :], N.c_inv[:, :], wtmp[:, 0:1], None, ALU.mult))

            def split_lo(out, raw, hi, col, ready):
                dve.scalar_tensor_tensor(out=out, in0=raw, scalar=w_scale[:, col:col + 1], in1=hi,
                                         op0=ALU.mult, op1=ALU.subtract).then_inc(ready, 1)

            def o_weights(g):
                dve.wait_ge(wo_hi_ready, g + 1)
                split_lo(wo_lo[:, g & 1, :, :], w_raw[:, :, :], wo_hi[:, g & 1, :, :], 3, wo_ready)

            def k_weights(g):
                dve.wait_ge(wk_hi_ready, g + 1)
                split_lo(wk_lo[:, :, :], wk_raw[:, :, :], wk_hi[:, :, :], 1, wk_ready)

            def v_weights(g):
                dve.wait_ge(wv_hi_ready, g + 1)
                split_lo(wv_lo[:, :, :], wv_raw[:, :, :], wv_hi[:, :, :], 2, wv_ready)

            def q_weights(g, hp):
                dve.wait_ge(wq_hi_ready, 2 * g + hp + 1)
                cols = slice(hp * 256, hp * 256 + 256)
                split_lo(wq_lo[:, :, cols], w_raw[:, :, cols], wq_hi[:, :, cols], 0, wq_ready)

            def rotate(ps, j, factor, span, free):
                cols = slice(span * SPAN, (span + 1) * SPAN)
                dve.scalar_tensor_tensor(out=by_cos[j][:, :], in0=ps[:, :], scalar=factor(0, P), in1=N.cos_t[:, cols],
                                         op0=ALU.mult, op1=ALU.mult)
                for a, b in ((0, 64), (64, 0)):
                    ins = dve.scalar_tensor_tensor(out=by_sin[j][b:b + 64, :], in0=ps[a:a + 64, :], scalar=factor(a, 64),
                                                   in1=N.sin_t[a:a + 64, cols], op0=ALU.mult, op1=ALU.mult)
                ins.then_inc(free, 1)

            def rotate_q(n, g, span):
                for j in range(2):
                    dve.wait_ge(q_done[j], n + 1)
                    at_least(dve, q_roped, 2 * n + j - 1)
                    rotate(q_ps[j], j, lambda a, w: inv_q[a:a + w, g & 1, :], span, q_free[j])

            def rotate_k(tau, g, span):
                dve.wait_ge(k_done, tau + 1)
                rotate(kv_ps, 0, lambda a, w: inv_k[a:a + w, g & 1, span:span + 1], span, k_free)

            def row_max(n, u, t):
                dve.wait_ge(s_done, 1)
                dve.wait_ge(s_done, n + 1)
                s3 = s_ps[:, :].rearrange("p (b k) -> p b k", b=SPAN_BATCHES)
                dve.copy_predicated(s3, N.pred[:, t * SPAN_BATCHES:(t + 1) * SPAN_BATCHES, :],
                                    N.fill[:, :].unsqueeze(1).to_broadcast([P, SPAN_BATCHES, SEQ])).then_inc(filled, 1)
                dve.wait_ge(filled, n + 1)
                dve.tensor_reduce(neg_max[u][:, :], s3, AX.X, ALU.max, negate=True).then_inc(max_ready, 1)

            def row_inverse(n, u):
                dve.wait_ge(exp_done, n + 1)
                dve.reciprocal(row_inv[u][:, :], row_sum[u][:, :]).then_inc(inv_ready, 1)

            def outputs_lo(n, par, u):
                for hf in (0, 1):
                    dve.wait_ge(o_hi_ready, 2 * n + hf + 1)
                    dve.tensor_tensor(o_view(o_lo[par], u, hf), o_psum(hf), o_view(o_hi[par], u, hf),
                                      ALU.subtract).then_inc(o_ready, 1)

            def add_y(tau, g, span, i):
                m = 4 * tau + i
                dve.wait_ge(y_done, m + 1)
                at_least(dve, y_added, m - 1)
                tile = N.acc[:, span * SPAN_TILES + i, :]
                dve.scalar_tensor_tensor(out=tile, in0=y_ps[i % 2][:, :], scalar=inv_y[:, g & 1, span:span + 1],
                                         in1=tile, op0=ALU.mult, op1=ALU.add).then_inc(y_added, 1)

            max_o(0)
            scale_o(0)
            o_weights(0)
            max_qkv(0)
            scale_qkv(0)
            k_weights(0)
            v_weights(0)
            q_weights(0, 0)
            q_weights(0, 1)
            rotate_k(0, 0, 0)
            dve.wait_ge(k_roped, 1)
            rotate_q(0, 0, 0)
            per_group = chain.n

            def body(g):
                chain.base, chain.n = per_group * (g + 1), 0
                first = isinstance(g, int) and g == 0
                for slot, (t, u) in enumerate(SLOTS):
                    tau = 4 * g + t
                    n = 2 * tau + u
                    if not (is_last(g) and slot == 7):
                        if u == 1:
                            dve.wait_ge(k_roped, tau + 2)
                        rotate_q(n + 1, g + 1 if slot == 7 else g, (slot + 1) // 2 % SPANS)
                    row_max(n, u, t)
                    if u == 0 and not (is_last(g) and t == SPANS - 1):
                        dve.wait_ge(q_roped, 2 * n + 3)
                        rotate_k(tau + 1, g + 1 if t == 3 else g, (t + 1) % SPANS)
                    row_inverse(n, u)
                    if not (first and slot == 0):
                        outputs_lo(n - 1, t % 2 if u else (t + 1) % 2, 1 - u)
                    back = 1 if u else 2
                    if not (first and t < back):
                        yg = g - 1 if t < back else g
                        for i in ((0, 1) if u else (2, 3)):
                            add_y(tau - back, yg, (t - back) % SPANS, i)
                    if not is_last(g):
                        if slot == 1:
                            max_o(g + 1)
                        if slot == 2:
                            scale_o(g + 1)
                        if slot == 3:
                            o_weights(g + 1)
                        if slot == 4:
                            max_qkv(g + 1)
                        if slot == 5:
                            scale_qkv(g + 1)
                            k_weights(g + 1)
                        if slot == 6:
                            v_weights(g + 1)
                            q_weights(g + 1, 0)
                        if slot == 7:
                            q_weights(g + 1, 1)
                assert is_last(g) or chain.n == per_group

            groups(dve, body)
            g = KV_HEADS - 1
            tau = 4 * g + 3
            outputs_lo(2 * tau + 1, 1, 1)
            for i in (2, 3):
                add_y(tau - 1, g, 2, i)
            for i in range(4):
                add_y(tau, g, 3, i)

        @block.tensor
        def _(pe):
            def product3(out, pairs):
                steps = [(a, b) for ah, al, bh, bl in pairs for a, b in ((ah, bh), (ah, bl), (al, bh))]
                for s, (a, b) in enumerate(steps):
                    ins = pe.matmul(out, a, b, start=(s == 0), stop=(s == len(steps) - 1))
                return ins

            def queries(n, hp, span, new, g):
                cols = slice(span * SPAN, (span + 1) * SPAN)
                if new:
                    pe.wait_ge(wq_ready, 2 * g + hp + 1)
                for j in range(2):
                    at_least(pe, q_free[j], n)
                    h = slice((2 * hp + j) * HEAD_DIM, (2 * hp + j + 1) * HEAD_DIM)
                    product3(q_ps[j][:, :], [(wq_hi[:, k, h], wq_lo[:, k, h], N.x_hi[:, k, cols], N.x_lo[:, k, cols])
                                             for k in range(KT)]).then_inc(q_done[j], 1)

            def keys(tau, span, new, g):
                cols = slice(span * SPAN, (span + 1) * SPAN)
                if new:
                    pe.wait_ge(wk_ready, g + 1)
                at_least(pe, v_ready, tau)
                product3(kv_ps[:, :], [(wk_hi[:, k, :], wk_lo[:, k, :], N.c_hi[:, k, cols], N.c_lo[:, k, cols])
                                       for k in range(KT)]).then_inc(k_done, 1)

            def values(tau, span, new, g):
                if new:
                    pe.wait_ge(wv_ready, g + 1)
                pe.wait_ge(k_free, tau + 1)
                for j in range(SPAN_TILES):
                    rows = slice(span * SPAN + j * P, span * SPAN + (j + 1) * P)
                    ins = product3(kv_ps[:, j * P:(j + 1) * P],
                                   [(N.c_hi[:, k, rows], N.c_lo[:, k, rows], wv_hi[:, k, :], wv_lo[:, k, :]) for k in range(KT)])
                ins.then_inc(v_done, 1)

            def turn_probs(n, u):
                pe.wait_ge(p_ready, n + 1)
                at_least(pe, o_ready, 2 * n)
                for j in range(SPAN_TILES):
                    ins = pe.transpose(pair_ps[0][:, j * P:(j + 1) * P],
                                       probs[u][:, 2 * j:2 * j + 2, :].rearrange("p b k -> p (b k)"), N.ident[:, :])
                ins.then_inc(t_done, 1)

            def scores(n, u, tau, par):
                pe.wait_ge(q_roped, 2 * n + 2)
                pe.wait_ge(k_roped, tau + 1)
                at_least(pe, exp_done, n)
                for b in range(SPAN_BATCHES):
                    rows = slice(b * SEQ, (b + 1) * SEQ)
                    ins = pe.matmul(s_ps[:, rows], q_sb[u][:, b, :, :].rearrange("p h q -> p (h q)"), k_sb[par][:, rows], start=True, stop=True)
                ins.then_inc(s_done, 1)

            def head_outputs(n, u, tau, par):
                pe.wait_ge(pt_ready, n + 1)
                pe.wait_ge(v_ready, tau + 1)
                at_least(pe, o_ready, 2 * n)
                for b in range(SPAN_BATCHES):
                    j, e = b // 2, b % 2
                    rows = slice(SEQ * e, SEQ * e + SEQ)
                    ins = pe.matmul(pair_ps[1 - e][:, j * P:(j + 1) * P], v_sb[par][rows, j, :],
                                    probs_t[u][rows, j, :], start=True, stop=True)
                    if j == 3:
                        ins.then_inc(pv_done, 1)

            def project(tau, par, i, g):
                m = 4 * tau + i
                if i == 0:
                    pe.wait_ge(wo_ready, g + 1)
                pe.wait_ge(o_ready, 4 * tau + 4)
                at_least(pe, y_added, m - 1)
                rows = slice(i * P, (i + 1) * P)
                product3(y_ps[i % 2][:, :], [(o_hi[par][:, h, rows], o_lo[par][:, h, rows],
                                              wo_hi[:, g & 1, h, :], wo_lo[:, g & 1, h, :])
                                             for h in range(GROUP)]).then_inc(y_done, 1)

            keys(0, 0, True, 0)
            queries(0, 0, 0, True, 0)
            values(0, 0, True, 0)

            def body(g):
                first = isinstance(g, int) and g == 0
                for slot, (t, u) in enumerate(SLOTS):
                    tau = 4 * g + t
                    n = 2 * tau + u
                    if not (is_last(g) and slot == 7):
                        queries(n + 1, 1 - u, (slot + 1) // 2 % SPANS, slot in (7, 0), g + 1 if slot == 7 else g)
                    if not (first and slot == 0):
                        turn_probs(n - 1, 1 - u)
                    scores(n, u, tau, t % 2)
                    if not (is_last(g) and t == SPANS - 1):
                        gn, new = (g + 1, True) if t == 3 else (g, False)
                        (values if u else keys)(tau + 1, (t + 1) % SPANS, new, gn)
                    if not (first and slot == 0):
                        head_outputs(n - 1, 1 - u, tau if u else tau - 1, t % 2 if u else (t + 1) % 2)
                    back = 1 if u else 2
                    if not (first and t < back):
                        for i in ((0, 1) if u else (2, 3)):
                            project(tau - back, (t - back) % 2, i, g - 1 if t < back else g)

            groups(pe, body)
            g = KV_HEADS - 1
            tau = 4 * g + 3
            turn_probs(2 * tau + 1, 1)
            head_outputs(2 * tau + 1, 1, tau, 1)
            for i in (2, 3):
                project(tau - 1, 0, i, g)
            for i in range(4):
                project(tau, 1, i, g)


def feed(nc, N):
    with ExitStack() as ctx:
        def sb(name, shape, dt):
            return ctx.enter_context(nc.sbuf_tensor(name, shape, dt))

        def sem(name):
            return N.sems.enter_context(nc.semaphore(name))

        m_gate = sb("m_gate", [P, KT, HIDDEN], F16)
        m_up = sb("m_up", [P, KT, HIDDEN], F16)
        m_down = sb("m_down2", [P, HCHUNKS, EMB], F16)
        normed = [sb(f"normed2_{j}", [P, EMB], F32) for j in range(2)]
        stats = sb("stats2", [P, TILES, 6], F32)
        mean_var = sb("mean_var2", [P, TILES, 2], F32)
        std, rstd = sb("std2", [P, TILES], F32), sb("rstd2", [P, TILES], F32)
        silu = [sb(f"silu{i}", [P, SPAN], F32) for i in range(2)]
        hid = [sb(f"hid{i}", [P, SPAN], F32) for i in range(2)]
        h_hi = sb("h_hi", [P, HCHUNKS, SPAN], F16)
        h_lo = sb("h_lo", [P, HCHUNKS, SPAN], F16)
        result = [sb(f"result{i}", [P, EMB], F32) for i in range(2)]

        def bank(name, shape=(P, SPAN)):
            return ctx.enter_context(nc.psum_tensor(name, list(shape), F32))

        turn = [bank(f"turn2_{i}", (P, KT, P)) for i in range(2)]
        gate_ps = [bank(f"gate_ps{i}") for i in range(2)]
        up_ps = [bank(f"up_ps{i}") for i in range(2)]
        y_ps = [bank(f"y2_ps{i}") for i in range(2)]

        m_loaded = sem("m_loaded")
        var_ready, std_ready, normed_ready = sem("var2_ready"), sem("std2_ready"), sem("normed2_ready")
        turned, hi_ready, lo_ready = sem("turned2"), sem("hi2_ready"), sem("lo2_ready")
        gate_done, up_done, silu_ready, hid_ready = sem("gate_done"), sem("up_done"), sem("silu_ready"), sem("hid_ready")
        h_hi_ready, h_ready = sem("h_hi_ready"), sem("h_ready")
        y_done, result_ready = sem("y2_done"), sem("result_ready")
        stored = [sem(f"stored{i}") for i in range(2)]
        dve_step = sem("f_dve_step")
        block = ctx.enter_context(nc.Block())

        @block.sync
        def _(sp):
            sp.dma_start(m_gate[:, :, :].rearrange("p k h -> p (k h)"), N.m_dram[0]).then_inc(m_loaded, 16)
            sp.dma_start(m_up[:, :, :].rearrange("p k h -> p (k h)"), N.m_dram[1]).then_inc(m_loaded, 16)
            sp.dma_start(m_down[:, :, :].rearrange("p k h -> p (k h)"), N.m_dram[2][:, 0:HCHUNKS * EMB]).then_inc(m_loaded, 16)
            with sp.Fori(0, SPANS) as t:
                for i in range(SPAN_TILES):
                    sp.wait_ge(result_ready, 4 * t + i + 1)
                    sp.dma_start(N.out[bass.ds((t * SPAN_TILES + i) * P, P), :], result[i % 2][:, :]).then_inc(stored[i % 2], 16)
            for s in stored:
                sp.wait_ge(s, 16 * TILES // 2)

        @block.gpsimd
        def _(pool):
            with pool.Fori(0, SPANS) as t:
                for c in range(HCHUNKS):
                    rows = P if c < HCHUNKS - 1 else HLAST
                    pool.wait_ge(h_hi_ready, HCHUNKS * t + c + 1)
                    pool.tensor_tensor(h_lo[0:rows, c, :], hid[c % 2][0:rows, :], h_hi[0:rows, c, :],
                                       ALU.subtract).then_inc(h_ready, 1)

        @block.scalar
        def _(act):
            act.wait_ge(var_ready, 1)
            act.activation(std[:, :], mean_var[:, :, 1], ACT.Sqrt, scale=XN_SCALE ** -2, bias=N.eps_tile[:, 0:1]).then_inc(std_ready, 1)
            for m in range(TILES):
                act.wait_ge(turned, m + 1)
                act.activation(N.x_hi[:, :, m * P:(m + 1) * P], turn[m % 2][:, :, :], ACT.Copy).then_inc(hi_ready, 1)
            with act.Fori(0, SPANS) as t:
                def hidden_hi(c):
                    rows = P if c < HCHUNKS - 1 else HLAST
                    act.wait_ge(hid_ready, HCHUNKS * t + c + 1)
                    act.activation(h_hi[0:rows, c, :], hid[c % 2][0:rows, :], ACT.Copy).then_inc(h_hi_ready, 1)

                for c in range(HCHUNKS):
                    rows = P if c < HCHUNKS - 1 else HLAST
                    act.wait_ge(gate_done, HCHUNKS * t + c + 1)
                    act.activation(silu[c % 2][0:rows, :], gate_ps[c % 2][0:rows, :], ACT.Silu,
                                   scale=N.ffn_factor[0:rows, 0:1]).then_inc(silu_ready, 1)
                    if c >= 1:
                        hidden_hi(c - 1)
                hidden_hi(HCHUNKS - 1)

        @block.vector
        def _(dve):
            chain = Chain(dve, dve_step)
            for i in range(TILES):
                ins = dve.bn_stats(stats[:, i, :], N.acc[:, i, :])
            chain.step(ins)
            for i in range(TILES):
                ins = dve.bn_aggr(mean_var[:, i, :], stats[:, i, :])
            ins.then_inc(var_ready, 1)
            dve.wait_ge(var_ready, 1)
            dve.wait_ge(std_ready, 1)
            chain.step(dve.reciprocal(rstd[:, :], std[:, :]))
            for m in range(TILES):
                if m >= 2:
                    dve.wait_ge(turned, m - 1)
                dve.tensor_scalar(normed[m % 2][:, :], N.acc[:, m, :], mean_var[:, m, 0:1], rstd[:, m:m + 1],
                                  ALU.subtract, ALU.mult).then_inc(normed_ready, 1)
                if m >= 1:
                    low(m - 1) if False else None
                if m >= 1:
                    k = m - 1
                    dve.wait_ge(hi_ready, k + 1)
                    dve.tensor_tensor(N.x_lo[:, :, k * P:(k + 1) * P], turn[k % 2][:, :, :],
                                      N.x_hi[:, :, k * P:(k + 1) * P], ALU.subtract).then_inc(lo_ready, 1)
            k = TILES - 1
            dve.wait_ge(hi_ready, k + 1)
            dve.tensor_tensor(N.x_lo[:, :, k * P:(k + 1) * P], turn[k % 2][:, :, :],
                              N.x_hi[:, :, k * P:(k + 1) * P], ALU.subtract).then_inc(lo_ready, 1)
            def body(t, peeled):
                for c in range(HCHUNKS):
                    rows = P if c < HCHUNKS - 1 else HLAST
                    n = HCHUNKS * t + c
                    dve.wait_ge(silu_ready, n + 1)
                    dve.wait_ge(up_done, n + 1)
                    if not (peeled and c < 2):
                        back = 2 if c >= 2 or not peeled else 0
                        at_least(dve, h_ready, n + 1 - (2 if c >= 2 else (1 if c == 0 else 2)))
                    dve.scalar_tensor_tensor(out=hid[c % 2][0:rows, :], in0=silu[c % 2][0:rows, :],
                                             scalar=N.ffn_factor[0:rows, 1:2], in1=up_ps[c % 2][0:rows, :],
                                             op0=ALU.mult, op1=ALU.mult).then_inc(hid_ready, 1)
                for i in range(SPAN_TILES):
                    m = 4 * t + i
                    dve.wait_ge(y_done, m + 1)
                    if not (peeled and i < 2):
                        dve.wait_ge(stored[i % 2], 16 * (2 * t + i // 2))
                    dve.scalar_tensor_tensor(out=result[i % 2][:, :], in0=y_ps[i % 2][:, :], scalar=N.ffn_factor[:, 2:3],
                                             in1=N.acc[:, bass.ds(t * SPAN_TILES + i, 1), :].rearrange("p a e -> p (a e)"),
                                             op0=ALU.mult, op1=ALU.add).then_inc(result_ready, 1)

            body(0, True)
            with dve.Fori(1, SPANS) as t:
                body(t, False)

        @block.tensor
        def _(pe):
            for m in range(TILES):
                pe.wait_ge(normed_ready, m + 1)
                if m >= 2:
                    pe.wait_ge(lo_ready, m - 1)
                for kt in range(KT):
                    ins = pe.transpose(turn[m % 2][:, kt, :], normed[m % 2][:, kt * P:(kt + 1) * P], N.ident[:, :])
                ins.then_inc(turned, 1)
            pe.wait_ge(m_loaded, 48)

            def body(t, peeled):
                pe.wait_ge(lo_ready, TILES)
                for c in range(HCHUNKS):
                    rows = P if c < HCHUNKS - 1 else HLAST
                    n = HCHUNKS * t + c
                    for w, ps, free, done in ((m_gate, gate_ps, silu_ready, gate_done), (m_up, up_ps, hid_ready, up_done)):
                        if not (peeled and c < 2):
                            pe.wait_ge(free, n - 1 if c >= 1 else n)
                        for k in range(KT):
                            for part in (N.x_hi, N.x_lo):
                                ins = pe.matmul(ps[c % 2][0:rows, :], w[:, k, c * P:c * P + rows],
                                                part[:, k, bass.ds(t * SPAN, SPAN)],
                                                start=(k == 0 and part is N.x_hi), stop=(k == KT - 1 and part is N.x_lo))
                        ins.then_inc(done, 1)
                for i in range(SPAN_TILES):
                    m = 4 * t + i
                    if not (peeled and i < 2):
                        pe.wait_ge(result_ready, m - 1)
                    for c in range(HCHUNKS):
                        rows = P if c < HCHUNKS - 1 else HLAST
                        if i == 0:
                            pe.wait_ge(h_ready, HCHUNKS * t + c + 1)
                        for part in (h_hi, h_lo):
                            ins = pe.matmul(y_ps[i % 2][:, :], part[0:rows, c, i * P:(i + 1) * P], m_down[0:rows, c, :],
                                            start=(c == 0 and part is h_hi), stop=(c == HCHUNKS - 1 and part is h_lo))
                    ins.then_inc(y_done, 1)

            body(0, True)
            with pe.Fori(1, SPANS) as t:
                body(t, False)


def build(nc, x, ctx_in, pos, mask, wq, wk, wv, wo, w_gate, w_up, w_down, rope_table, out):
    N = Net()
    N.x = x.rearrange("b s e -> (b s) e")
    N.ctx = ctx_in.rearrange("b s e -> (b s) e")
    N.out = out.rearrange("b s e -> (b s) e")
    N.pos, N.mask, N.rope_table = pos, mask, rope_table
    N.wq, N.wk, N.wv, N.wo = wq, wk, wv, wo
    N.w_gate, N.w_up, N.w_down = w_gate, w_up, w_down
    N.m_dram = [nc.dram_tensor(f"m_store{w}", [P, max(KT * HIDDEN, HCHUNKS * EMB)] if w == 2 else [P, KT * HIDDEN], F16,
                               kind="Internal").ap() for w in range(3)]
    with ExitStack() as ctx:
        N.sems = ctx

        def sb(name, shape, dt):
            return ctx.enter_context(nc.sbuf_tensor(name, shape, dt))

        N.acc = sb("acc", [P, TILES, EMB], F32)
        N.x_hi, N.x_lo = sb("x_hi", [P, KT, TOKENS], F16), sb("x_lo", [P, KT, TOKENS], F16)
        N.ident = sb("ident", [P, P], F32)
        N.eps_tile = sb("eps_tile", [P, 1], F32)
        N.fill = sb("fill", [P, SEQ], F32)
        N.ffn_scale, N.ffn_factor = sb("ffn_scale", [P, 3], F32), sb("ffn_factor", [P, 3], F32)
        N.c_scale, N.c_inv = sb("c_scale", [P, SPANS], F32), sb("c_inv", [P, SPANS], F32)
        N.consts_ready = ctx.enter_context(nc.semaphore("consts_ready"))
        with ExitStack() as attention:
            def sba(name, shape, dt):
                return attention.enter_context(nc.sbuf_tensor(name, shape, dt))

            N.c_hi, N.c_lo = sba("c_hi", [P, KT, TOKENS], F16), sba("c_lo", [P, KT, TOKENS], F16)
            N.cos_t, N.sin_t = sba("cos_t", [P, TOKENS], F32), sba("sin_t", [P, TOKENS], F32)
            N.pred = sba("pred", [P, BATCH, SEQ], U8)
            prepare(nc, N)
            attend(nc, N)
        feed(nc, N)


_INS = ["x", "ctx_4096", "pos_BxS2", "mask_BxSxS2_ik0", "L0_xattn_Wq", "L0_xattn_Wk", "L0_xattn_Wv", "L0_xattn_Wo",
        "L0_ffn_w_gate", "L0_ffn_w_up", "L0_ffn_w_down"]


def rope_rows():
    import numpy as np
    inv_freq = (np.float32(1.0) / np.float32(THETA) ** (np.arange(0, HEAD_DIM, 2, dtype=np.float32) / np.float32(HEAD_DIM))).astype(np.float32)
    ang = np.arange(MAX_POS, dtype=np.float32)[:, None] * inv_freq[None, :]
    return np.concatenate([np.cos(ang), np.cos(ang), np.sin(ang), -np.sin(ang)], axis=1).astype(np.float32)


def kernel(**inputs):
    import numpy as np
    import concourse.bacc as bacc
    from concourse.bass_utils import run_bass_kernel_spmd

    nc = bacc.Bacc("TRN2", target_bir_lowering=False, num_devices=1)
    arrays, args = {}, []
    for name in _INS:
        a = np.ascontiguousarray(inputs[name])
        arrays[f"in_{name}"] = a
        args.append(nc.dram_tensor(f"in_{name}", a.shape, mybir.dt.from_np(a.dtype), kind="ExternalInput").ap())
    table = rope_rows()
    arrays["rope_table"] = table
    args.append(nc.dram_tensor("rope_table", table.shape, F32, kind="ExternalInput").ap())
    args.append(nc.dram_tensor("out", (BATCH, SEQ, EMB), F32, kind="ExternalOutput").ap())
    build(nc, *args)
    r = run_bass_kernel_spmd(nc, [arrays], core_ids=[0])
    return r.results[0]["out"]
```

```python
from contextlib import ExitStack

import concourse.bass as bass
from concourse import mybir

F32 = mybir.dt.float32
F16 = mybir.dt.float16
I32 = mybir.dt.int32
U8 = mybir.dt.uint8
ALU = mybir.AluOpType
ACT = mybir.ActivationFunctionType
AX = mybir.AxisListType
REDUCE = bass.bass_isa.ReduceOp

P = 128
BATCH, SEQ, EMB = 32, 64, 512
TOKENS = BATCH * SEQ
HEADS, KV_HEADS, HEAD_DIM = 32, 8, 128
GROUP = HEADS // KV_HEADS
MAX_POS, THETA = 512, 10000.0
EPS = 1e-5
KT = EMB // P
TILES = TOKENS // P
SPAN = 512
SPANS = TOKENS // SPAN
SPAN_TILES = SPAN // P
SPAN_BATCHES = SPAN // SEQ
GCOLS = GROUP * HEAD_DIM

OCT = 8
HID8, EMB8 = 170, EMB // OCT
HIDDEN = OCT * HID8
HCHUNKS = -(-HIDDEN // P)
HLAST = HIDDEN - (HCHUNKS - 1) * P
FFN_COUNT = float(OCT * HID8 * EMB8)

MASKED = -1.0e9
XN_SCALE = 128.0
TOP = 2.0 ** 11
V_SCALE = 2.0 ** -18
QK_SCALE = 2.0 ** -19
SCORE_FLOOR = 1e-28
H_SCALE = 2.0 ** -4
TINY = 1e-30
EXP_BITS = 0x7F800000

_TRIPLES = [(1, 2, 3), (1, 4, 5), (1, 7, 6), (2, 4, 6), (2, 5, 7), (3, 4, 7), (3, 6, 5)]


def octonion_signs():
    s = {(0, 0): (0, 1)}
    for i in range(1, OCT):
        s[(0, i)] = (i, 1)
        s[(i, 0)] = (i, 1)
        s[(i, i)] = (0, -1)
    for a, b, c in _TRIPLES:
        for x, y, z in ((a, b, c), (b, c, a), (c, a, b)):
            s[(x, y)] = (z, 1)
            s[(y, x)] = (z, -1)
    sign = [[0] * OCT for _ in range(OCT)]
    for (j, i), (k, v) in s.items():
        assert j == i ^ k
        sign[i][k] = v
    return sign


SIGN = octonion_signs()


def at_least(eng, sem, value):
    if isinstance(value, int) and value <= 0:
        return
    eng.wait_ge(sem, value)


class Chain:

    def __init__(self, eng, sem):
        self.eng, self.sem, self.base, self.n = eng, sem, 0, 0

    def step(self, ins):
        ins.then_inc(self.sem, 1)
        self.n += 1
        self.eng.wait_ge(self.sem, self.base + self.n)


class Net:
    pass


class Weights:

    STEPS = 10

    def __init__(self, nc, sb, sem, N):
        self.N = N
        self.wq_dram = N.wq.rearrange("(k p) n -> p k n", p=P)
        self.wk_dram = N.wk.rearrange("(k p) n -> p k n", p=P)
        self.wv_dram = N.wv.rearrange("(k p) n -> p k n", p=P)
        self.wo_dram = N.wo.rearrange("(h p) n -> p h n", p=P)
        self.w_raw = sb("w_raw", [P, KT, GCOLS], F32)
        self.wk_raw = sb("wk_raw", [P, KT, HEAD_DIM], F32)
        self.wv_raw = sb("wv_raw", [P, KT, HEAD_DIM], F32)
        self.wq_hi, self.wq_lo = sb("wq_hi", [P, KT, GCOLS], F16), sb("wq_lo", [P, KT, GCOLS], F16)
        self.wk_hi, self.wk_lo = sb("wk_hi", [P, KT, HEAD_DIM], F16), sb("wk_lo", [P, KT, HEAD_DIM], F16)
        self.wv_hi, self.wv_lo = sb("wv_hi", [P, KT, HEAD_DIM], F16), sb("wv_lo", [P, KT, HEAD_DIM], F16)
        self.wo_hi, self.wo_lo = sb("wo_hi", [P, 2, GROUP, EMB], F16), sb("wo_lo", [P, 2, GROUP, EMB], F16)
        self.wmax, self.wmax_all = sb("wmax", [P, 4], F32), sb("wmax_all", [P, 4], F32)
        self.wtmp = sb("wtmp", [P, 4], F32)
        self.w_scale, self.w_inv = sb("w_scale", [P, 4], F32), sb("w_inv", [P, 4], F32)
        self.score_next = sb("score_next", [P, 2, SPANS], F32)
        self.score_now = sb("score_now", [P, 2, SPANS], F32)
        self.score_scale, self.masked_raw = self.score_now[:, 0, :], self.score_now[:, 1, :]
        self.inv_y = sb("inv_y", [P, 2, SPANS], F32)
        self.raw_in, self.kv_in = sem("raw_in"), sem("kv_in")
        self.omax_ready, self.omax_reduced, self.oscale_ready = sem("omax_ready"), sem("omax_reduced"), sem("oscale_ready")
        self.qmax_ready, self.qmax_reduced, self.qscale_ready = sem("qmax_ready"), sem("qmax_reduced"), sem("qscale_ready")
        self.wo_hi_ready, self.wo_ready = sem("wo_hi_ready"), sem("wo_ready")
        self.wk_hi_ready, self.wk_ready = sem("wk_hi_ready"), sem("wk_ready")
        self.wv_hi_ready, self.wv_ready = sem("wv_hi_ready"), sem("wv_ready")
        self.wq_hi_ready, self.wq_ready = sem("wq_hi_ready"), sem("wq_ready")

    def load_o(self, sp, g):
        at_least(sp, self.wq_ready, 2 * g)
        sp.dma_start(self.w_raw[:, :, :], self.wo_dram[:, bass.ds(g * GROUP, GROUP), :]).then_inc(self.raw_in, 16)

    def load_kv(self, sp, g):
        at_least(sp, self.wk_ready, g)
        at_least(sp, self.wv_ready, g)
        sp.dma_start(self.wk_raw[:, :, :], self.wk_dram[:, :, bass.ds(g * HEAD_DIM, HEAD_DIM)]).then_inc(self.kv_in, 16)
        sp.dma_start(self.wv_raw[:, :, :], self.wv_dram[:, :, bass.ds(g * HEAD_DIM, HEAD_DIM)]).then_inc(self.kv_in, 16)

    def load_q(self, sp, g):
        sp.wait_ge(self.wo_ready, g + 1)
        sp.dma_start(self.w_raw[:, :, :], self.wq_dram[:, :, bass.ds(g * GCOLS, GCOLS)]).then_inc(self.raw_in, 16)

    def load(self, sp, g):
        self.load_o(sp, g)
        self.load_kv(sp, g)
        self.load_q(sp, g)

    def reduce_o(self, pool):
        pool.partition_all_reduce(self.wmax_all[:, 3:4], self.wmax[:, 3:4], P, REDUCE.max).then_inc(self.omax_reduced, 1)

    def reduce_qkv(self, pool):
        pool.partition_all_reduce(self.wmax_all[:, 0:3], self.wmax[:, 0:3], P, REDUCE.max).then_inc(self.qmax_reduced, 1)

    def high(self, act, out, raw, col, ready):
        act.activation(out, raw, ACT.Copy, scale=self.w_scale[:, col:col + 1]).then_inc(ready, 1)

    def o_high(self, act, g):
        act.wait_ge(self.oscale_ready, g + 1)
        self.high(act, self.wo_hi[:, g & 1, :, :], self.w_raw[:, :, :], 3, self.wo_hi_ready)

    def k_high(self, act, g):
        act.wait_ge(self.qscale_ready, g + 1)
        self.high(act, self.wk_hi[:, :, :], self.wk_raw[:, :, :], 1, self.wk_hi_ready)

    def v_high(self, act, g):
        self.high(act, self.wv_hi[:, :, :], self.wv_raw[:, :, :], 2, self.wv_hi_ready)

    def q_high(self, act, g, hp):
        cols = slice(hp * 256, hp * 256 + 256)
        self.high(act, self.wq_hi[:, :, cols], self.w_raw[:, :, cols], 0, self.wq_hi_ready)

    def max_o(self, dve, g):
        dve.wait_ge(self.raw_in, 32 * g + 16)
        dve.tensor_reduce(self.wmax[:, 3:4], self.w_raw[:, :, :], AX.XY, ALU.max,
                          apply_absolute_value=True).then_inc(self.omax_ready, 1)

    def scale_o(self, dve, chain, g):
        dve.wait_ge(self.omax_reduced, g + 1)
        pow2_scale(dve, chain, self.wmax_all[:, 3:4], self.wtmp[:, 3:4], self.w_scale[:, 3:4], self.w_inv[:, 3:4],
                   self.oscale_ready)

    def max_qkv(self, dve, g):
        dve.wait_ge(self.raw_in, 32 * g + 32)
        dve.wait_ge(self.kv_in, 32 * g + 32)
        for col, raw in enumerate((self.w_raw, self.wk_raw, self.wv_raw)):
            ins = dve.tensor_reduce(self.wmax[:, col:col + 1], raw[:, :, :], AX.XY, ALU.max, apply_absolute_value=True)
        ins.then_inc(self.qmax_ready, 1)

    def scale_qkv(self, dve, chain, g):
        dve.wait_ge(self.qmax_reduced, g + 1)
        pow2_scale(dve, chain, self.wmax_all[:, 0:3], self.wtmp[:, 0:3], self.w_scale[:, 0:3], self.w_inv[:, 0:3],
                   self.qscale_ready)
        dve.wait_ge(self.qscale_ready, g + 1)
        dve.tensor_scalar(self.wtmp[:, 0:1], self.w_inv[:, 0:1], self.w_inv[:, 1:2],
                          1.0 / (QK_SCALE * QK_SCALE * XN_SCALE * float(HEAD_DIM) ** 0.5), ALU.mult, ALU.mult)
        chain.step(dve.tensor_scalar(self.wtmp[:, 1:2], self.w_inv[:, 2:3], self.w_inv[:, 3:4], 1.0 / V_SCALE,
                                     ALU.mult, ALU.mult))
        dve.tensor_scalar(self.inv_y[:, g & 1, :], self.N.c_inv[:, :], self.wtmp[:, 1:2], None, ALU.mult)
        chain.step(dve.tensor_scalar(self.score_next[:, 0, :], self.N.c_inv[:, :], self.wtmp[:, 0:1],
                                     SCORE_FLOOR, ALU.mult, ALU.max))
        chain.step(dve.reciprocal(self.score_next[:, 1, :], self.score_next[:, 0, :]))
        chain.step(dve.tensor_scalar(self.score_next[:, 1, :], self.score_next[:, 1, :], MASKED, None, ALU.mult))

    def low(self, dve, out, raw, hi, col, ready):
        dve.scalar_tensor_tensor(out=out, in0=raw, scalar=self.w_scale[:, col:col + 1], in1=hi,
                                 op0=ALU.mult, op1=ALU.subtract).then_inc(ready, 1)

    def o_low(self, dve, g):
        dve.wait_ge(self.wo_hi_ready, g + 1)
        self.low(dve, self.wo_lo[:, g & 1, :, :], self.w_raw[:, :, :], self.wo_hi[:, g & 1, :, :], 3, self.wo_ready)

    def k_low(self, dve, g):
        dve.wait_ge(self.wk_hi_ready, g + 1)
        self.low(dve, self.wk_lo[:, :, :], self.wk_raw[:, :, :], self.wk_hi[:, :, :], 1, self.wk_ready)

    def v_low(self, dve, g):
        dve.wait_ge(self.wv_hi_ready, g + 1)
        self.low(dve, self.wv_lo[:, :, :], self.wv_raw[:, :, :], self.wv_hi[:, :, :], 2, self.wv_ready)

    def q_low(self, dve, g, hp):
        dve.wait_ge(self.wq_hi_ready, 2 * g + hp + 1)
        cols = slice(hp * 256, hp * 256 + 256)
        self.low(dve, self.wq_lo[:, :, cols], self.w_raw[:, :, cols], self.wq_hi[:, :, cols], 0, self.wq_ready)


def prepare(nc, N):
    with ExitStack() as ctx:
        def sb(name, shape, dt):
            return ctx.enter_context(nc.sbuf_tensor(name, shape, dt))

        def sem(name):
            return N.sems.enter_context(nc.semaphore(name))

        ctx_both = sb("ctx_both", [P, 2, SPAN_TILES, EMB], F32)
        ctx_raw = [ctx_both[:, s, :, :] for s in range(2)]
        normed = [sb(f"normed{j}", [P, EMB], F32) for j in range(2)]
        stats = sb("stats1", [P, SPAN_TILES, 6], F32)
        mean_var = sb("mean_var", [P, SPAN_TILES, 2], F32)
        std = sb("std", [P, SPAN_TILES], F32)
        rstd = sb("rstd", [P, SPAN_TILES], F32)
        cmax = sb("cmax", [P, 1], F32)
        cmax_all = sb("cmax_all", [P, 1], F32)
        cpow = sb("cpow", [P, 1], F32)
        pos = sb("pos", [P, TILES], I32)
        pos_wrap = sb("pos_wrap", [P, TILES], I32)
        rope_rows = [sb(f"rope_rows{s}", [P, 2 * HEAD_DIM], F32) for s in range(4)]
        mask_raw = sb("mask_raw", [P, BATCH, SEQ], I32)
        turn = [ctx.enter_context(nc.psum_tensor(f"turn{i}", [P, KT, P], F32)) for i in range(4)]
        rope_ps = [ctx.enter_context(nc.psum_tensor(f"rope_ps{i}", [P, 2, P], F32)) for i in range(2)]

        W = N.weights
        ident_zero, ident_in = sem("ident_zero"), sem("ident_in")
        pos_in, mask_in = sem("pos_in"), sem("mask_in")
        ctx_in = [sem(f"ctx_in{s}") for s in range(2)]
        x_in = [sem(f"x_in{s}") for s in range(2)]
        dve_step = sem("p_dve_step")
        pos_ready, rows_in, rows_turned, rows_out = sem("pos_ready"), [sem(f"rows_in{s}") for s in range(4)], sem("rows_turned"), sem("rows_out")
        pred_ready = sem("pred_ready")
        cmax_ready, cmax_reduced, cscale_ready = sem("cmax_ready"), sem("cmax_reduced"), sem("cscale_ready")
        var_ready, std_ready, normed_ready = sem("var_ready"), sem("std_ready"), sem("normed_ready")
        turned, hi_ready, lo_ready = sem("turned"), sem("p_hi_ready"), sem("p_lo_ready")

        block = ctx.enter_context(nc.Block())

        @block.sync
        def _(sp):
            sp.dma_start(pos[:, :], N.pos.rearrange("b s -> (b s)").rearrange("(i p) -> p i", p=P),
                         allow_slow_non_contiguous=True).then_inc(pos_in, 16)

            def load_tokens(t):
                rows = slice(t * SPAN, (t + 1) * SPAN)
                sp.dma_start(ctx_raw[t % 2][:, :, :], N.ctx[rows, :].rearrange("(j p) e -> p j e", p=P)).then_inc(ctx_in[t % 2], 16)
                sp.dma_start(N.acc[:, t * SPAN_TILES:(t + 1) * SPAN_TILES, :],
                             N.x[rows, :].rearrange("(j p) e -> p j e", p=P)).then_inc(x_in[t % 2], 16)

            load_tokens(0)
            W.load_o(sp, 0)
            load_tokens(1)
            W.load_kv(sp, 0)
            sp.wait_ge(lo_ready, 8)
            load_tokens(2)
            W.load_q(sp, 0)
            sp.wait_ge(lo_ready, 16)
            load_tokens(3)
            for half_rows in range(2):
                sp.dma_start(mask_raw[64 * half_rows:64 * half_rows + 64, :, :], N.mask.rearrange("b q k -> q b k")).then_inc(mask_in, 16)

        @block.gpsimd
        def _(pool):
            pool.memset(N.ident[:, :], 0.0).then_inc(ident_zero, 1)
            pool.wait_ge(ident_zero, 1)
            pool.affine_select(out=N.ident[:, :], in_=N.ident[:, :], compare_op=ALU.not_equal, fill=1.0,
                               base=0, pattern=[[-1, P]], channel_multiplier=1).then_inc(ident_in, 1)
            pool.wait_ge(pos_ready, 1)
            for i in range(TILES):
                if i >= 4:
                    pool.wait_ge(rows_turned, i - 3)
                pool.indirect_dma_start(rope_rows[i % 4][:, :], None, N.rope_table,
                                        bass.IndirectOffsetOnAxis(pos[:, i:i + 1], 0)).then_inc(rows_in[i % 4], 16)
                if i == 7:
                    pool.wait_ge(W.omax_ready, 1)
                    W.reduce_o(pool)
                if i % SPAN_TILES == SPAN_TILES - 1:
                    pool.wait_ge(cmax_ready, i // SPAN_TILES + 1)
                    pool.partition_all_reduce(cmax_all[:, :], cmax[:, :], P, REDUCE.max).then_inc(cmax_reduced, 1)
            pool.wait_ge(W.qmax_ready, 1)
            W.reduce_qkv(pool)

        @block.scalar
        def _(act):
            def deviation(t):
                act.wait_ge(var_ready, t + 1)
                act.activation(std[:, :], mean_var[:, :, 1], ACT.Sqrt, scale=XN_SCALE ** -2,
                               bias=N.eps_tile[:, 0:1]).then_inc(std_ready, 1)

            def high(m, out, scale):
                act.wait_ge(turned, m + 1)
                act.activation(out, turn[m % 4][:, :, :], ACT.Copy, scale=scale).then_inc(hi_ready, 1)

            act.wait_ge(N.consts_ready, 1)
            for t in range(SPANS):
                deviation(t)
                act.wait_ge(cscale_ready, t + 1)
                for j in range(SPAN_TILES):
                    tile = SPAN_TILES * t + j
                    high(8 * t + j, N.c_hi[:, :, tile * P:(tile + 1) * P], N.c_scale[:, t:t + 1])
                for j in range(SPAN_TILES):
                    tile = SPAN_TILES * t + j
                    high(8 * t + 4 + j, N.x_hi[:, :, tile * P:(tile + 1) * P], 1.0)
                for i in range(SPAN_TILES * t, SPAN_TILES * (t + 1)):
                    act.wait_ge(rows_turned, i + 1)
                    act.activation(N.cos_t[:, i * P:(i + 1) * P], rope_ps[i % 2][:, 0, :], ACT.Copy)
                    act.activation(N.sin_t[:, i * P:(i + 1) * P], rope_ps[i % 2][:, 1, :], ACT.Copy).then_inc(rows_out, 1)
                if t == 1:
                    W.o_high(act, 0)
            W.k_high(act, 0)
            W.v_high(act, 0)
            W.q_high(act, 0, 0)
            W.q_high(act, 0, 1)

        @block.vector
        def _(dve):
            chain = Chain(dve, dve_step)
            dve.memset(N.eps_tile[:, :], EPS / XN_SCALE ** 2).then_inc(N.consts_ready, 1)
            dve.wait_ge(pos_in, 16)
            chain.step(dve.tensor_scalar(pos_wrap[:, :], pos[:, :], 0.0, float(MAX_POS), ALU.is_lt, ALU.mult))
            chain.step(dve.tensor_tensor(pos_wrap[:, :], pos_wrap[:, :], pos[:, :], ALU.add))
            dve.tensor_scalar(pos[:, :], pos_wrap[:, :], 0.0, float(MAX_POS - 1), ALU.max, ALU.min).then_inc(pos_ready, 1)

            def low_part(m, out, hi, scale):
                dve.wait_ge(hi_ready, m + 1)
                dve.scalar_tensor_tensor(out=out, in0=turn[m % 4][:, :, :], scalar=scale, in1=hi,
                                         op0=ALU.mult, op1=ALU.subtract).then_inc(lo_ready, 1)

            for t in range(SPANS):
                s = t % 2
                dve.wait_ge(ctx_in[s], 16 * (t // 2 + 1))
                if t:
                    dve.wait_ge(cmax_reduced, t)
                dve.tensor_reduce(cmax[:, :], ctx_raw[s][:, :, :], AX.XY, ALU.max,
                                  apply_absolute_value=True).then_inc(cmax_ready, 1)
                dve.wait_ge(x_in[s], 16 * (t // 2 + 1))
                for j in range(SPAN_TILES):
                    ins = dve.bn_stats(stats[:, j, :], N.acc[:, SPAN_TILES * t + j, :])
                chain.step(ins)
                if t:
                    dve.wait_ge(std_ready, t)
                for j in range(SPAN_TILES):
                    ins = dve.bn_aggr(mean_var[:, j, :], stats[:, j, :])
                ins.then_inc(var_ready, 1)
                if t == 2:
                    W.o_low(dve, 0)
                if t == 3:
                    W.max_qkv(dve, 0)
                dve.wait_ge(cmax_reduced, t + 1)
                pow2_scale(dve, chain, cmax_all[:, :], cpow[:, :], N.c_scale[:, t:t + 1], N.c_inv[:, t:t + 1], cscale_ready)
                dve.wait_ge(std_ready, t + 1)
                chain.step(dve.reciprocal(rstd[:, :], std[:, :]))
                for j in range(SPAN_TILES):
                    tile = SPAN_TILES * t + j
                    m = 8 * t + 4 + j
                    k = 8 * t + 4 + j - 2 if j >= 2 else 8 * (t - 1) + 4 + j + 2
                    if k > 0:
                        dve.wait_ge(turned, k + 1)
                    dve.tensor_scalar(normed[j % 2][:, :], N.acc[:, tile, :], mean_var[:, j, 0:1], rstd[:, j:j + 1],
                                      ALU.subtract, ALU.mult).then_inc(normed_ready, 1)
                    if j == 1:
                        for jj in range(SPAN_TILES):
                            ct = SPAN_TILES * t + jj
                            low_part(8 * t + jj, N.c_lo[:, :, ct * P:(ct + 1) * P], N.c_hi[:, :, ct * P:(ct + 1) * P],
                                     N.c_scale[:, t:t + 1])
                for j in range(SPAN_TILES):
                    tile = SPAN_TILES * t + j
                    low_part(8 * t + 4 + j, N.x_lo[:, :, tile * P:(tile + 1) * P], N.x_hi[:, :, tile * P:(tile + 1) * P], 1.0)
                if t == 0:
                    W.max_o(dve, 0)
                if t == 1:
                    W.scale_o(dve, chain, 0)
            dve.wait_ge(mask_in, 32)
            dve.tensor_scalar(N.pred[:, :, :], mask_raw[:, :, :], 0.0, None, ALU.is_equal).then_inc(pred_ready, 1)
            W.scale_qkv(dve, chain, 0)
            W.k_low(dve, 0)
            W.v_low(dve, 0)
            W.q_low(dve, 0, 0)
            W.q_low(dve, 0, 1)

        @block.tensor
        def _(pe):
            pe.wait_ge(ident_in, 1)

            def turn_tile(m, src):
                if m >= 4:
                    pe.wait_ge(lo_ready, m - 3)
                for kt in range(KT):
                    ins = pe.transpose(turn[m % 4][:, kt, :], src[:, kt * P:(kt + 1) * P], N.ident[:, :])
                ins.then_inc(turned, 1)

            for t in range(SPANS):
                pe.wait_ge(ctx_in[t % 2], 16 * (t // 2 + 1))
                for j in range(SPAN_TILES):
                    turn_tile(8 * t + j, ctx_raw[t % 2][:, j, :])
                for j in range(SPAN_TILES):
                    pe.wait_ge(normed_ready, SPAN_TILES * t + j + 1)
                    turn_tile(8 * t + 4 + j, normed[j % 2])
                for i in range(SPAN_TILES * t, SPAN_TILES * (t + 1)):
                    pe.wait_ge(rows_in[i % 4], 16 * (i // 4 + 1))
                    if i >= 2:
                        pe.wait_ge(rows_out, i - 1)
                    for c in range(2):
                        ins = pe.transpose(rope_ps[i % 2][:, c, :], rope_rows[i % 4][:, c * P:(c + 1) * P], N.ident[:, :])
                    ins.then_inc(rows_turned, 1)


def pow2_scale(dve, chain, amax, tmp, scale, inverse, ready):
    chain.step(dve.tensor_scalar(tmp, amax, TINY, None, ALU.max))
    chain.step(dve.tensor_scalar(amax.bitcast(I32), tmp.bitcast(I32), EXP_BITS, None, ALU.bitwise_and))
    chain.step(dve.tensor_scalar(inverse, amax, 1.0 / TOP, None, ALU.mult))
    ins = dve.reciprocal(scale, inverse)
    if ready is None:
        chain.step(ins)
    else:
        ins.then_inc(ready, 1)


def attend(nc, N):
    with ExitStack() as ctx:
        def sb(name, shape, dt):
            return ctx.enter_context(nc.sbuf_tensor(name, shape, dt))

        def sem(name):
            return N.sems.enter_context(nc.semaphore(name))

        W = N.weights
        k_hi = [sb(f"k_hi{i}", [P, SPAN], F16) for i in range(2)]
        k_lo = [sb(f"k_lo{i}", [P, SPAN], F16) for i in range(2)]
        v_sb = [sb(f"v_sb{i}", [P, SPAN_TILES, HEAD_DIM], F32) for i in range(2)]
        q_hi = [sb(f"q_hi{i}", [P, SPAN_BATCHES, 2, SEQ], F16) for i in range(2)]
        q_lo = [sb(f"q_lo{i}", [P, SPAN_BATCHES, 2, SEQ], F16) for i in range(2)]
        by_cos = [sb(f"by_cos{j}", [P, SPAN], F32) for j in range(2)]
        by_sin = [sb(f"by_sin{j}", [P, SPAN], F32) for j in range(2)]
        probs = [sb(f"probs{i}", [P, SPAN_BATCHES, SEQ], F32) for i in range(2)]
        probs_t = [sb(f"probs_t{i}", [P, SPAN_TILES, P], F32) for i in range(2)]
        raw_max = sb("raw_max", [P, SPAN_BATCHES], F32)
        neg_max = [sb(f"neg_max{i}", [P, SPAN_BATCHES], F32) for i in range(2)]
        row_sum = [sb(f"row_sum{i}", [P, SPAN_BATCHES], F32) for i in range(2)]
        row_inv = [sb(f"row_inv{i}", [P, SPAN_BATCHES], F32) for i in range(2)]
        o_hi = [sb(f"o_hi{i}", [P, GROUP, SPAN], F16) for i in range(2)]
        o_lo = [sb(f"o_lo{i}", [P, GROUP, SPAN], F16) for i in range(2)]

        def bank(name):
            return ctx.enter_context(nc.psum_tensor(name, [P, SPAN], F32))

        q_ps = [bank("q_ps0"), bank("q_ps1")]
        kv_ps = bank("kv_ps")
        s_ps = bank("s_ps")
        pair_ps = [bank("pair_ps0"), bank("pair_ps1")]
        y_ps = [bank("y_ps0"), bank("y_ps1")]

        q_done, q_free = [sem("q_done0"), sem("q_done1")], [sem("q_free0"), sem("q_free1")]
        q_summed, q_hi_ready, q_roped = sem("q_summed"), sem("q_hi_ready"), sem("q_roped")
        k_done, k_free, k_roped = sem("k_done"), sem("k_free"), sem("k_roped")
        k_summed, k_hi_ready = sem("k_summed"), sem("k_hi_ready")
        v_done, v_ready = sem("v_done"), sem("v_ready")
        scores_scaled = sem("scores_scaled")
        s_done, filled, raw_max_ready, max_ready, exp_done, inv_ready, p_ready = (
            sem("s_done"), sem("filled"), sem("raw_max_ready"), sem("max_ready"), sem("exp_done"), sem("inv_ready"), sem("p_ready"))
        t_done, pt_ready = sem("t_done"), sem("pt_ready")
        pv_done, o_hi_ready, o_ready = sem("pv_done"), sem("o_hi_ready"), sem("o_ready")
        y_done, y_added = sem("y_done"), sem("y_added")
        dve_step = sem("a_dve_step")
        STEPS = W.STEPS

        block = ctx.enter_context(nc.Block())
        SLOTS = [(t, u) for t in range(SPANS) for u in range(2)]

        def groups(eng, body):
            body(0)
            with eng.Fori(1, KV_HEADS - 1) as g:
                body(g)
            body(KV_HEADS - 1)

        def is_last(g):
            return isinstance(g, int) and g == KV_HEADS - 1

        def o_view(buf, u, e):
            return buf[:, 2 * u:2 * u + 2, :].rearrange("p h (b e q) -> p e b h q", e=2, q=SEQ)[:, e, :, :, :]

        def o_psum(e):
            return pair_ps[1 - e][:, :].rearrange("p (b h q) -> p b h q", b=4, h=2)

        @block.sync
        def _(sp):
            with sp.Fori(1, KV_HEADS) as g:
                W.load(sp, g)

        @block.gpsimd
        def _(pool):
            def sum_q(n, j):
                pool.wait_ge(q_free[j], n + 1)
                pool.tensor_tensor(by_cos[j][:, :], by_cos[j][:, :], by_sin[j][:, :], ALU.add).then_inc(q_summed, 1)

            def low_q(n, par, j):
                if j == 0:
                    at_least(pool, s_done, n - 1)
                pool.wait_ge(q_hi_ready, 2 * n + j + 1)
                pool.tensor_tensor(q_lo[par][:, :, j, :], by_cos[j][:, :].rearrange("p (b q) -> p b q", q=SEQ),
                                   q_hi[par][:, :, j, :], ALU.subtract).then_inc(q_roped, 1)

            def rotate_q(n, par):
                for j in range(2):
                    sum_q(n, j)
                for j in range(2):
                    low_q(n, par, j)

            def sum_k(tau):
                pool.wait_ge(k_free, tau + 1)
                pool.tensor_tensor(by_cos[0][:, :], by_cos[0][:, :], by_sin[0][:, :], ALU.add).then_inc(k_summed, 1)

            def low_k(tau, par):
                at_least(pool, s_done, 2 * (tau - 1))
                pool.wait_ge(k_hi_ready, tau + 1)
                pool.tensor_tensor(k_lo[par][:, :], by_cos[0][:, :], k_hi[par][:, :], ALU.subtract).then_inc(k_roped, 1)

            def normalize(n, u, maxima=None, count=None):
                if maxima is not None:
                    pool.wait_ge(maxima, count)
                pool.wait_ge(inv_ready, n + 1)
                pool.tensor_tensor(probs[u][:, :, :], probs[u][:, :, :],
                                   row_inv[u][:, :].unsqueeze(2).to_broadcast([P, SPAN_BATCHES, SEQ]),
                                   ALU.mult).then_inc(p_ready, 1)

            sum_k(0)
            low_k(0, 0)
            rotate_q(0, 0)

            def body(g):
                for slot, (t, u) in enumerate(SLOTS):
                    tau = 4 * g + t
                    n = 2 * tau + u
                    more = not is_last(g) or slot < 7
                    if more:
                        rotate_q(n + 1, 1 - u)
                    next_keys = u == 0 and not (is_last(g) and t == SPANS - 1)
                    if next_keys:
                        sum_k(tau + 1)
                    if is_last(g) or slot not in (2, 5):
                        normalize(n, u)
                    elif slot == 2:
                        normalize(n, u, W.omax_ready, g + 2)
                        W.reduce_o(pool)
                    else:
                        normalize(n, u, W.qmax_ready, g + 2)
                        W.reduce_qkv(pool)
                    if next_keys:
                        low_k(tau + 1, (t + 1) % 2)

            groups(pool, body)

        @block.scalar
        def _(act):
            def turned_probs(n, u):
                act.wait_ge(t_done, n + 1)
                act.activation(probs_t[u][:, :, :].rearrange("p a b -> p (a b)"), pair_ps[0][:, :], ACT.Copy).then_inc(pt_ready, 1)

            def query_hi(n, par, j):
                if j == 0:
                    at_least(act, s_done, n - 1)
                act.wait_ge(q_summed, 2 * n + j + 1)
                act.activation(q_hi[par][:, :, j, :], by_cos[j][:, :].rearrange("p (b q) -> p b q", q=SEQ),
                               ACT.Copy).then_inc(q_hi_ready, 1)

            def key_hi(tau, par):
                at_least(act, s_done, 2 * (tau - 1))
                act.wait_ge(k_summed, tau + 1)
                act.activation(k_hi[par][:, :], by_cos[0][:, :], ACT.Copy).then_inc(k_hi_ready, 1)

            def exponentials(n, u, t):
                act.wait_ge(max_ready, n + 1)
                at_least(act, t_done, n - 1)
                for b in range(SPAN_BATCHES):
                    ins = act.activation(probs[u][:, b, :], s_ps[:, b * SEQ:(b + 1) * SEQ], ACT.Exp,
                                         scale=W.score_scale[:, t:t + 1], bias=neg_max[u][:, b:b + 1],
                                         accum_out=row_sum[u][:, b:b + 1])
                ins.then_inc(exp_done, 1)

            def values(tau, par):
                act.wait_ge(v_done, tau + 1)
                at_least(act, pv_done, 4 * (tau - 1))
                act.activation(v_sb[par][:, :, :].rearrange("p a b -> p (a b)"), kv_ps[:, :], ACT.Copy,
                               scale=V_SCALE).then_inc(v_ready, 1)

            def outputs_hi(n, tau, par, u):
                at_least(act, y_done, 4 * tau - 4)
                for hf in (0, 1):
                    act.wait_ge(pv_done, 2 * n + hf + 1)
                    act.activation(o_view(o_hi[par], u, hf), o_psum(hf), ACT.Copy).then_inc(o_hi_ready, 1)

            key_hi(0, 0)
            query_hi(0, 0, 0)
            query_hi(0, 0, 1)
            values(0, 0)

            def body(g):
                first = isinstance(g, int) and g == 0
                for slot, (t, u) in enumerate(SLOTS):
                    tau = 4 * g + t
                    n = 2 * tau + u
                    prev = not (first and slot == 0)
                    more = not (is_last(g) and slot == 7)
                    if more:
                        query_hi(n + 1, 1 - u, 0)
                    if prev:
                        turned_probs(n - 1, 1 - u)
                    if more:
                        query_hi(n + 1, 1 - u, 1)
                    exponentials(n, u, t)
                    if u == 0 and not (is_last(g) and t == SPANS - 1):
                        key_hi(tau + 1, (t + 1) % 2)
                    if u == 1 and not (is_last(g) and t == SPANS - 1):
                        values(tau + 1, (t + 1) % 2)
                    if prev:
                        pt, pp = (tau, t % 2) if u else (tau - 1, (t + 1) % 2)
                        outputs_hi(n - 1, pt, pp, 1 - u)
                    if not is_last(g):
                        if slot == 3:
                            at_least(act, y_done, 16 * g)
                            W.o_high(act, g + 1)
                        if slot == 5:
                            act.wait_ge(k_done, 4 * g + 4)
                            W.k_high(act, g + 1)
                        if slot == 6:
                            act.wait_ge(v_done, 4 * g + 4)
                            W.v_high(act, g + 1)
                            act.wait_ge(q_done[1], 8 * g + 7)
                            W.q_high(act, g + 1, 0)
                        if slot == 7:
                            act.wait_ge(q_done[1], 8 * g + 8)
                            W.q_high(act, g + 1, 1)

            groups(act, body)
            last = 2 * SPANS * KV_HEADS - 1
            turned_probs(last, 1)
            outputs_hi(last, SPANS * KV_HEADS - 1, 1, 1)

        @block.vector
        def _(dve):
            chain = Chain(dve, dve_step)

            def rotate(ps, j, span, free):
                cols = slice(span * SPAN, (span + 1) * SPAN)
                dve.scalar_tensor_tensor(out=by_cos[j][:, :], in0=ps[:, :], scalar=QK_SCALE, in1=N.cos_t[:, cols],
                                         op0=ALU.mult, op1=ALU.mult)
                for a, b in ((0, 64), (64, 0)):
                    ins = dve.scalar_tensor_tensor(out=by_sin[j][b:b + 64, :], in0=ps[a:a + 64, :], scalar=QK_SCALE,
                                                   in1=N.sin_t[a:a + 64, cols], op0=ALU.mult, op1=ALU.mult)
                ins.then_inc(free, 1)

            def rotate_q(n, span):
                for j in range(2):
                    dve.wait_ge(q_done[j], n + 1)
                    at_least(dve, q_roped, 2 * n + j - 1)
                    rotate(q_ps[j], j, span, q_free[j])

            def rotate_k(tau, span):
                dve.wait_ge(k_done, tau + 1)
                rotate(kv_ps, 0, span, k_free)

            def row_max(n, u, t):
                dve.wait_ge(s_done, 1)
                dve.wait_ge(s_done, n + 1)
                s3 = s_ps[:, :].rearrange("p (b k) -> p b k", b=SPAN_BATCHES)
                dve.copy_predicated(s3, N.pred[:, t * SPAN_BATCHES:(t + 1) * SPAN_BATCHES, :],
                                    W.masked_raw[:, t:t + 1].unsqueeze(2).to_broadcast([P, SPAN_BATCHES, SEQ])).then_inc(filled, 1)
                dve.wait_ge(filled, n + 1)
                dve.tensor_reduce(raw_max[:, :], s3, AX.X, ALU.max, negate=True).then_inc(raw_max_ready, 1)
                dve.wait_ge(raw_max_ready, n + 1)
                dve.tensor_scalar(neg_max[u][:, :], raw_max[:, :], W.score_scale[:, t:t + 1], None,
                                  ALU.mult).then_inc(max_ready, 1)

            def row_inverse(n, u):
                dve.wait_ge(exp_done, n + 1)
                dve.reciprocal(row_inv[u][:, :], row_sum[u][:, :]).then_inc(inv_ready, 1)

            def outputs_lo(n, par, u):
                for hf in (0, 1):
                    dve.wait_ge(o_hi_ready, 2 * n + hf + 1)
                    dve.tensor_tensor(o_view(o_lo[par], u, hf), o_psum(hf), o_view(o_hi[par], u, hf),
                                      ALU.subtract).then_inc(o_ready, 1)

            def add_y(tau, g, span, i):
                m = 4 * tau + i
                dve.wait_ge(y_done, m + 1)
                at_least(dve, y_added, m - 1)
                tile = N.acc[:, span * SPAN_TILES + i, :]
                dve.scalar_tensor_tensor(out=tile, in0=y_ps[i % 2][:, :], scalar=W.inv_y[:, g & 1, span:span + 1],
                                         in1=tile, op0=ALU.mult, op1=ALU.add).then_inc(y_added, 1)

            def token_stats(tau, span, i):
                dve.wait_ge(y_added, 4 * tau + i + 1)
                dve.bn_stats(N.stats[:, span * SPAN_TILES + i, :], N.acc[:, span * SPAN_TILES + i, :])

            rotate_k(0, 0)
            dve.wait_ge(k_roped, 1)
            rotate_q(0, 0)

            def body(g):
                chain.base, chain.n = STEPS * g, 0
                first = isinstance(g, int) and g == 0
                dve.tensor_copy(W.score_now[:, :, :], W.score_next[:, :, :]).then_inc(scores_scaled, 1)
                dve.wait_ge(scores_scaled, g + 1)
                for slot, (t, u) in enumerate(SLOTS):
                    tau = 4 * g + t
                    n = 2 * tau + u
                    if not (is_last(g) and slot == 7):
                        if u == 1:
                            dve.wait_ge(k_roped, tau + 2)
                        rotate_q(n + 1, (slot + 1) // 2 % SPANS)
                    row_max(n, u, t)
                    if u == 0 and not (is_last(g) and t == SPANS - 1):
                        dve.wait_ge(q_roped, 2 * n + 3)
                        rotate_k(tau + 1, (t + 1) % SPANS)
                    row_inverse(n, u)
                    if not (first and slot == 0):
                        outputs_lo(n - 1, t % 2 if u else (t + 1) % 2, 1 - u)
                    back = 1 if u else 2
                    if not (first and t < back):
                        yg = g - 1 if t < back else g
                        for i in ((0, 1) if u else (2, 3)):
                            add_y(tau - back, yg, (t - back) % SPANS, i)
                        if is_last(g) and t >= back:
                            for i in ((0, 1) if u else (2, 3)):
                                token_stats(tau - back, t - back, i)
                    if not is_last(g):
                        if slot == 1:
                            W.max_o(dve, g + 1)
                        if slot == 2:
                            W.scale_o(dve, chain, g + 1)
                        if slot == 3:
                            W.o_low(dve, g + 1)
                        if slot == 4:
                            W.max_qkv(dve, g + 1)
                        if slot == 5:
                            W.scale_qkv(dve, chain, g + 1)
                            W.k_low(dve, g + 1)
                        if slot == 6:
                            W.v_low(dve, g + 1)
                            W.q_low(dve, g + 1, 0)
                        if slot == 7:
                            W.q_low(dve, g + 1, 1)
                assert is_last(g) or chain.n == STEPS

            groups(dve, body)
            g = KV_HEADS - 1
            tau = 4 * g + 3
            outputs_lo(2 * tau + 1, 1, 1)
            for i in (2, 3):
                add_y(tau - 1, g, 2, i)
            for i in (2, 3):
                token_stats(tau - 1, 2, i)
            for i in range(4):
                add_y(tau, g, 3, i)
                if i:
                    token_stats(tau, 3, i - 1)
            token_stats(tau, 3, 3)

        @block.tensor
        def _(pe):
            def product3(out, pairs):
                steps = [(a, b) for ah, al, bh, bl in pairs for a, b in ((ah, bh), (ah, bl), (al, bh))]
                for s, (a, b) in enumerate(steps):
                    ins = pe.matmul(out, a, b, start=(s == 0), stop=(s == len(steps) - 1))
                return ins

            def queries(n, hp, span, new, g):
                cols = slice(span * SPAN, (span + 1) * SPAN)
                if new:
                    pe.wait_ge(W.wq_ready, 2 * g + hp + 1)
                for j in range(2):
                    at_least(pe, q_free[j], n)
                    h = slice((2 * hp + j) * HEAD_DIM, (2 * hp + j + 1) * HEAD_DIM)
                    product3(q_ps[j][:, :], [(W.wq_hi[:, k, h], W.wq_lo[:, k, h], N.x_hi[:, k, cols], N.x_lo[:, k, cols])
                                             for k in range(KT)]).then_inc(q_done[j], 1)

            def keys(tau, span, new, g):
                cols = slice(span * SPAN, (span + 1) * SPAN)
                if new:
                    pe.wait_ge(W.wk_ready, g + 1)
                at_least(pe, v_ready, tau)
                product3(kv_ps[:, :], [(W.wk_hi[:, k, :], W.wk_lo[:, k, :], N.c_hi[:, k, cols], N.c_lo[:, k, cols])
                                       for k in range(KT)]).then_inc(k_done, 1)

            def values(tau, span, new, g):
                if new:
                    pe.wait_ge(W.wv_ready, g + 1)
                pe.wait_ge(k_free, tau + 1)
                for j in range(SPAN_TILES):
                    rows = slice(span * SPAN + j * P, span * SPAN + (j + 1) * P)
                    ins = product3(kv_ps[:, j * P:(j + 1) * P],
                                   [(N.c_hi[:, k, rows], N.c_lo[:, k, rows], W.wv_hi[:, k, :], W.wv_lo[:, k, :]) for k in range(KT)])
                ins.then_inc(v_done, 1)

            def turn_probs(n, u):
                pe.wait_ge(p_ready, n + 1)
                at_least(pe, o_ready, 2 * n)
                for j in range(SPAN_TILES):
                    ins = pe.transpose(pair_ps[0][:, j * P:(j + 1) * P],
                                       probs[u][:, 2 * j:2 * j + 2, :].rearrange("p b k -> p (b k)"), N.ident[:, :])
                ins.then_inc(t_done, 1)

            def scores(n, u, tau, par):
                pe.wait_ge(q_roped, 2 * n + 2)
                pe.wait_ge(k_roped, tau + 1)
                at_least(pe, exp_done, n)
                for b in range(SPAN_BATCHES):
                    rows = slice(b * SEQ, (b + 1) * SEQ)
                    ins = product3(s_ps[:, rows], [(q_hi[u][:, b, :, :].rearrange("p h q -> p (h q)"),
                                                    q_lo[u][:, b, :, :].rearrange("p h q -> p (h q)"),
                                                    k_hi[par][:, rows], k_lo[par][:, rows])])
                ins.then_inc(s_done, 1)

            def head_outputs(n, u, tau, par):
                pe.wait_ge(pt_ready, n + 1)
                pe.wait_ge(v_ready, tau + 1)
                at_least(pe, o_ready, 2 * n)
                for b in range(SPAN_BATCHES):
                    j, e = b // 2, b % 2
                    rows = slice(SEQ * e, SEQ * e + SEQ)
                    ins = pe.matmul(pair_ps[1 - e][:, j * P:(j + 1) * P], v_sb[par][rows, j, :],
                                    probs_t[u][rows, j, :], start=True, stop=True)
                    if j == 3:
                        ins.then_inc(pv_done, 1)

            def project(tau, par, i, g):
                m = 4 * tau + i
                if i == 0:
                    pe.wait_ge(W.wo_ready, g + 1)
                pe.wait_ge(o_ready, 4 * tau + 4)
                at_least(pe, y_added, m - 1)
                rows = slice(i * P, (i + 1) * P)
                product3(y_ps[i % 2][:, :], [(o_hi[par][:, h, rows], o_lo[par][:, h, rows],
                                              W.wo_hi[:, g & 1, h, :], W.wo_lo[:, g & 1, h, :])
                                             for h in range(GROUP)]).then_inc(y_done, 1)

            keys(0, 0, True, 0)
            queries(0, 0, 0, True, 0)
            values(0, 0, True, 0)

            def body(g):
                first = isinstance(g, int) and g == 0
                for slot, (t, u) in enumerate(SLOTS):
                    tau = 4 * g + t
                    n = 2 * tau + u
                    if not (is_last(g) and slot == 7):
                        queries(n + 1, 1 - u, (slot + 1) // 2 % SPANS, slot in (7, 0), g + 1 if slot == 7 else g)
                    if not (first and slot == 0):
                        turn_probs(n - 1, 1 - u)
                    scores(n, u, tau, t % 2)
                    if not (is_last(g) and t == SPANS - 1):
                        gn, new = (g + 1, True) if t == 3 else (g, False)
                        (values if u else keys)(tau + 1, (t + 1) % SPANS, new, gn)
                    if not (first and slot == 0):
                        head_outputs(n - 1, 1 - u, tau if u else tau - 1, t % 2 if u else (t + 1) % 2)
                    back = 1 if u else 2
                    if not (first and t < back):
                        for i in ((0, 1) if u else (2, 3)):
                            project(tau - back, (t - back) % 2, i, g - 1 if t < back else g)

            groups(pe, body)
            g = KV_HEADS - 1
            tau = 4 * g + 3
            turn_probs(2 * tau + 1, 1)
            head_outputs(2 * tau + 1, 1, tau, 1)
            for i in (2, 3):
                project(tau - 1, 0, i, g)
            for i in range(4):
                project(tau, 1, i, g)


def feed(nc, N):
    with ExitStack() as ctx:
        def sb(name, shape, dt):
            return ctx.enter_context(nc.sbuf_tensor(name, shape, dt))

        def sem(name):
            return N.sems.enter_context(nc.semaphore(name))

        w_nat = [sb(f"w_nat{w}", [P, OCT, 2, EMB8], F32) for w in range(2)]
        wd_nat = sb("wd_nat", [P, OCT // 2, HID8], F32)
        below = sb("below", [P, OCT * 2 * EMB8], F16)
        tern = [sb(f"tern{w}", [P, OCT, 2, 2, EMB8], F16) for w in range(2)]
        ternd = [sb(f"ternd{w}", [P, OCT // 2, HID8], F16) for w in range(2)]
        tern_t = [sb(f"tern_t{w}", [P, OCT, HID8], F16) for w in range(2)]
        signs = sb("signs", [P, 4], F32)
        ident16 = sb("ident16", [P, P], F16)
        wsum, wsum_all = sb("wsum", [P, 3], F32), sb("wsum_all", [P, 3], F32)
        half, nhalf, spow = sb("half", [P, 3], F32), sb("nhalf", [P, 3], F32), sb("spow", [P, 3], F32)
        m_in = [sb("m_gate", [P, KT, HIDDEN], F16), sb("m_up", [P, KT, HIDDEN], F16)]
        down_rows = sb("down_rows", [P, OCT // 2, HIDDEN], F16)
        m_down = sb("m_down", [P, HCHUNKS, EMB], F16)
        normed = [sb(f"normed2_{j}", [P, EMB], F32) for j in range(SPAN_TILES)]
        mean_var = sb("mean_var2", [P, TILES, 2], F32)
        std, rstd = sb("std2", [P, TILES], F32), sb("rstd2", [P, TILES], F32)
        silu = [sb(f"silu{i}", [P, SPAN], F32) for i in range(2)]
        hid = [sb(f"hid{i}", [P, SPAN], F32) for i in range(2)]
        h_hi = sb("h_hi", [P, HCHUNKS, SPAN], F16)
        h_lo = sb("h_lo", [P, HCHUNKS, SPAN], F16)
        result = [sb(f"result{i}", [P, EMB], F32) for i in range(2)]

        def bank(name, shape=(P, SPAN)):
            return ctx.enter_context(nc.psum_tensor(name, list(shape), F32))

        turn = [bank(f"turn2_{i}", (P, KT, P)) for i in range(2)]
        gate_ps = [bank(f"gate_ps{i}") for i in range(2)]
        up_ps = [bank(f"up_ps{i}") for i in range(2)]
        y_ps = [bank(f"y2_ps{i}") for i in range(2)]
        tern_ps = [y_ps, up_ps]

        wffn_in, const_ready = sem("wffn_in"), sem("f_const_ready")
        wsum_ready, wsum_reduced = sem("wsum_ready"), sem("wsum_reduced")
        tern_ready, tern_turned, tern_out = sem("tern_ready"), sem("tern_turned"), sem("tern_out")
        m_by_dve, m_by_act = sem("m_by_dve"), sem("m_by_act")
        down_ready, down_turned, down_out = sem("down_ready"), sem("down_turned"), sem("down_out")
        var_ready, std_ready, normed_ready = sem("var2_ready"), sem("std2_ready"), sem("normed2_ready")
        turned, hi_ready, lo_ready = sem("turned2"), sem("hi2_ready"), sem("lo2_ready")
        gate_done, up_done, silu_ready, hid_ready = sem("gate_done"), sem("up_done"), sem("silu_ready"), sem("hid_ready")
        h_hi_ready, h_ready = sem("h_hi_ready"), sem("h_ready")
        y_done, result_ready = sem("y2_done"), sem("result_ready")
        stored = [sem(f"stored{i}") for i in range(2)]
        dve_step = sem("f_dve_step")

        block = ctx.enter_context(nc.Block())
        ROWS = HID8 // 2
        STEP = ROWS + ROWS % 2
        AHEAD, DOWN_FROM = 4, 2
        DOWN_TURNS = {4: (0,), 5: (1, 2), 6: (3,), 7: (4, 5), 8: (6,), 9: (7, 8), 10: (9, 10)}

        def chunk_rows(c):
            return P if c < HCHUNKS - 1 else HLAST

        def last_block(c):
            return (c * P + chunk_rows(c) - 1) // HID8

        def sign_pair(s_even, s_odd):
            col = (2 if s_even < 0 else 0) + (1 if s_odd < 0 else 0)
            return signs[:, col:col + 1]

        def expand(w, kt, k):
            return (m_in[w][:, kt, k * HID8:(k + 1) * HID8], tern_t[w][:, (2 * kt) ^ k, :],
                    sign_pair(SIGN[2 * kt][k], SIGN[2 * kt + 1][k]))

        def spans(eng, body):
            body(0)
            with eng.Fori(1, SPANS - 1) as t:
                body(t)
            body(SPANS - 1)

        def is_first(t):
            return isinstance(t, int) and t == 0

        def is_last(t):
            return isinstance(t, int) and t == SPANS - 1

        def token_cols(m):
            return bass.ds(m * P, P)

        @block.sync
        def _(sp):
            for w, dram in enumerate((N.w_gate, N.w_up)):
                sp.dma_start(w_nat[w][0:ROWS, :, :, :], dram.rearrange("j (h p) d -> p j h d", p=ROWS)).then_inc(wffn_in, 16)
            for e in range(2):
                sp.dma_start(wd_nat[64 * e:64 * e + 64, :, :],
                             N.w_down.rearrange("(a e) o d -> e o a d", e=2)[e]).then_inc(wffn_in, 16)
            with sp.Fori(0, SPANS) as t:
                for i in range(SPAN_TILES):
                    sp.wait_ge(result_ready, 4 * t + i + 1)
                    sp.dma_start(N.out[bass.ds((t * SPAN_TILES + i) * P, P), :], result[i % 2][:, :]).then_inc(stored[i % 2], 16)
            for s in stored:
                sp.wait_ge(s, 16 * TILES // 2)

        @block.gpsimd
        def _(pool):
            pool.wait_ge(wsum_ready, 1)
            pool.partition_all_reduce(wsum_all[:, :], wsum[:, :], P, REDUCE.add).then_inc(wsum_reduced, 1)
            with pool.Fori(0, SPANS) as t:
                for c in range(HCHUNKS):
                    rows = chunk_rows(c)
                    pool.wait_ge(h_hi_ready, HCHUNKS * t + c + 1)
                    pool.tensor_tensor(h_lo[0:rows, c, :], hid[c % 2][0:rows, :], h_hi[0:rows, c, :],
                                       ALU.subtract).then_inc(h_ready, 1)

        @block.scalar
        def _(act):
            act.wait_ge(var_ready, 1)
            act.activation(std[:, :], mean_var[:, :, 1], ACT.Sqrt, scale=XN_SCALE ** -2, bias=N.eps_tile[:, 0:1]).then_inc(std_ready, 1)

            def high(m, i):
                act.wait_ge(turned, 1)
                act.wait_ge(turned, m + 1)
                act.activation(N.x_hi[:, :, token_cols(m)], turn[i % 2][:, :, :], ACT.Copy).then_inc(hi_ready, 1)

            def transposed_out(w):
                for part in range(2):
                    act.wait_ge(tern_turned, 2 * w + part + 1)
                    act.activation(tern_t[w][:, 4 * part:4 * part + 4, :].rearrange("p j (h o) -> p (j h) o", h=2),
                                   tern_ps[w][part][:, :].bitcast(F16)[:, 0:8 * STEP].rearrange("p (a o) -> p a o", a=8)[:, :, 0:ROWS],
                                   ACT.Copy).then_inc(tern_out, 1)

            def expand_last(k):
                for w in range(2):
                    out, src, sign = expand(w, KT - 1, k)
                    ins = act.activation(out, src, ACT.Copy, scale=sign)
                ins.then_inc(m_by_act, 1)

            high(0, 0)
            high(1, 1)
            transposed_out(0)
            high(2, 2)
            high(3, 3)
            transposed_out(1)
            act.wait_ge(tern_out, 4)
            for k in range(AHEAD):
                expand_last(k)

            def body(t):
                def hidden_hi(c):
                    rows = chunk_rows(c)
                    act.wait_ge(hid_ready, HCHUNKS * t + c + 1)
                    act.activation(h_hi[0:rows, c, :], hid[c % 2][0:rows, :], ACT.Copy).then_inc(h_hi_ready, 1)

                for c in range(HCHUNKS):
                    rows = chunk_rows(c)
                    act.wait_ge(gate_done, HCHUNKS * t + c + 1)
                    act.activation(silu[c % 2][0:rows, :], gate_ps[c % 2][0:rows, :], ACT.Silu,
                                   scale=N.ffn_factor[0:rows, 0:1]).then_inc(silu_ready, 1)
                    if c >= 1:
                        hidden_hi(c - 1)
                    if is_first(t):
                        if AHEAD + c < OCT:
                            expand_last(AHEAD + c)
                        for d in DOWN_TURNS.get(c, ()):
                            act.wait_ge(down_turned, d + 1)
                            act.activation(m_down[0:chunk_rows(d), d, :],
                                           y_ps[d % 2][0:chunk_rows(d), :].bitcast(F16)[:, 0:EMB], ACT.Copy).then_inc(down_out, 1)
                    if not is_last(t) and c in (2, 4, 6, 8):
                        i = (c - 2) // 2
                        high(SPAN_TILES * (t + 1) + i, i)
                hidden_hi(HCHUNKS - 1)

            spans(act, body)

        @block.vector
        def _(dve):
            chain = Chain(dve, dve_step)
            for i in range(TILES):
                ins = dve.bn_aggr(mean_var[:, i, :], N.stats[:, i, :])
            ins.then_inc(var_ready, 1)
            dve.tensor_copy(ident16[:, :], N.ident[:, :])
            for col in range(4):
                dve.memset(signs[0:64, col:col + 1], -1.0 if col & 2 else 1.0)
                dve.memset(signs[64:P, col:col + 1], -1.0 if col & 1 else 1.0)
            dve.memset(wsum[:, :], 0.0).then_inc(const_ready, 1)
            dve.wait_ge(const_ready, 1)

            dve.wait_ge(wffn_in, 16 * 4)
            for w in range(2):
                dve.tensor_reduce(wsum[0:ROWS, w:w + 1], w_nat[w][0:ROWS, :, :, :], AX.XYZ, ALU.add, apply_absolute_value=True)
            dve.tensor_reduce(wsum[:, 2:3], wd_nat[:, :, :], AX.XY, ALU.add, apply_absolute_value=True).then_inc(wsum_ready, 1)

            dve.wait_ge(std_ready, 1)
            chain.step(dve.reciprocal(rstd[:, :], std[:, :]))

            def normalize(m, i):
                at_least(dve, turned, m - 3)
                dve.tensor_scalar(normed[i][:, :], N.acc[:, bass.ds(m, 1), :].rearrange("p a e -> p (a e)"),
                                  mean_var[:, bass.ds(m, 1), 0:1].rearrange("p a b -> p (a b)"), rstd[:, bass.ds(m, 1)],
                                  ALU.subtract, ALU.mult).then_inc(normed_ready, 1)

            def low(m, i):
                dve.wait_ge(hi_ready, m + 1)
                dve.tensor_tensor(N.x_lo[:, :, token_cols(m)], turn[i % 2][:, :, :], N.x_hi[:, :, token_cols(m)],
                                  ALU.subtract).then_inc(lo_ready, 1)

            for i in range(SPAN_TILES):
                normalize(i, i)

            dve.wait_ge(wsum_reduced, 1)
            chain.step(dve.tensor_scalar(N.ffn_scale[:, :], wsum_all[:, :], 1.0 / FFN_COUNT, None, ALU.mult))
            dve.tensor_scalar(half[:, :], N.ffn_scale[:, :], 0.5, None, ALU.mult)
            chain.step(dve.tensor_scalar(nhalf[:, :], N.ffn_scale[:, :], -0.5, None, ALU.mult))

            def ternary_in(w):
                r = slice(0, ROWS)
                b = below[r, :].rearrange("p (j h d) -> p j h d", j=OCT, h=2)
                chain.step(dve.tensor_scalar(b, w_nat[w][r, :, :, :], nhalf[r, w:w + 1], None, ALU.is_lt))
                chain.step(dve.scalar_tensor_tensor(out=tern[w][r, :, :, 0, :], in0=w_nat[w][r, :, :, :], scalar=half[r, w:w + 1],
                                                    in1=b, op0=ALU.is_gt, op1=ALU.subtract))
                pairs = tern[w][r, :, :, :, :].rearrange("p (a e) h c d -> p e a h c d", e=2)
                dve.tensor_copy(pairs[:, 0, :, :, 1, :], pairs[:, 1, :, :, 0, :])
                dve.tensor_copy(pairs[:, 1, :, :, 1, :], pairs[:, 0, :, :, 0, :]).then_inc(tern_ready, 1)

            ternary_in(0)
            low(0, 0)
            low(1, 1)
            ternary_in(1)
            low(2, 2)
            low(3, 3)

            def expand_first(k):
                for w in range(2):
                    for kt in range(KT - 1):
                        out, src, sign = expand(w, kt, k)
                        ins = dve.tensor_scalar(out, src, sign, None, ALU.mult)
                ins.then_inc(m_by_dve, 1)

            chain.step(dve.tensor_scalar(spow[:, 0:1], N.ffn_scale[:, 0:1], TINY, None, ALU.max))
            chain.step(dve.tensor_scalar(spow[:, 1:2].bitcast(I32), spow[:, 0:1].bitcast(I32), EXP_BITS, None, ALU.bitwise_and))
            chain.step(dve.reciprocal(spow[:, 2:3], spow[:, 1:2]))
            chain.step(dve.tensor_scalar(N.ffn_factor[:, 0:1], N.ffn_scale[:, 0:1], 1.0 / XN_SCALE, None, ALU.mult))
            chain.step(dve.tensor_scalar(N.ffn_factor[:, 1:2], spow[:, 2:3], H_SCALE / XN_SCALE, None, ALU.mult))
            chain.step(dve.tensor_tensor(spow[:, 0:1], spow[:, 1:2], N.ffn_scale[:, 1:2], ALU.mult))
            chain.step(dve.tensor_scalar(N.ffn_factor[:, 2:3], spow[:, 0:1], N.ffn_scale[:, 2:3], 1.0 / H_SCALE, ALU.mult, ALU.mult))
            dve.wait_ge(tern_out, 4)
            for k in range(AHEAD):
                expand_first(k)

            def ternary_down():
                b = below[:, 0:OCT // 2 * HID8].rearrange("p (a d) -> p a d", a=OCT // 2)
                chain.step(dve.tensor_scalar(b, wd_nat[:, :, :], nhalf[:, 2:3], None, ALU.is_lt))
                chain.step(dve.scalar_tensor_tensor(out=ternd[0][:, :, :], in0=wd_nat[:, :, :], scalar=half[:, 2:3], in1=b,
                                                    op0=ALU.is_gt, op1=ALU.subtract))
                dve.tensor_copy(ternd[1][0:64, :, :], ternd[0][64:P, :, :])
                chain.step(dve.tensor_copy(ternd[1][64:P, :, :], ternd[0][0:64, :, :]))

            def down_block(i):
                for kp in range(OCT // 2):
                    ins = dve.tensor_scalar(down_rows[:, kp, i * HID8:(i + 1) * HID8], ternd[i % 2][:, (i // 2) ^ kp, :],
                                            sign_pair(SIGN[i][2 * kp], SIGN[i][2 * kp + 1]), None, ALU.mult)
                ins.then_inc(down_ready, 1)

            def body(t):
                for c in range(HCHUNKS):
                    rows = chunk_rows(c)
                    n = HCHUNKS * t + c
                    dve.wait_ge(silu_ready, n + 1)
                    dve.wait_ge(up_done, n + 1)
                    at_least(dve, h_ready, n - 1 if c >= 1 else n)
                    dve.scalar_tensor_tensor(out=hid[c % 2][0:rows, :], in0=silu[c % 2][0:rows, :],
                                             scalar=N.ffn_factor[0:rows, 1:2], in1=up_ps[c % 2][0:rows, :],
                                             op0=ALU.mult, op1=ALU.mult).then_inc(hid_ready, 1)
                    if is_first(t):
                        if AHEAD + c < OCT:
                            expand_first(AHEAD + c)
                        if c == DOWN_FROM - 1:
                            ternary_down()
                        if 0 <= c - DOWN_FROM < OCT:
                            down_block(c - DOWN_FROM)
                    if not is_last(t):
                        if c in (3, 5, 7, 9):
                            i = (c - 3) // 2
                            low(SPAN_TILES * (t + 1) + i, i)
                        if c in (1, 3, 5, 7):
                            i = (c - 1) // 2
                            normalize(SPAN_TILES * (t + 1) + i, i)
                for i in range(SPAN_TILES):
                    m = SPAN_TILES * t + i
                    dve.wait_ge(y_done, m + 1)
                    if not (is_first(t) and i < 2):
                        dve.wait_ge(stored[i % 2], 16 * (2 * t + i // 2))
                    dve.scalar_tensor_tensor(out=result[i % 2][:, :], in0=y_ps[i % 2][:, :], scalar=N.ffn_factor[:, 2:3],
                                             in1=N.acc[:, bass.ds(m, 1), :].rearrange("p a e -> p (a e)"),
                                             op0=ALU.mult, op1=ALU.add).then_inc(result_ready, 1)

            spans(dve, body)

        @block.tensor
        def _(pe):
            def turn_tile(m, i):
                pe.wait_ge(normed_ready, m + 1)
                at_least(pe, lo_ready, m - 1)
                for kt in range(KT):
                    ins = pe.transpose(turn[i % 2][:, kt, :], normed[i][:, kt * P:(kt + 1) * P], N.ident[:, :])
                ins.then_inc(turned, 1)

            def turn_ternary(w):
                pe.wait_ge(tern_ready, w + 1)
                for part in range(2):
                    for j in range(4):
                        for h in range(2):
                            at = (2 * j + h) * STEP
                            ins = pe.transpose(tern_ps[w][part][:, :].bitcast(F16)[:, at:at + ROWS],
                                               tern[w][0:ROWS, 4 * part + j, h, :, :].rearrange("p c d -> p (c d)"),
                                               ident16[0:ROWS, 0:ROWS])
                    ins.then_inc(tern_turned, 1)

            pe.wait_ge(const_ready, 1)
            turn_tile(0, 0)
            turn_tile(1, 1)
            turn_ternary(0)
            turn_tile(2, 2)
            turn_tile(3, 3)
            turn_ternary(1)

            def turn_down(d):
                rows = chunk_rows(d)
                pe.wait_ge(down_ready, last_block(d) + 1)
                at_least(pe, down_out, d - 1)
                for kp in range(OCT // 2):
                    ins = pe.transpose(y_ps[d % 2][0:rows, :].bitcast(F16)[:, kp * P:(kp + 1) * P],
                                       down_rows[:, kp, d * P:d * P + rows], ident16[:, :])
                ins.then_inc(down_turned, 1)

            def body(t):
                pe.wait_ge(lo_ready, SPAN_TILES * (t + 1))
                for c in range(HCHUNKS):
                    rows = chunk_rows(c)
                    n = HCHUNKS * t + c
                    if is_first(t):
                        pe.wait_ge(m_by_dve, last_block(c) + 1)
                        pe.wait_ge(m_by_act, last_block(c) + 1)
                    for w, ps, free, done in ((0, gate_ps, silu_ready, gate_done), (1, up_ps, hid_ready, up_done)):
                        at_least(pe, free, n - 1 if c >= 1 else n)
                        for k in range(KT):
                            for part in (N.x_hi, N.x_lo):
                                ins = pe.matmul(ps[c % 2][0:rows, :], m_in[w][:, k, c * P:c * P + rows],
                                                part[:, k, bass.ds(t * SPAN, SPAN)],
                                                start=(k == 0 and part is N.x_hi), stop=(k == KT - 1 and part is N.x_lo))
                        ins.then_inc(done, 1)
                    if is_first(t):
                        for d in DOWN_TURNS.get(c, ()):
                            turn_down(d)
                    if not is_last(t) and c in (2, 4, 6, 8):
                        i = (c - 2) // 2
                        turn_tile(SPAN_TILES * (t + 1) + i, i)
                if is_first(t):
                    pe.wait_ge(down_out, HCHUNKS)
                for i in range(SPAN_TILES):
                    m = SPAN_TILES * t + i
                    at_least(pe, result_ready, m - 1)
                    for c in range(HCHUNKS):
                        rows = chunk_rows(c)
                        if i == 0:
                            pe.wait_ge(h_ready, HCHUNKS * t + c + 1)
                        for part in (h_hi, h_lo):
                            ins = pe.matmul(y_ps[i % 2][:, :], part[0:rows, c, i * P:(i + 1) * P], m_down[0:rows, c, :],
                                            start=(c == 0 and part is h_hi), stop=(c == HCHUNKS - 1 and part is h_lo))
                    ins.then_inc(y_done, 1)

            spans(pe, body)


def build(nc, x, ctx_in, pos, mask, wq, wk, wv, wo, w_gate, w_up, w_down, rope_table, out):
    N = Net()
    N.x = x.rearrange("b s e -> (b s) e")
    N.ctx = ctx_in.rearrange("b s e -> (b s) e")
    N.out = out.rearrange("b s e -> (b s) e")
    N.pos, N.mask, N.rope_table = pos, mask, rope_table
    N.wq, N.wk, N.wv, N.wo = wq, wk, wv, wo
    N.w_gate, N.w_up, N.w_down = w_gate, w_up, w_down
    with ExitStack() as ctx:
        N.sems = ctx

        def sb(name, shape, dt):
            return ctx.enter_context(nc.sbuf_tensor(name, shape, dt))

        N.acc = sb("acc", [P, TILES, EMB], F32)
        N.x_hi, N.x_lo = sb("x_hi", [P, KT, TOKENS], F16), sb("x_lo", [P, KT, TOKENS], F16)
        N.ident = sb("ident", [P, P], F32)
        N.eps_tile = sb("eps_tile", [P, 1], F32)
        N.stats = sb("stats", [P, TILES, 6], F32)
        N.ffn_scale, N.ffn_factor = sb("ffn_scale", [P, 3], F32), sb("ffn_factor", [P, 3], F32)
        N.c_scale, N.c_inv = sb("c_scale", [P, SPANS], F32), sb("c_inv", [P, SPANS], F32)
        N.consts_ready = ctx.enter_context(nc.semaphore("consts_ready"))
        with ExitStack() as attention:
            def sba(name, shape, dt):
                return attention.enter_context(nc.sbuf_tensor(name, shape, dt))

            N.c_hi, N.c_lo = sba("c_hi", [P, KT, TOKENS], F16), sba("c_lo", [P, KT, TOKENS], F16)
            N.cos_t, N.sin_t = sba("cos_t", [P, TOKENS], F32), sba("sin_t", [P, TOKENS], F32)
            N.pred = sba("pred", [P, BATCH, SEQ], U8)
            N.weights = Weights(nc, sba, lambda name: ctx.enter_context(nc.semaphore(name)), N)
            prepare(nc, N)
            attend(nc, N)
        feed(nc, N)


_INS = ["x", "ctx_4096", "pos_BxS2", "mask_BxSxS2_ik0", "L0_xattn_Wq", "L0_xattn_Wk", "L0_xattn_Wv", "L0_xattn_Wo",
        "L0_ffn_w_gate", "L0_ffn_w_up", "L0_ffn_w_down"]


def rope_rows():
    import numpy as np
    inv_freq = (np.float32(1.0) / np.float32(THETA) ** (np.arange(0, HEAD_DIM, 2, dtype=np.float32) / np.float32(HEAD_DIM))).astype(np.float32)
    ang = np.arange(MAX_POS, dtype=np.float32)[:, None] * inv_freq[None, :]
    return np.concatenate([np.cos(ang), np.cos(ang), np.sin(ang), -np.sin(ang)], axis=1).astype(np.float32)


def kernel(**inputs):
    import numpy as np
    import concourse.bacc as bacc
    from concourse.bass_utils import run_bass_kernel_spmd

    nc = bacc.Bacc("TRN2", target_bir_lowering=False, num_devices=1)
    arrays, args = {}, []
    for name in _INS:
        a = np.ascontiguousarray(inputs[name])
        arrays[f"in_{name}"] = a
        args.append(nc.dram_tensor(f"in_{name}", a.shape, mybir.dt.from_np(a.dtype), kind="ExternalInput").ap())
    table = rope_rows()
    arrays["rope_table"] = table
    args.append(nc.dram_tensor("rope_table", table.shape, F32, kind="ExternalInput").ap())
    args.append(nc.dram_tensor("out", (BATCH, SEQ, EMB), F32, kind="ExternalOutput").ap())
    build(nc, *args)
    r = run_bass_kernel_spmd(nc, [arrays], core_ids=[0])
    return r.results[0]["out"]
```

```python
from contextlib import ExitStack

import concourse.bass as bass
from concourse import mybir

F32 = mybir.dt.float32
F16 = mybir.dt.float16
I32 = mybir.dt.int32
U8 = mybir.dt.uint8
ALU = mybir.AluOpType
ACT = mybir.ActivationFunctionType
AX = mybir.AxisListType
REDUCE = bass.bass_isa.ReduceOp

P = 128
BATCH, SEQ, EMB = 32, 64, 512
TOKENS = BATCH * SEQ
HEADS, KV_HEADS, HEAD_DIM = 32, 8, 128
GROUP = HEADS // KV_HEADS
MAX_POS, THETA = 512, 10000.0
EPS = 1e-5
KT = EMB // P
TILES = TOKENS // P
SPAN = 512
SPANS = TOKENS // SPAN
SPAN_TILES = SPAN // P
SPAN_BATCHES = SPAN // SEQ
GCOLS = GROUP * HEAD_DIM

OCT = 8
HID8, EMB8 = 170, EMB // OCT
HIDDEN = OCT * HID8
HCHUNKS = -(-HIDDEN // P)
HLAST = HIDDEN - (HCHUNKS - 1) * P
FFN_COUNT = float(OCT * HID8 * EMB8)

MASKED = -1.0e9
XN_SCALE = 128.0
TOP = 2.0 ** 11
V_SCALE = 2.0 ** -18
QK_SCALE = 2.0 ** -19
SCORE_FLOOR = 1e-28
PROB_SCALE = 2.0 ** 14
H_SCALE = 2.0 ** -4
TINY = 1e-30
EXP_BITS = 0x7F800000

_TRIPLES = [(1, 2, 3), (1, 4, 5), (1, 7, 6), (2, 4, 6), (2, 5, 7), (3, 4, 7), (3, 6, 5)]


def octonion_signs():
    s = {(0, 0): (0, 1)}
    for i in range(1, OCT):
        s[(0, i)] = (i, 1)
        s[(i, 0)] = (i, 1)
        s[(i, i)] = (0, -1)
    for a, b, c in _TRIPLES:
        for x, y, z in ((a, b, c), (b, c, a), (c, a, b)):
            s[(x, y)] = (z, 1)
            s[(y, x)] = (z, -1)
    sign = [[0] * OCT for _ in range(OCT)]
    for (j, i), (k, v) in s.items():
        assert j == i ^ k
        sign[i][k] = v
    return sign


SIGN = octonion_signs()


def at_least(eng, sem, value):
    if isinstance(value, int) and value <= 0:
        return
    eng.wait_ge(sem, value)


class Chain:

    def __init__(self, eng, sem):
        self.eng, self.sem, self.base, self.n = eng, sem, 0, 0

    def step(self, ins):
        ins.then_inc(self.sem, 1)
        self.n += 1
        self.eng.wait_ge(self.sem, self.base + self.n)


class Net:
    pass


class Weights:

    STEPS = 10

    def __init__(self, nc, sb, sem, N):
        self.N = N
        self.wq_dram = N.wq.rearrange("(k p) n -> p k n", p=P)
        self.wk_dram = N.wk.rearrange("(k p) n -> p k n", p=P)
        self.wv_dram = N.wv.rearrange("(k p) n -> p k n", p=P)
        self.wo_dram = N.wo.rearrange("(h p) n -> p h n", p=P)
        self.w_raw = sb("w_raw", [P, KT, GCOLS], F32)
        self.wk_raw = sb("wk_raw", [P, KT, HEAD_DIM], F32)
        self.wv_raw = sb("wv_raw", [P, KT, HEAD_DIM], F32)
        self.wq_hi, self.wq_lo = sb("wq_hi", [P, KT, GCOLS], F16), sb("wq_lo", [P, KT, GCOLS], F16)
        self.wk_hi, self.wk_lo = sb("wk_hi", [P, KT, HEAD_DIM], F16), sb("wk_lo", [P, KT, HEAD_DIM], F16)
        self.wv_hi, self.wv_lo = sb("wv_hi", [P, KT, HEAD_DIM], F16), sb("wv_lo", [P, KT, HEAD_DIM], F16)
        self.wo_hi, self.wo_lo = sb("wo_hi", [P, 2, GROUP, EMB], F16), sb("wo_lo", [P, 2, GROUP, EMB], F16)
        self.wmax, self.wmax_all = sb("wmax", [P, 4], F32), sb("wmax_all", [P, 4], F32)
        self.wtmp = sb("wtmp", [P, 4], F32)
        self.w_scale, self.w_inv = sb("w_scale", [P, 4], F32), sb("w_inv", [P, 4], F32)
        self.score_next = sb("score_next", [P, 2, SPANS], F32)
        self.score_now = sb("score_now", [P, 2, SPANS], F32)
        self.score_scale, self.masked_raw = self.score_now[:, 0, :], self.score_now[:, 1, :]
        self.inv_y = sb("inv_y", [P, 2, SPANS], F32)
        self.raw_in, self.kv_in = sem("raw_in"), sem("kv_in")
        self.omax_ready, self.omax_reduced, self.oscale_ready = sem("omax_ready"), sem("omax_reduced"), sem("oscale_ready")
        self.qmax_ready, self.qmax_reduced, self.qscale_ready = sem("qmax_ready"), sem("qmax_reduced"), sem("qscale_ready")
        self.wo_hi_ready, self.wo_ready = sem("wo_hi_ready"), sem("wo_ready")
        self.wk_hi_ready, self.wk_ready = sem("wk_hi_ready"), sem("wk_ready")
        self.wv_hi_ready, self.wv_ready = sem("wv_hi_ready"), sem("wv_ready")
        self.wq_hi_ready, self.wq_ready = sem("wq_hi_ready"), sem("wq_ready")

    def load_o(self, sp, g):
        at_least(sp, self.wq_ready, 2 * g)
        sp.dma_start(self.w_raw[:, :, :], self.wo_dram[:, bass.ds(g * GROUP, GROUP), :]).then_inc(self.raw_in, 16)

    def load_kv(self, sp, g):
        at_least(sp, self.wk_ready, g)
        at_least(sp, self.wv_ready, g)
        sp.dma_start(self.wk_raw[:, :, :], self.wk_dram[:, :, bass.ds(g * HEAD_DIM, HEAD_DIM)]).then_inc(self.kv_in, 16)
        sp.dma_start(self.wv_raw[:, :, :], self.wv_dram[:, :, bass.ds(g * HEAD_DIM, HEAD_DIM)]).then_inc(self.kv_in, 16)

    def load_q(self, sp, g):
        sp.wait_ge(self.wo_ready, g + 1)
        sp.dma_start(self.w_raw[:, :, :], self.wq_dram[:, :, bass.ds(g * GCOLS, GCOLS)]).then_inc(self.raw_in, 16)

    def load(self, sp, g):
        self.load_o(sp, g)
        self.load_kv(sp, g)
        self.load_q(sp, g)

    def reduce_o(self, pool):
        pool.partition_all_reduce(self.wmax_all[:, 3:4], self.wmax[:, 3:4], P, REDUCE.max).then_inc(self.omax_reduced, 1)

    def reduce_qkv(self, pool):
        pool.partition_all_reduce(self.wmax_all[:, 0:3], self.wmax[:, 0:3], P, REDUCE.max).then_inc(self.qmax_reduced, 1)

    def high(self, act, out, raw, col, ready):
        act.activation(out, raw, ACT.Copy, scale=self.w_scale[:, col:col + 1]).then_inc(ready, 1)

    def o_high(self, act, g):
        act.wait_ge(self.oscale_ready, g + 1)
        self.high(act, self.wo_hi[:, g & 1, :, :], self.w_raw[:, :, :], 3, self.wo_hi_ready)

    def k_high(self, act, g):
        act.wait_ge(self.qscale_ready, g + 1)
        self.high(act, self.wk_hi[:, :, :], self.wk_raw[:, :, :], 1, self.wk_hi_ready)

    def v_high(self, act, g):
        self.high(act, self.wv_hi[:, :, :], self.wv_raw[:, :, :], 2, self.wv_hi_ready)

    def q_high(self, act, g, hp):
        cols = slice(hp * 256, hp * 256 + 256)
        self.high(act, self.wq_hi[:, :, cols], self.w_raw[:, :, cols], 0, self.wq_hi_ready)

    def max_o(self, dve, g):
        dve.wait_ge(self.raw_in, 32 * g + 16)
        dve.tensor_reduce(self.wmax[:, 3:4], self.w_raw[:, :, :], AX.XY, ALU.max,
                          apply_absolute_value=True).then_inc(self.omax_ready, 1)

    def scale_o(self, dve, chain, g):
        dve.wait_ge(self.omax_reduced, g + 1)
        pow2_scale(dve, chain, self.wmax_all[:, 3:4], self.wtmp[:, 3:4], self.w_scale[:, 3:4], self.w_inv[:, 3:4],
                   self.oscale_ready)

    def max_kv(self, dve, g):
        dve.wait_ge(self.kv_in, 32 * g + 32)
        for col, raw in ((1, self.wk_raw), (2, self.wv_raw)):
            dve.tensor_reduce(self.wmax[:, col:col + 1], raw[:, :, :], AX.XY, ALU.max, apply_absolute_value=True)

    def max_q(self, dve, g):
        dve.wait_ge(self.raw_in, 32 * g + 32)
        dve.tensor_reduce(self.wmax[:, 0:1], self.w_raw[:, :, :], AX.XY, ALU.max,
                          apply_absolute_value=True).then_inc(self.qmax_ready, 1)

    def scale_qkv(self, dve, chain, g):
        dve.wait_ge(self.qmax_reduced, g + 1)
        pow2_scale(dve, chain, self.wmax_all[:, 0:3], self.wtmp[:, 0:3], self.w_scale[:, 0:3], self.w_inv[:, 0:3],
                   self.qscale_ready)
        dve.wait_ge(self.qscale_ready, g + 1)
        dve.tensor_scalar(self.wtmp[:, 0:1], self.w_inv[:, 0:1], self.w_inv[:, 1:2],
                          1.0 / (QK_SCALE * QK_SCALE * XN_SCALE * float(HEAD_DIM) ** 0.5), ALU.mult, ALU.mult)
        chain.step(dve.tensor_scalar(self.wtmp[:, 1:2], self.w_inv[:, 2:3], self.w_inv[:, 3:4], 1.0 / V_SCALE,
                                     ALU.mult, ALU.mult))
        dve.tensor_scalar(self.inv_y[:, g & 1, :], self.N.c_inv[:, :], self.wtmp[:, 1:2], None, ALU.mult)
        chain.step(dve.tensor_scalar(self.score_next[:, 0, :], self.N.c_inv[:, :], self.wtmp[:, 0:1],
                                     SCORE_FLOOR, ALU.mult, ALU.max))
        chain.step(dve.reciprocal(self.score_next[:, 1, :], self.score_next[:, 0, :]))
        chain.step(dve.tensor_scalar(self.score_next[:, 1, :], self.score_next[:, 1, :], MASKED, None, ALU.mult))

    def low(self, dve, out, raw, hi, col, ready):
        dve.scalar_tensor_tensor(out=out, in0=raw, scalar=self.w_scale[:, col:col + 1], in1=hi,
                                 op0=ALU.mult, op1=ALU.subtract).then_inc(ready, 1)

    def o_low(self, dve, g):
        dve.wait_ge(self.wo_hi_ready, g + 1)
        self.low(dve, self.wo_lo[:, g & 1, :, :], self.w_raw[:, :, :], self.wo_hi[:, g & 1, :, :], 3, self.wo_ready)

    def k_low(self, dve, g):
        dve.wait_ge(self.wk_hi_ready, g + 1)
        self.low(dve, self.wk_lo[:, :, :], self.wk_raw[:, :, :], self.wk_hi[:, :, :], 1, self.wk_ready)

    def v_low(self, dve, g):
        dve.wait_ge(self.wv_hi_ready, g + 1)
        self.low(dve, self.wv_lo[:, :, :], self.wv_raw[:, :, :], self.wv_hi[:, :, :], 2, self.wv_ready)

    def q_low(self, dve, g, hp):
        dve.wait_ge(self.wq_hi_ready, 2 * g + hp + 1)
        cols = slice(hp * 256, hp * 256 + 256)
        self.low(dve, self.wq_lo[:, :, cols], self.w_raw[:, :, cols], self.wq_hi[:, :, cols], 0, self.wq_ready)


class FfnWeights:

    ROWS = HID8 // 2
    STEP = ROWS + ROWS % 2

    def __init__(self, sb, sem, N):
        self.N = N
        self.signs = sb("signs", [P, 4], F32)
        self.ident16 = sb("ident16", [P, P], F16)
        self.wsum, self.wsum_all = sb("wsum", [P, 2], F32), sb("wsum_all", [P, 2], F32)
        self.scale = sb("ffn_scale", [P, 2], F32)
        self.half, self.nhalf = sb("half", [P, 2], F32), sb("nhalf", [P, 2], F32)
        self.spow = sb("spow", [P, 3], F32)
        self.loaded, self.wsum_ready, self.wsum_reduced = sem("ffn_in"), sem("wsum_ready"), sem("wsum_reduced")
        self.tern_ready, self.tern_turned, self.tern_out = sem("tern_ready"), sem("tern_turned"), sem("tern_out")

    def place(self, W):
        self.W = W

        def flat(a):
            return a.rearrange("p a b -> p (a b)")

        self.raw = [flat(W.w_raw[:, 2 * w:2 * w + 2, :]).rearrange("p (j h d) -> p j h d", j=OCT, h=2) for w in range(2)]
        self.below = flat(W.wk_raw[:, :, :]).bitcast(F16).rearrange("p (j h d) -> p j h d", j=OCT, h=2)
        self.tern = [flat(o[:, KV_HEADS & 1, :, :]).rearrange("p (j h c d) -> p j h c d", j=OCT, h=2, c=2)
                     for o in (W.wo_hi, W.wo_lo)]
        self.tern_t = [flat(q[:, :, :])[:, 0:HIDDEN].rearrange("p (j o) -> p j o", j=OCT) for q in (W.wq_hi, W.wq_lo)]
        self.m = [c[:, :, 0:HIDDEN] for c in (self.N.c_hi, self.N.c_lo)]

    def constants(self, dve, done):
        for col in range(4):
            dve.memset(self.signs[0:64, col:col + 1], -1.0 if col & 2 else 1.0)
            dve.memset(self.signs[64:P, col:col + 1], -1.0 if col & 1 else 1.0)
        dve.memset(self.wsum[:, :], 0.0)
        dve.tensor_copy(self.ident16[:, :], self.N.ident[:, :]).then_inc(done, 1)

    def sign_pair(self, s_even, s_odd):
        col = (2 if s_even < 0 else 0) + (1 if s_odd < 0 else 0)
        return self.signs[:, col:col + 1]

    def load(self, sp):
        sp.wait_ge(self.W.wq_ready, 2 * KV_HEADS)
        for w, dram in enumerate((self.N.w_gate, self.N.w_up)):
            sp.dma_start(self.raw[w][0:self.ROWS, :, :, :],
                         dram.rearrange("j (h p) d -> p j h d", p=self.ROWS)).then_inc(self.loaded, 16)

    def reduce(self, pool):
        pool.wait_ge(self.wsum_ready, 1)
        pool.partition_all_reduce(self.wsum_all[:, :], self.wsum[:, :], P, REDUCE.add).then_inc(self.wsum_reduced, 1)

    def sums(self, dve):
        dve.wait_ge(self.loaded, 32)
        for w in range(2):
            ins = dve.tensor_reduce(self.wsum[0:self.ROWS, w:w + 1], self.raw[w][0:self.ROWS, :, :, :], AX.XYZ, ALU.add,
                                    apply_absolute_value=True)
        ins.then_inc(self.wsum_ready, 1)

    def scales(self, dve, chain):
        dve.wait_ge(self.wsum_reduced, 1)
        chain.step(dve.tensor_scalar(self.scale[:, :], self.wsum_all[:, :], 1.0 / FFN_COUNT, None, ALU.mult))
        dve.tensor_scalar(self.half[:, :], self.scale[:, :], 0.5, None, ALU.mult)
        chain.step(dve.tensor_scalar(self.nhalf[:, :], self.scale[:, :], -0.5, None, ALU.mult))
        spow, factor = self.spow, self.N.ffn_factor
        chain.step(dve.tensor_scalar(spow[:, 0:1], self.scale[:, 0:1], TINY, None, ALU.max))
        chain.step(dve.tensor_scalar(spow[:, 1:2].bitcast(I32), spow[:, 0:1].bitcast(I32), EXP_BITS, None, ALU.bitwise_and))
        chain.step(dve.reciprocal(spow[:, 2:3], spow[:, 1:2]))
        chain.step(dve.tensor_scalar(factor[:, 0:1], self.scale[:, 0:1], 1.0 / XN_SCALE, None, ALU.mult))
        chain.step(dve.tensor_scalar(factor[:, 1:2], spow[:, 2:3], H_SCALE / XN_SCALE, None, ALU.mult))

    def ternary(self, dve, chain, w):
        r = slice(0, self.ROWS)
        chain.step(dve.tensor_scalar(self.below[r, :, :, :], self.raw[w][r, :, :, :], self.nhalf[r, w:w + 1], None, ALU.is_lt))
        chain.step(dve.scalar_tensor_tensor(out=self.tern[w][r, :, :, 0, :], in0=self.raw[w][r, :, :, :],
                                            scalar=self.half[r, w:w + 1], in1=self.below[r, :, :, :],
                                            op0=ALU.is_gt, op1=ALU.subtract))
        pairs = self.tern[w][r, :, :, :, :].rearrange("p (a e) h c d -> p e a h c d", e=2)
        dve.tensor_copy(pairs[:, 0, :, :, 1, :], pairs[:, 1, :, :, 0, :])
        dve.tensor_copy(pairs[:, 1, :, :, 1, :], pairs[:, 0, :, :, 0, :]).then_inc(self.tern_ready, 1)

    def turn(self, pe, w, part, bank):
        pe.wait_ge(self.tern_ready, w + 1)
        for j in range(4):
            for h in range(2):
                at = (2 * j + h) * self.STEP
                ins = pe.transpose(bank[:, :].bitcast(F16)[:, at:at + self.ROWS],
                                   self.tern[w][0:self.ROWS, 4 * part + j, h, :, :].rearrange("p c d -> p (c d)"),
                                   self.ident16[0:self.ROWS, 0:self.ROWS])
        ins.then_inc(self.tern_turned, 1)

    def out(self, act, w, part, bank):
        act.wait_ge(self.tern_turned, 2 * w + part + 1)
        act.activation(self.tern_t[w][:, 4 * part:4 * part + 4, :].rearrange("p j (h o) -> p (j h) o", h=2),
                       bank[:, :].bitcast(F16)[:, 0:8 * self.STEP].rearrange("p (a o) -> p a o", a=8)[:, :, 0:self.ROWS],
                       ACT.Copy).then_inc(self.tern_out, 1)

    def expand(self, w, kt, k):
        return (self.m[w][:, kt, k * HID8:(k + 1) * HID8], self.tern_t[w][:, (2 * kt) ^ k, :],
                self.sign_pair(SIGN[2 * kt][k], SIGN[2 * kt + 1][k]))


def prepare(nc, N):
    with ExitStack() as ctx:
        def sb(name, shape, dt):
            return ctx.enter_context(nc.sbuf_tensor(name, shape, dt))

        def sem(name):
            return N.sems.enter_context(nc.semaphore(name))

        ctx_both = sb("ctx_both", [P, 2, SPAN_TILES, EMB], F32)
        ctx_raw = [ctx_both[:, s, :, :] for s in range(2)]
        normed = [sb(f"normed{j}", [P, EMB], F32) for j in range(2)]
        stats = sb("stats1", [P, SPAN_TILES, 6], F32)
        mean_var = sb("mean_var", [P, SPAN_TILES, 2], F32)
        std = sb("std", [P, SPAN_TILES], F32)
        rstd = sb("rstd", [P, SPAN_TILES], F32)
        cmax = sb("cmax", [P, 1], F32)
        cmax_all = sb("cmax_all", [P, 1], F32)
        cpow = sb("cpow", [P, 1], F32)
        pos = sb("pos", [P, TILES], I32)
        pos_wrap = sb("pos_wrap", [P, TILES], I32)
        rope_rows = [sb(f"rope_rows{s}", [P, 2 * HEAD_DIM], F32) for s in range(4)]
        mask_raw = sb("mask_raw", [P, BATCH, SEQ], I32)
        turn = [ctx.enter_context(nc.psum_tensor(f"turn{i}", [P, KT, P], F32)) for i in range(4)]
        rope_ps = [ctx.enter_context(nc.psum_tensor(f"rope_ps{i}", [P, 2, P], F32)) for i in range(2)]

        W = N.weights
        ident_zero, ident_in = sem("ident_zero"), sem("ident_in")
        pos_in, mask_in = sem("pos_in"), sem("mask_in")
        ctx_in = [sem(f"ctx_in{s}") for s in range(2)]
        x_in = [sem(f"x_in{s}") for s in range(2)]
        dve_step = sem("p_dve_step")
        pos_ready, rows_in, rows_turned, rows_out = sem("pos_ready"), [sem(f"rows_in{s}") for s in range(4)], sem("rows_turned"), sem("rows_out")
        pred_ready = sem("pred_ready")
        cmax_ready, cmax_reduced, cscale_ready = sem("cmax_ready"), sem("cmax_reduced"), sem("cscale_ready")
        var_ready, std_ready, normed_ready = sem("var_ready"), sem("std_ready"), sem("normed_ready")
        turned, hi_ready, lo_ready = sem("turned"), sem("p_hi_ready"), sem("p_lo_ready")

        block = ctx.enter_context(nc.Block())

        @block.sync
        def _(sp):
            sp.dma_start(pos[:, :], N.pos.rearrange("b s -> (b s)").rearrange("(i p) -> p i", p=P),
                         allow_slow_non_contiguous=True).then_inc(pos_in, 16)

            def load_tokens(t):
                rows = slice(t * SPAN, (t + 1) * SPAN)
                sp.dma_start(ctx_raw[t % 2][:, :, :], N.ctx[rows, :].rearrange("(j p) e -> p j e", p=P)).then_inc(ctx_in[t % 2], 16)
                sp.dma_start(N.acc[:, t * SPAN_TILES:(t + 1) * SPAN_TILES, :],
                             N.x[rows, :].rearrange("(j p) e -> p j e", p=P)).then_inc(x_in[t % 2], 16)

            load_tokens(0)
            W.load_o(sp, 0)
            load_tokens(1)
            W.load_kv(sp, 0)
            sp.wait_ge(lo_ready, 8)
            load_tokens(2)
            W.load_q(sp, 0)
            sp.wait_ge(lo_ready, 16)
            load_tokens(3)
            for half_rows in range(2):
                sp.dma_start(mask_raw[64 * half_rows:64 * half_rows + 64, :, :], N.mask.rearrange("b q k -> q b k")).then_inc(mask_in, 16)

        @block.gpsimd
        def _(pool):
            pool.memset(N.ident[:, :], 0.0).then_inc(ident_zero, 1)
            pool.wait_ge(ident_zero, 1)
            pool.affine_select(out=N.ident[:, :], in_=N.ident[:, :], compare_op=ALU.not_equal, fill=1.0,
                               base=0, pattern=[[-1, P]], channel_multiplier=1).then_inc(ident_in, 1)
            pool.wait_ge(pos_ready, 1)
            for i in range(TILES):
                if i >= 4:
                    pool.wait_ge(rows_turned, i - 3)
                pool.indirect_dma_start(rope_rows[i % 4][:, :], None, N.rope_table,
                                        bass.IndirectOffsetOnAxis(pos[:, i:i + 1], 0)).then_inc(rows_in[i % 4], 16)
                if i == 7:
                    pool.wait_ge(W.omax_ready, 1)
                    W.reduce_o(pool)
                if i % SPAN_TILES == SPAN_TILES - 1:
                    pool.wait_ge(cmax_ready, i // SPAN_TILES + 1)
                    pool.partition_all_reduce(cmax_all[:, :], cmax[:, :], P, REDUCE.max).then_inc(cmax_reduced, 1)
            pool.wait_ge(W.qmax_ready, 1)
            W.reduce_qkv(pool)

        @block.scalar
        def _(act):
            def deviation(t):
                act.wait_ge(var_ready, t + 1)
                act.activation(std[:, :], mean_var[:, :, 1], ACT.Sqrt, scale=XN_SCALE ** -2,
                               bias=N.eps_tile[:, 0:1]).then_inc(std_ready, 1)

            def high(m, out, scale):
                act.wait_ge(turned, m + 1)
                act.activation(out, turn[m % 4][:, :, :], ACT.Copy, scale=scale).then_inc(hi_ready, 1)

            act.wait_ge(N.consts_ready, 1)
            for t in range(SPANS):
                deviation(t)
                act.wait_ge(cscale_ready, t + 1)
                for j in range(SPAN_TILES):
                    tile = SPAN_TILES * t + j
                    high(8 * t + j, N.c_hi[:, :, tile * P:(tile + 1) * P], N.c_scale[:, t:t + 1])
                for j in range(SPAN_TILES):
                    tile = SPAN_TILES * t + j
                    high(8 * t + 4 + j, N.x_hi[:, :, tile * P:(tile + 1) * P], 1.0)
                for i in range(SPAN_TILES * t, SPAN_TILES * (t + 1)):
                    act.wait_ge(rows_turned, i + 1)
                    act.activation(N.cos_t[:, i * P:(i + 1) * P], rope_ps[i % 2][:, 0, :], ACT.Copy)
                    act.activation(N.sin_t[:, i * P:(i + 1) * P], rope_ps[i % 2][:, 1, :], ACT.Copy).then_inc(rows_out, 1)
                if t == 1:
                    W.o_high(act, 0)
            W.k_high(act, 0)
            W.v_high(act, 0)
            W.q_high(act, 0, 0)
            W.q_high(act, 0, 1)

        @block.vector
        def _(dve):
            chain = Chain(dve, dve_step)
            dve.memset(N.eps_tile[:, :], EPS / XN_SCALE ** 2).then_inc(N.consts_ready, 1)
            dve.wait_ge(ident_in, 1)
            N.ffn.constants(dve, N.consts_ready)
            dve.wait_ge(pos_in, 16)
            chain.step(dve.tensor_scalar(pos_wrap[:, :], pos[:, :], 0.0, float(MAX_POS), ALU.is_lt, ALU.mult))
            chain.step(dve.tensor_tensor(pos_wrap[:, :], pos_wrap[:, :], pos[:, :], ALU.add))
            dve.tensor_scalar(pos[:, :], pos_wrap[:, :], 0.0, float(MAX_POS - 1), ALU.max, ALU.min).then_inc(pos_ready, 1)

            def low_part(m, out, hi, scale):
                dve.wait_ge(hi_ready, m + 1)
                dve.scalar_tensor_tensor(out=out, in0=turn[m % 4][:, :, :], scalar=scale, in1=hi,
                                         op0=ALU.mult, op1=ALU.subtract).then_inc(lo_ready, 1)

            for t in range(SPANS):
                s = t % 2
                dve.wait_ge(ctx_in[s], 16 * (t // 2 + 1))
                if t:
                    dve.wait_ge(cmax_reduced, t)
                dve.tensor_reduce(cmax[:, :], ctx_raw[s][:, :, :], AX.XY, ALU.max,
                                  apply_absolute_value=True).then_inc(cmax_ready, 1)
                dve.wait_ge(x_in[s], 16 * (t // 2 + 1))
                for j in range(SPAN_TILES):
                    ins = dve.bn_stats(stats[:, j, :], N.acc[:, SPAN_TILES * t + j, :])
                chain.step(ins)
                if t:
                    dve.wait_ge(std_ready, t)
                for j in range(SPAN_TILES):
                    ins = dve.bn_aggr(mean_var[:, j, :], stats[:, j, :])
                ins.then_inc(var_ready, 1)
                if t == 2:
                    W.o_low(dve, 0)
                if t == 3:
                    W.max_kv(dve, 0)
                    W.max_q(dve, 0)
                dve.wait_ge(cmax_reduced, t + 1)
                pow2_scale(dve, chain, cmax_all[:, :], cpow[:, :], N.c_scale[:, t:t + 1], N.c_inv[:, t:t + 1], cscale_ready)
                dve.wait_ge(std_ready, t + 1)
                chain.step(dve.reciprocal(rstd[:, :], std[:, :]))
                for j in range(SPAN_TILES):
                    tile = SPAN_TILES * t + j
                    m = 8 * t + 4 + j
                    k = 8 * t + 4 + j - 2 if j >= 2 else 8 * (t - 1) + 4 + j + 2
                    if k > 0:
                        dve.wait_ge(turned, k + 1)
                    dve.tensor_scalar(normed[j % 2][:, :], N.acc[:, tile, :], mean_var[:, j, 0:1], rstd[:, j:j + 1],
                                      ALU.subtract, ALU.mult).then_inc(normed_ready, 1)
                    if j == 1:
                        for jj in range(SPAN_TILES):
                            ct = SPAN_TILES * t + jj
                            low_part(8 * t + jj, N.c_lo[:, :, ct * P:(ct + 1) * P], N.c_hi[:, :, ct * P:(ct + 1) * P],
                                     N.c_scale[:, t:t + 1])
                for j in range(SPAN_TILES):
                    tile = SPAN_TILES * t + j
                    low_part(8 * t + 4 + j, N.x_lo[:, :, tile * P:(tile + 1) * P], N.x_hi[:, :, tile * P:(tile + 1) * P], 1.0)
                if t == 0:
                    W.max_o(dve, 0)
                if t == 1:
                    W.scale_o(dve, chain, 0)
            dve.wait_ge(mask_in, 32)
            dve.tensor_scalar(N.pred[:, :, :], mask_raw[:, :, :], 0.0, None, ALU.is_equal).then_inc(pred_ready, 1)
            W.scale_qkv(dve, chain, 0)
            W.k_low(dve, 0)
            W.v_low(dve, 0)
            W.q_low(dve, 0, 0)
            W.q_low(dve, 0, 1)

        @block.tensor
        def _(pe):
            pe.wait_ge(ident_in, 1)

            def turn_tile(m, src):
                if m >= 4:
                    pe.wait_ge(lo_ready, m - 3)
                for kt in range(KT):
                    ins = pe.transpose(turn[m % 4][:, kt, :], src[:, kt * P:(kt + 1) * P], N.ident[:, :])
                ins.then_inc(turned, 1)

            for t in range(SPANS):
                pe.wait_ge(ctx_in[t % 2], 16 * (t // 2 + 1))
                for j in range(SPAN_TILES):
                    turn_tile(8 * t + j, ctx_raw[t % 2][:, j, :])
                for j in range(SPAN_TILES):
                    pe.wait_ge(normed_ready, SPAN_TILES * t + j + 1)
                    turn_tile(8 * t + 4 + j, normed[j % 2])
                for i in range(SPAN_TILES * t, SPAN_TILES * (t + 1)):
                    pe.wait_ge(rows_in[i % 4], 16 * (i // 4 + 1))
                    if i >= 2:
                        pe.wait_ge(rows_out, i - 1)
                    for c in range(2):
                        ins = pe.transpose(rope_ps[i % 2][:, c, :], rope_rows[i % 4][:, c * P:(c + 1) * P], N.ident[:, :])
                    ins.then_inc(rows_turned, 1)


def pow2_scale(dve, chain, amax, tmp, scale, inverse, ready):
    chain.step(dve.tensor_scalar(tmp, amax, TINY, None, ALU.max))
    chain.step(dve.tensor_scalar(amax.bitcast(I32), tmp.bitcast(I32), EXP_BITS, None, ALU.bitwise_and))
    chain.step(dve.tensor_scalar(inverse, amax, 1.0 / TOP, None, ALU.mult))
    ins = dve.reciprocal(scale, inverse)
    if ready is None:
        chain.step(ins)
    else:
        ins.then_inc(ready, 1)


def attend(nc, N):
    with ExitStack() as ctx:
        def sb(name, shape, dt):
            return ctx.enter_context(nc.sbuf_tensor(name, shape, dt))

        def sem(name):
            return N.sems.enter_context(nc.semaphore(name))

        W, F = N.weights, N.ffn
        k_hi = [sb(f"k_hi{i}", [P, SPAN], F16) for i in range(2)]
        k_lo = [sb(f"k_lo{i}", [P, SPAN], F16) for i in range(2)]
        v_hi = [sb(f"v_hi{i}", [P, SPAN_TILES, HEAD_DIM], F16) for i in range(2)]
        v_lo = [sb(f"v_lo{i}", [P, SPAN_TILES, HEAD_DIM], F16) for i in range(2)]
        q_hi = [sb(f"q_hi{i}", [P, SPAN_BATCHES, 2, SEQ], F16) for i in range(2)]
        q_lo = [sb(f"q_lo{i}", [P, SPAN_BATCHES, 2, SEQ], F16) for i in range(2)]
        by_cos = [sb(f"by_cos{j}", [P, SPAN], F32) for j in range(2)]
        by_sin = [sb(f"by_sin{j}", [P, SPAN], F32) for j in range(2)]
        probs = [sb(f"probs{i}", [P, SPAN_BATCHES, SEQ], F32) for i in range(2)]
        pt_hi = [sb(f"pt_hi{i}", [P, SPAN_TILES, P], F16) for i in range(2)]
        pt_lo = [sb(f"pt_lo{i}", [P, SPAN_TILES, P], F16) for i in range(2)]
        raw_max = sb("raw_max", [P, SPAN_BATCHES], F32)
        neg_max = [sb(f"neg_max{i}", [P, SPAN_BATCHES], F32) for i in range(2)]
        row_sum = [sb(f"row_sum{i}", [P, SPAN_BATCHES], F32) for i in range(2)]
        row_inv = [sb(f"row_inv{i}", [P, SPAN_BATCHES], F32) for i in range(2)]
        o_hi = [sb(f"o_hi{i}", [P, GROUP, SPAN], F16) for i in range(2)]
        o_lo = [sb(f"o_lo{i}", [P, GROUP, SPAN], F16) for i in range(2)]

        def bank(name):
            return ctx.enter_context(nc.psum_tensor(name, [P, SPAN], F32))

        q_ps = [bank("q_ps0"), bank("q_ps1")]
        kv_ps = bank("kv_ps")
        s_ps = bank("s_ps")
        pair_ps = [bank("pair_ps0"), bank("pair_ps1")]
        y_ps = [bank("y_ps0"), bank("y_ps1")]

        q_done, q_free = [sem("q_done0"), sem("q_done1")], [sem("q_free0"), sem("q_free1")]
        q_summed, q_hi_ready, q_roped = sem("q_summed"), sem("q_hi_ready"), sem("q_roped")
        k_done, k_free, k_roped = sem("k_done"), sem("k_free"), sem("k_roped")
        k_summed, k_hi_ready = sem("k_summed"), sem("k_hi_ready")
        v_done, v_hi_ready, v_ready = sem("v_done"), sem("v_hi_ready"), sem("v_ready")
        scores_scaled = sem("scores_scaled")
        s_done, filled, raw_max_ready, max_ready, exp_done, inv_ready, p_ready = (
            sem("s_done"), sem("filled"), sem("raw_max_ready"), sem("max_ready"), sem("exp_done"), sem("inv_ready"), sem("p_ready"))
        t_done, pt_hi_ready, pt_ready = sem("t_done"), sem("pt_hi_ready"), sem("pt_ready")
        pv_done, o_hi_ready, o_ready = sem("pv_done"), sem("o_hi_ready"), sem("o_ready")
        y_done, y_added = sem("y_done"), sem("y_added")
        dve_step = sem("a_dve_step")
        mean_var0 = sb("mean_var0", [P, SPAN_TILES, 2], F32)
        std0, rstd0 = sb("std0", [P, SPAN_TILES], F32), sb("rstd0", [P, SPAN_TILES], F32)
        var0_ready, std0_ready, normed0_ready = sem("var0_ready"), sem("std0_ready"), sem("normed0_ready")
        turned0, hi0_ready, lo0_ready = sem("turned0"), sem("hi0_ready"), sem("lo0_ready")
        STEPS = W.STEPS

        block = ctx.enter_context(nc.Block())
        SLOTS = [(t, u) for t in range(SPANS) for u in range(2)]

        def groups(eng, body):
            body(0)
            with eng.Fori(1, KV_HEADS - 1) as g:
                body(g)
            body(KV_HEADS - 1)

        def is_last(g):
            return isinstance(g, int) and g == KV_HEADS - 1

        def o_view(buf, u, e):
            return buf[:, 2 * u:2 * u + 2, :].rearrange("p h (b e q) -> p e b h q", e=2, q=SEQ)[:, e, :, :, :]

        def o_psum(e):
            return pair_ps[1 - e][:, :].rearrange("p (b h q) -> p b h q", b=4, h=2)

        def turn_bank(i):
            return (q_ps[0], q_ps[1], kv_ps, q_ps[0])[i]

        def norm_bank(i):
            return (q_ps[1], kv_ps)[i % 2]

        normed0 = (by_cos[0], by_cos[1], by_sin[0], by_sin[1])

        @block.sync
        def _(sp):
            with sp.Fori(1, KV_HEADS) as g:
                W.load(sp, g)
            F.load(sp)

        @block.gpsimd
        def _(pool):
            def sum_q(n, j):
                pool.wait_ge(q_free[j], n + 1)
                pool.tensor_tensor(by_cos[j][:, :], by_cos[j][:, :], by_sin[j][:, :], ALU.add).then_inc(q_summed, 1)

            def low_q(n, par, j):
                if j == 0:
                    at_least(pool, s_done, n - 1)
                pool.wait_ge(q_hi_ready, 2 * n + j + 1)
                pool.tensor_tensor(q_lo[par][:, :, j, :], by_cos[j][:, :].rearrange("p (b q) -> p b q", q=SEQ),
                                   q_hi[par][:, :, j, :], ALU.subtract).then_inc(q_roped, 1)

            def rotate_q(n, par, maxima=None):
                if maxima is not None:
                    pool.wait_ge(W.qmax_ready, maxima)
                sum_q(n, 0)
                if maxima is not None:
                    W.reduce_qkv(pool)
                sum_q(n, 1)
                for j in range(2):
                    low_q(n, par, j)

            def sum_k(tau):
                pool.wait_ge(k_free, tau + 1)
                pool.tensor_tensor(by_cos[0][:, :], by_cos[0][:, :], by_sin[0][:, :], ALU.add).then_inc(k_summed, 1)

            def low_k(tau, par):
                at_least(pool, s_done, 2 * (tau - 1))
                pool.wait_ge(k_hi_ready, tau + 1)
                pool.tensor_tensor(k_lo[par][:, :], by_cos[0][:, :], k_hi[par][:, :], ALU.subtract).then_inc(k_roped, 1)

            def normalize(n, u, maxima=None, count=None):
                if maxima is not None:
                    pool.wait_ge(maxima, count)
                pool.wait_ge(inv_ready, n + 1)
                pool.tensor_tensor(probs[u][:, :, :], probs[u][:, :, :],
                                   row_inv[u][:, :].unsqueeze(2).to_broadcast([P, SPAN_BATCHES, SEQ]),
                                   ALU.mult).then_inc(p_ready, 1)

            sum_k(0)
            low_k(0, 0)
            rotate_q(0, 0)

            def body(g):
                for slot, (t, u) in enumerate(SLOTS):
                    tau = 4 * g + t
                    n = 2 * tau + u
                    more = not is_last(g) or slot < 7
                    if more:
                        rotate_q(n + 1, 1 - u, g + 2 if slot == 5 and not is_last(g) else None)
                    next_keys = u == 0 and not (is_last(g) and t == SPANS - 1)
                    if next_keys:
                        sum_k(tau + 1)
                    if is_last(g) or slot != 2:
                        normalize(n, u)
                        if is_last(g) and slot == 2:
                            F.reduce(pool)
                    else:
                        normalize(n, u, W.omax_ready, g + 2)
                        W.reduce_o(pool)
                    if next_keys:
                        low_k(tau + 1, (t + 1) % 2)

            groups(pool, body)

        @block.scalar
        def _(act):
            def turned_probs(n, u):
                act.wait_ge(t_done, n + 1)
                act.activation(pt_hi[u][:, :, :].rearrange("p a b -> p (a b)"), pair_ps[0][:, :], ACT.Copy,
                               scale=PROB_SCALE).then_inc(pt_hi_ready, 1)

            def query_hi(n, par, j):
                if j == 0:
                    at_least(act, s_done, n - 1)
                act.wait_ge(q_summed, 2 * n + j + 1)
                act.activation(q_hi[par][:, :, j, :], by_cos[j][:, :].rearrange("p (b q) -> p b q", q=SEQ),
                               ACT.Copy).then_inc(q_hi_ready, 1)

            def key_hi(tau, par):
                at_least(act, s_done, 2 * (tau - 1))
                act.wait_ge(k_summed, tau + 1)
                act.activation(k_hi[par][:, :], by_cos[0][:, :], ACT.Copy).then_inc(k_hi_ready, 1)

            def exponentials(n, u, t):
                act.wait_ge(max_ready, n + 1)
                at_least(act, t_done, n - 1)
                for b in range(SPAN_BATCHES):
                    ins = act.activation(probs[u][:, b, :], s_ps[:, b * SEQ:(b + 1) * SEQ], ACT.Exp,
                                         scale=W.score_scale[:, t:t + 1], bias=neg_max[u][:, b:b + 1],
                                         accum_out=row_sum[u][:, b:b + 1])
                ins.then_inc(exp_done, 1)

            def values(tau, par):
                act.wait_ge(v_done, tau + 1)
                at_least(act, pv_done, 4 * (tau - 1))
                act.activation(v_hi[par][:, :, :].rearrange("p a b -> p (a b)"), kv_ps[:, :], ACT.Copy,
                               scale=V_SCALE).then_inc(v_hi_ready, 1)

            def outputs_hi(n, tau, par, u):
                at_least(act, y_done, 4 * tau - 4)
                for hf in (0, 1):
                    act.wait_ge(pv_done, 2 * n + hf + 1)
                    act.activation(o_view(o_hi[par], u, hf), o_psum(hf), ACT.Copy, scale=1.0 / PROB_SCALE).then_inc(o_hi_ready, 1)

            key_hi(0, 0)
            query_hi(0, 0, 0)
            query_hi(0, 0, 1)
            values(0, 0)

            def body(g):
                first = isinstance(g, int) and g == 0
                for slot, (t, u) in enumerate(SLOTS):
                    tau = 4 * g + t
                    n = 2 * tau + u
                    prev = not (first and slot == 0)
                    more = not (is_last(g) and slot == 7)
                    if not is_last(g) and slot == 3:
                        at_least(act, y_done, 16 * g)
                        W.o_high(act, g + 1)
                    if not is_last(g) and slot in (6, 7):
                        act.wait_ge(q_done[1], n + 1)
                        W.q_high(act, g + 1, u)
                    if more:
                        query_hi(n + 1, 1 - u, 0)
                    else:
                        for i in range(4):
                            F.out(act, i // 2, i % 2, turn_bank(i))
                    if prev:
                        turned_probs(n - 1, 1 - u)
                    if more:
                        query_hi(n + 1, 1 - u, 1)
                    exponentials(n, u, t)
                    if u == 0 and not (is_last(g) and t == SPANS - 1):
                        key_hi(tau + 1, (t + 1) % 2)
                    if u == 1 and not (is_last(g) and t == SPANS - 1):
                        values(tau + 1, (t + 1) % 2)
                    if prev:
                        pt, pp = (tau, t % 2) if u else (tau - 1, (t + 1) % 2)
                        outputs_hi(n - 1, pt, pp, 1 - u)
                    if not is_last(g):
                        if slot == 5:
                            act.wait_ge(k_done, 4 * g + 4)
                            W.k_high(act, g + 1)
                        if slot == 6:
                            act.wait_ge(v_done, 4 * g + 4)
                            W.v_high(act, g + 1)

            groups(act, body)
            act.wait_ge(var0_ready, 1)
            act.activation(std0[:, :], mean_var0[:, :, 1], ACT.Sqrt, scale=XN_SCALE ** -2,
                           bias=N.eps_tile[:, 0:1]).then_inc(std0_ready, 1)
            last = 2 * SPANS * KV_HEADS - 1

            def expand(w, k):
                for kt in (2, 3):
                    out, src, sign = F.expand(w, kt, k)
                    act.activation(out, src, ACT.Copy, scale=sign)

            act.wait_ge(F.tern_out, 4)
            act.wait_ge(v_done, SPANS * KV_HEADS)
            expand(0, 0)
            turned_probs(last, 1)
            expand(1, 0)
            expand(0, 1)
            outputs_hi(last, SPANS * KV_HEADS - 1, 1, 1)
            for i in range(SPAN_TILES):
                act.wait_ge(turned0, i + 1)
                act.activation(N.x_hi[:, :, i * P:(i + 1) * P], norm_bank(i).rearrange("p (k t) -> p k t", k=KT),
                               ACT.Copy).then_inc(hi0_ready, 1)
            expand(1, 1)
            for k in range(2, OCT):
                for w in range(2):
                    expand(w, k)

        @block.vector
        def _(dve):
            chain = Chain(dve, dve_step)

            def rotate(ps, j, span, free):
                cols = slice(span * SPAN, (span + 1) * SPAN)
                dve.scalar_tensor_tensor(out=by_cos[j][:, :], in0=ps[:, :], scalar=QK_SCALE, in1=N.cos_t[:, cols],
                                         op0=ALU.mult, op1=ALU.mult)
                for a, b in ((0, 64), (64, 0)):
                    ins = dve.scalar_tensor_tensor(out=by_sin[j][b:b + 64, :], in0=ps[a:a + 64, :], scalar=QK_SCALE,
                                                   in1=N.sin_t[a:a + 64, cols], op0=ALU.mult, op1=ALU.mult)
                ins.then_inc(free, 1)

            def turned_lo(n, u):
                dve.wait_ge(pt_hi_ready, n + 1)
                dve.scalar_tensor_tensor(out=pt_lo[u][:, :, :].rearrange("p a b -> p (a b)"), in0=pair_ps[0][:, :],
                                         scalar=PROB_SCALE, in1=pt_hi[u][:, :, :].rearrange("p a b -> p (a b)"),
                                         op0=ALU.mult, op1=ALU.subtract).then_inc(pt_ready, 1)

            def values_lo(tau, par):
                dve.wait_ge(v_hi_ready, tau + 1)
                dve.scalar_tensor_tensor(out=v_lo[par][:, :, :].rearrange("p a b -> p (a b)"), in0=kv_ps[:, :],
                                         scalar=V_SCALE, in1=v_hi[par][:, :, :].rearrange("p a b -> p (a b)"),
                                         op0=ALU.mult, op1=ALU.subtract).then_inc(v_ready, 1)

            def rotate_q(n, span):
                for j in range(2):
                    dve.wait_ge(q_done[j], n + 1)
                    at_least(dve, q_roped, 2 * n + j - 1)
                    rotate(q_ps[j], j, span, q_free[j])

            def rotate_k(tau, span):
                dve.wait_ge(k_done, tau + 1)
                rotate(kv_ps, 0, span, k_free)

            def row_max(n, u, t):
                dve.wait_ge(s_done, 1)
                dve.wait_ge(s_done, n + 1)
                s3 = s_ps[:, :].rearrange("p (b k) -> p b k", b=SPAN_BATCHES)
                dve.copy_predicated(s3, N.pred[:, t * SPAN_BATCHES:(t + 1) * SPAN_BATCHES, :],
                                    W.masked_raw[:, t:t + 1].unsqueeze(2).to_broadcast([P, SPAN_BATCHES, SEQ])).then_inc(filled, 1)
                dve.wait_ge(filled, n + 1)
                dve.tensor_reduce(raw_max[:, :], s3, AX.X, ALU.max, negate=True).then_inc(raw_max_ready, 1)
                dve.wait_ge(raw_max_ready, n + 1)
                dve.tensor_scalar(neg_max[u][:, :], raw_max[:, :], W.score_scale[:, t:t + 1], None,
                                  ALU.mult).then_inc(max_ready, 1)

            def row_inverse(n, u):
                dve.wait_ge(exp_done, n + 1)
                dve.reciprocal(row_inv[u][:, :], row_sum[u][:, :]).then_inc(inv_ready, 1)

            def outputs_lo(n, par, u):
                for hf in (0, 1):
                    dve.wait_ge(o_hi_ready, 2 * n + hf + 1)
                    for h in range(2):
                        ins = dve.scalar_tensor_tensor(out=o_view(o_lo[par], u, hf)[:, :, h, :], in0=o_psum(hf)[:, :, h, :],
                                                       scalar=1.0 / PROB_SCALE, in1=o_view(o_hi[par], u, hf)[:, :, h, :],
                                                       op0=ALU.mult, op1=ALU.subtract)
                    ins.then_inc(o_ready, 1)

            def add_y(tau, g, span, i):
                m = 4 * tau + i
                dve.wait_ge(y_done, m + 1)
                at_least(dve, y_added, m - 1)
                tile = N.acc[:, span * SPAN_TILES + i, :]
                dve.scalar_tensor_tensor(out=tile, in0=y_ps[i % 2][:, :], scalar=W.inv_y[:, g & 1, span:span + 1],
                                         in1=tile, op0=ALU.mult, op1=ALU.add).then_inc(y_added, 1)

            def expand(k):
                for w in range(2):
                    for kt in (0, 1):
                        out, src, sign = F.expand(w, kt, k)
                        dve.tensor_scalar(out, src, sign, None, ALU.mult)

            def token_stats(tau, span, i):
                dve.wait_ge(y_added, 4 * tau + i + 1)
                dve.bn_stats(N.stats[:, span * SPAN_TILES + i, :], N.acc[:, span * SPAN_TILES + i, :])

            rotate_k(0, 0)
            dve.wait_ge(k_roped, 1)
            rotate_q(0, 0)
            values_lo(0, 0)

            def body(g):
                chain.base, chain.n = STEPS * g, 0
                first = isinstance(g, int) and g == 0
                dve.tensor_copy(W.score_now[:, :, :], W.score_next[:, :, :]).then_inc(scores_scaled, 1)
                dve.wait_ge(scores_scaled, g + 1)
                for slot, (t, u) in enumerate(SLOTS):
                    tau = 4 * g + t
                    n = 2 * tau + u
                    if not (is_last(g) and slot == 7):
                        if u == 1:
                            dve.wait_ge(k_roped, tau + 2)
                        rotate_q(n + 1, (slot + 1) // 2 % SPANS)
                    if not (first and slot == 0):
                        turned_lo(n - 1, 1 - u)
                    row_max(n, u, t)
                    if u == 0 and not (is_last(g) and t == SPANS - 1):
                        dve.wait_ge(q_roped, 2 * n + 3)
                        rotate_k(tau + 1, (t + 1) % SPANS)
                    if is_last(g):
                        if slot == 1:
                            F.sums(dve)
                        if slot == 3:
                            dve.wait_ge(y_done, 16 * g)
                            F.ternary(dve, chain, 0)
                        if slot == 5:
                            F.ternary(dve, chain, 1)
                        if slot == 7:
                            dve.wait_ge(F.tern_out, 4)
                            dve.wait_ge(v_done, SPANS * KV_HEADS)
                            expand(0)
                            expand(1)
                    if not is_last(g):
                        if slot == 1:
                            W.max_o(dve, g + 1)
                        if slot == 3:
                            W.o_low(dve, g + 1)
                        if slot == 5:
                            W.scale_qkv(dve, chain, g + 1)
                        if slot == 7:
                            W.q_low(dve, g + 1, 1)
                    row_inverse(n, u)
                    if slot == 6 and not is_last(g):
                        W.q_low(dve, g + 1, 0)
                    if u == 1 and not (is_last(g) and t == SPANS - 1):
                        values_lo(tau + 1, (t + 1) % 2)
                    if not (first and slot == 0):
                        outputs_lo(n - 1, t % 2 if u else (t + 1) % 2, 1 - u)
                    back = 1 if u else 2
                    if not (first and t < back):
                        yg = g - 1 if t < back else g
                        for i in ((0, 1) if u else (2, 3)):
                            add_y(tau - back, yg, (t - back) % SPANS, i)
                        if is_last(g) and t >= back:
                            for i in ((0, 1) if u else (2, 3)):
                                token_stats(tau - back, t - back, i)
                    if not is_last(g):
                        if slot == 2:
                            W.scale_o(dve, chain, g + 1)
                            W.max_kv(dve, g + 1)
                        if slot == 4:
                            W.max_q(dve, g + 1)
                        if slot == 5:
                            W.k_low(dve, g + 1)
                        if slot == 6:
                            W.v_low(dve, g + 1)
                    if is_last(g) and slot == 2:
                        F.scales(dve, chain)
                    if is_last(g) and slot == 6:
                        for i in range(SPAN_TILES):
                            ins = dve.bn_aggr(mean_var0[:, i, :], N.stats[:, i, :])
                        ins.then_inc(var0_ready, 1)
                assert is_last(g) or chain.n == STEPS

            groups(dve, body)
            g = KV_HEADS - 1
            tau = 4 * g + 3
            dve.wait_ge(var0_ready, 1)
            dve.wait_ge(std0_ready, 1)
            chain.step(dve.reciprocal(rstd0[:, :], std0[:, :]))
            dve.wait_ge(q_roped, 2 * (2 * tau + 2))
            for i in range(SPAN_TILES):
                dve.tensor_scalar(normed0[i][:, :], N.acc[:, i, :], mean_var0[:, i, 0:1], rstd0[:, i:i + 1],
                                  ALU.subtract, ALU.mult).then_inc(normed0_ready, 1)
            add_y(tau - 1, g, 2, 2)
            turned_lo(2 * tau + 1, 1)
            add_y(tau - 1, g, 2, 3)
            expand(2)
            outputs_lo(2 * tau + 1, 1, 1)
            for i in range(SPAN_TILES):
                dve.wait_ge(hi0_ready, i + 1)
                dve.tensor_tensor(N.x_lo[:, :, i * P:(i + 1) * P], norm_bank(i).rearrange("p (k t) -> p k t", k=KT),
                                  N.x_hi[:, :, i * P:(i + 1) * P], ALU.subtract).then_inc(lo0_ready, 1)
            token_stats(tau - 1, 2, 2)
            token_stats(tau - 1, 2, 3)
            for k in (3, 4, 5):
                expand(k)
            for i in range(4):
                add_y(tau, g, 3, i)
                if i < 2:
                    expand(6 + i)
                if i:
                    token_stats(tau, 3, i - 1)

        @block.tensor
        def _(pe):
            def product3(out, pairs):
                steps = [(a, b) for ah, al, bh, bl in pairs for a, b in ((ah, bh), (ah, bl), (al, bh))]
                for s, (a, b) in enumerate(steps):
                    ins = pe.matmul(out, a, b, start=(s == 0), stop=(s == len(steps) - 1))
                return ins

            def queries(n, hp, span, new, g):
                cols = slice(span * SPAN, (span + 1) * SPAN)
                if new:
                    pe.wait_ge(W.wq_ready, 2 * g + hp + 1)
                for j in range(2):
                    at_least(pe, q_free[j], n)
                    h = slice((2 * hp + j) * HEAD_DIM, (2 * hp + j + 1) * HEAD_DIM)
                    product3(q_ps[j][:, :], [(W.wq_hi[:, k, h], W.wq_lo[:, k, h], N.x_hi[:, k, cols], N.x_lo[:, k, cols])
                                             for k in range(KT)]).then_inc(q_done[j], 1)

            def keys(tau, span, new, g):
                cols = slice(span * SPAN, (span + 1) * SPAN)
                if new:
                    pe.wait_ge(W.wk_ready, g + 1)
                at_least(pe, v_ready, tau)
                product3(kv_ps[:, :], [(W.wk_hi[:, k, :], W.wk_lo[:, k, :], N.c_hi[:, k, cols], N.c_lo[:, k, cols])
                                       for k in range(KT)]).then_inc(k_done, 1)

            def values(tau, span, new, g):
                if new:
                    pe.wait_ge(W.wv_ready, g + 1)
                pe.wait_ge(k_free, tau + 1)
                for j in range(SPAN_TILES):
                    rows = slice(span * SPAN + j * P, span * SPAN + (j + 1) * P)
                    ins = product3(kv_ps[:, j * P:(j + 1) * P],
                                   [(N.c_hi[:, k, rows], N.c_lo[:, k, rows], W.wv_hi[:, k, :], W.wv_lo[:, k, :]) for k in range(KT)])
                ins.then_inc(v_done, 1)

            def turn_probs(n, u):
                pe.wait_ge(p_ready, n + 1)
                at_least(pe, o_ready, 2 * n)
                for j in range(SPAN_TILES):
                    ins = pe.transpose(pair_ps[0][:, j * P:(j + 1) * P],
                                       probs[u][:, 2 * j:2 * j + 2, :].rearrange("p b k -> p (b k)"), N.ident[:, :])
                ins.then_inc(t_done, 1)

            def scores(n, u, tau, par):
                pe.wait_ge(q_roped, 2 * n + 2)
                pe.wait_ge(k_roped, tau + 1)
                at_least(pe, exp_done, n)
                for b in range(SPAN_BATCHES):
                    rows = slice(b * SEQ, (b + 1) * SEQ)
                    ins = product3(s_ps[:, rows], [(q_hi[u][:, b, :, :].rearrange("p h q -> p (h q)"),
                                                    q_lo[u][:, b, :, :].rearrange("p h q -> p (h q)"),
                                                    k_hi[par][:, rows], k_lo[par][:, rows])])
                ins.then_inc(s_done, 1)

            def head_outputs(n, u, tau, par):
                pe.wait_ge(pt_ready, n + 1)
                pe.wait_ge(v_ready, tau + 1)
                at_least(pe, o_ready, 2 * n)
                for b in range(SPAN_BATCHES):
                    j, e = b // 2, b % 2
                    rows = slice(SEQ * e, SEQ * e + SEQ)
                    ins = product3(pair_ps[1 - e][:, j * P:(j + 1) * P], [(v_hi[par][rows, j, :], v_lo[par][rows, j, :],
                                                                           pt_hi[u][rows, j, :], pt_lo[u][rows, j, :])])
                    if j == 3:
                        ins.then_inc(pv_done, 1)

            def project(tau, par, i, g):
                m = 4 * tau + i
                if i == 0:
                    pe.wait_ge(W.wo_ready, g + 1)
                pe.wait_ge(o_ready, 4 * tau + 4)
                at_least(pe, y_added, m - 1)
                rows = slice(i * P, (i + 1) * P)
                product3(y_ps[i % 2][:, :], [(o_hi[par][:, h, rows], o_lo[par][:, h, rows],
                                              W.wo_hi[:, g & 1, h, :], W.wo_lo[:, g & 1, h, :])
                                             for h in range(GROUP)]).then_inc(y_done, 1)

            keys(0, 0, True, 0)
            queries(0, 0, 0, True, 0)
            values(0, 0, True, 0)

            def body(g):
                first = isinstance(g, int) and g == 0
                for slot, (t, u) in enumerate(SLOTS):
                    tau = 4 * g + t
                    n = 2 * tau + u
                    if not (is_last(g) and slot == 7):
                        queries(n + 1, 1 - u, (slot + 1) // 2 % SPANS, slot in (7, 0), g + 1 if slot == 7 else g)
                    else:
                        for i in range(4):
                            if i < 2:
                                pe.wait_ge(q_free[i], n + 1)
                            if i == 2:
                                pe.wait_ge(v_ready, SPANS * KV_HEADS)
                            if i == 3:
                                pe.wait_ge(F.tern_out, 1)
                            F.turn(pe, i // 2, i % 2, turn_bank(i))
                    if not (first and slot == 0):
                        turn_probs(n - 1, 1 - u)
                    scores(n, u, tau, t % 2)
                    if not (is_last(g) and t == SPANS - 1):
                        gn, new = (g + 1, True) if t == 3 else (g, False)
                        (values if u else keys)(tau + 1, (t + 1) % SPANS, new, gn)
                    if not (first and slot == 0):
                        head_outputs(n - 1, 1 - u, tau if u else tau - 1, t % 2 if u else (t + 1) % 2)
                    back = 1 if u else 2
                    if not (first and t < back):
                        for i in ((0, 1) if u else (2, 3)):
                            project(tau - back, (t - back) % 2, i, g - 1 if t < back else g)

            groups(pe, body)
            g = KV_HEADS - 1
            tau = 4 * g + 3
            project(tau - 1, 0, 2, g)
            turn_probs(2 * tau + 1, 1)
            project(tau - 1, 0, 3, g)
            head_outputs(2 * tau + 1, 1, tau, 1)
            pe.wait_ge(F.tern_out, 4)
            for i in range(SPAN_TILES):
                pe.wait_ge(normed0_ready, i + 1)
                at_least(pe, lo0_ready, i - 1)
                for kt in range(KT):
                    ins = pe.transpose(norm_bank(i)[:, kt * P:(kt + 1) * P], normed0[i][:, kt * P:(kt + 1) * P], N.ident[:, :])
                ins.then_inc(turned0, 1)
            for i in range(4):
                project(tau, 1, i, g)


def feed(nc, N):
    with ExitStack() as ctx:
        def sb(name, shape, dt):
            return ctx.enter_context(nc.sbuf_tensor(name, shape, dt))

        def sem(name):
            return N.sems.enter_context(nc.semaphore(name))

        F = N.ffn
        wd_nat = sb("wd_nat", [P, OCT // 2, HID8], F32)
        below = sb("below", [P, OCT // 2, HID8], F16)
        ternd = [sb(f"ternd{w}", [P, OCT // 2, HID8], F16) for w in range(2)]
        wsum, wsum_all = sb("wsum_d", [P, 1], F32), sb("wsum_d_all", [P, 1], F32)
        scale_d = sb("scale_d", [P, 1], F32)
        half, nhalf = sb("half_d", [P, 1], F32), sb("nhalf_d", [P, 1], F32)
        down_rows = sb("down_rows", [P, OCT // 2, HIDDEN], F16)
        m_down = sb("m_down", [P, HCHUNKS, EMB], F16)
        normed = [sb(f"normed2_{j}", [P, EMB], F32) for j in range(SPAN_TILES)]
        mean_var = sb("mean_var2", [P, TILES, 2], F32)
        std, rstd = sb("std2", [P, TILES], F32), sb("rstd2", [P, TILES], F32)
        silu = [sb(f"silu{i}", [P, SPAN], F32) for i in range(2)]
        hid = [sb(f"hid{i}", [P, SPAN], F32) for i in range(2)]
        h_hi = sb("h_hi", [P, HCHUNKS, SPAN], F16)
        h_lo = sb("h_lo", [P, HCHUNKS, SPAN], F16)
        result = [sb(f"result{i}", [P, EMB], F32) for i in range(2)]

        def bank(name, shape=(P, SPAN)):
            return ctx.enter_context(nc.psum_tensor(name, list(shape), F32))

        turn = [bank(f"turn2_{i}", (P, KT, P)) for i in range(2)]
        gate_ps = [bank(f"gate_ps{i}") for i in range(2)]
        up_ps = [bank(f"up_ps{i}") for i in range(2)]
        y_ps = [bank(f"y2_ps{i}") for i in range(2)]

        down_in, wsum_ready, wsum_reduced = sem("down_in"), sem("wsum_d_ready"), sem("wsum_d_reduced")
        down_ready, down_turned, down_out = sem("down_ready"), sem("down_turned"), sem("down_out")
        var_ready, std_ready, normed_ready = sem("var2_ready"), sem("std2_ready"), sem("normed2_ready")
        turned, hi_ready, lo_ready = sem("turned2"), sem("hi2_ready"), sem("lo2_ready")
        gate_done, up_done, silu_ready, hid_ready = sem("gate_done"), sem("up_done"), sem("silu_ready"), sem("hid_ready")
        h_hi_ready, h_ready = sem("h_hi_ready"), sem("h_ready")
        y_done, result_ready = sem("y2_done"), sem("result_ready")
        stored = [sem(f"stored{i}") for i in range(2)]
        rstd_ready, dve_step = sem("rstd_ready"), sem("f_dve_step")

        block = ctx.enter_context(nc.Block())
        DOWN_FROM = 3
        DOWN_TURNS = {5: (0, 1), 6: (2,), 7: (3, 4), 8: (5,), 9: (6, 7), 10: (8, 9, 10)}

        def chunk_rows(c):
            return P if c < HCHUNKS - 1 else HLAST

        def last_block(c):
            return (c * P + chunk_rows(c) - 1) // HID8

        def spans(eng, body):
            body(0)
            with eng.Fori(1, SPANS - 1) as t:
                body(t)
            body(SPANS - 1)

        def is_first(t):
            return isinstance(t, int) and t == 0

        def is_last(t):
            return isinstance(t, int) and t == SPANS - 1

        def token_cols(m):
            return bass.ds(m * P, P)

        @block.sync
        def _(sp):
            for e in range(2):
                sp.dma_start(wd_nat[64 * e:64 * e + 64, :, :],
                             N.w_down.rearrange("(a e) o d -> e o a d", e=2)[e]).then_inc(down_in, 16)
            with sp.Fori(0, SPANS) as t:
                for i in range(SPAN_TILES):
                    sp.wait_ge(result_ready, 4 * t + i + 1)
                    sp.dma_start(N.out[bass.ds((t * SPAN_TILES + i) * P, P), :], result[i % 2][:, :]).then_inc(stored[i % 2], 16)
            for s in stored:
                sp.wait_ge(s, 16 * TILES // 2)

        @block.gpsimd
        def _(pool):
            pool.wait_ge(wsum_ready, 1)
            pool.partition_all_reduce(wsum_all[:, :], wsum[:, :], P, REDUCE.add).then_inc(wsum_reduced, 1)
            with pool.Fori(0, SPANS) as t:
                for c in range(HCHUNKS):
                    rows = chunk_rows(c)
                    pool.wait_ge(h_hi_ready, HCHUNKS * t + c + 1)
                    pool.tensor_tensor(h_lo[0:rows, c, :], hid[c % 2][0:rows, :], h_hi[0:rows, c, :],
                                       ALU.subtract).then_inc(h_ready, 1)

        @block.scalar
        def _(act):
            act.wait_ge(var_ready, 1)
            act.activation(std[:, SPAN_TILES:TILES], mean_var[:, SPAN_TILES:TILES, 1], ACT.Sqrt, scale=XN_SCALE ** -2,
                           bias=N.eps_tile[:, 0:1]).then_inc(std_ready, 1)

            def high(m, i):
                act.wait_ge(turned, 1)
                act.wait_ge(turned, m - SPAN_TILES + 1)
                act.activation(N.x_hi[:, :, token_cols(m)], turn[i % 2][:, :, :], ACT.Copy).then_inc(hi_ready, 1)

            def body(t):
                def hidden_hi(c):
                    rows = chunk_rows(c)
                    act.wait_ge(hid_ready, HCHUNKS * t + c + 1)
                    act.activation(h_hi[0:rows, c, :], hid[c % 2][0:rows, :], ACT.Copy).then_inc(h_hi_ready, 1)

                for c in range(HCHUNKS):
                    rows = chunk_rows(c)
                    act.wait_ge(gate_done, HCHUNKS * t + c + 1)
                    act.activation(silu[c % 2][0:rows, :], gate_ps[c % 2][0:rows, :], ACT.Silu,
                                   scale=N.ffn_factor[0:rows, 0:1]).then_inc(silu_ready, 1)
                    if c >= 1:
                        hidden_hi(c - 1)
                    if is_first(t):
                        for d in DOWN_TURNS.get(c, ()):
                            act.wait_ge(down_turned, d + 1)
                            act.activation(m_down[0:chunk_rows(d), d, :],
                                           y_ps[d % 2][0:chunk_rows(d), :].bitcast(F16)[:, 0:EMB], ACT.Copy).then_inc(down_out, 1)
                    if not is_last(t) and c in (2, 4, 6, 8):
                        i = (c - 2) // 2
                        high(SPAN_TILES * (t + 1) + i, i)
                hidden_hi(HCHUNKS - 1)

            spans(act, body)

        @block.vector
        def _(dve):
            chain = Chain(dve, dve_step)
            chain.step(dve.bn_stats(N.stats[:, TILES - 1, :], N.acc[:, TILES - 1, :]))
            for i in range(SPAN_TILES, TILES):
                ins = dve.bn_aggr(mean_var[:, i, :], N.stats[:, i, :])
            ins.then_inc(var_ready, 1)
            dve.wait_ge(std_ready, 1)
            dve.reciprocal(rstd[:, SPAN_TILES:TILES], std[:, SPAN_TILES:TILES]).then_inc(rstd_ready, 1)
            dve.wait_ge(rstd_ready, 1)

            def normalize(m, i):
                at_least(dve, turned, m - SPAN_TILES - 3)
                dve.tensor_scalar(normed[i][:, :], N.acc[:, bass.ds(m, 1), :].rearrange("p a e -> p (a e)"),
                                  mean_var[:, bass.ds(m, 1), 0:1].rearrange("p a b -> p (a b)"), rstd[:, bass.ds(m, 1)],
                                  ALU.subtract, ALU.mult).then_inc(normed_ready, 1)

            def low(m, i):
                dve.wait_ge(hi_ready, m - SPAN_TILES + 1)
                dve.tensor_tensor(N.x_lo[:, :, token_cols(m)], turn[i % 2][:, :, :], N.x_hi[:, :, token_cols(m)],
                                  ALU.subtract).then_inc(lo_ready, 1)

            def scale_down():
                dve.wait_ge(wsum_reduced, 1)
                chain.step(dve.tensor_scalar(scale_d[:, :], wsum_all[:, :], 1.0 / FFN_COUNT, None, ALU.mult))
                dve.tensor_scalar(half[:, :], scale_d[:, :], 0.5, None, ALU.mult)
                chain.step(dve.tensor_scalar(nhalf[:, :], scale_d[:, :], -0.5, None, ALU.mult))
                chain.step(dve.tensor_tensor(F.spow[:, 0:1], F.spow[:, 1:2], F.scale[:, 1:2], ALU.mult))
                chain.step(dve.tensor_scalar(N.ffn_factor[:, 2:3], F.spow[:, 0:1], scale_d[:, 0:1], 1.0 / H_SCALE, ALU.mult, ALU.mult))

            def ternary_down():
                chain.step(dve.tensor_scalar(below[:, :, :], wd_nat[:, :, :], nhalf[:, 0:1], None, ALU.is_lt))
                chain.step(dve.scalar_tensor_tensor(out=ternd[0][:, :, :], in0=wd_nat[:, :, :], scalar=half[:, 0:1],
                                                    in1=below[:, :, :], op0=ALU.is_gt, op1=ALU.subtract))
                dve.tensor_copy(ternd[1][0:64, :, :], ternd[0][64:P, :, :])
                chain.step(dve.tensor_copy(ternd[1][64:P, :, :], ternd[0][0:64, :, :]))

            def down_block(i):
                for kp in range(OCT // 2):
                    ins = dve.tensor_scalar(down_rows[:, kp, i * HID8:(i + 1) * HID8], ternd[i % 2][:, (i // 2) ^ kp, :],
                                            F.sign_pair(SIGN[i][2 * kp], SIGN[i][2 * kp + 1]), None, ALU.mult)
                ins.then_inc(down_ready, 1)

            def body(t):
                for c in range(HCHUNKS):
                    rows = chunk_rows(c)
                    n = HCHUNKS * t + c
                    dve.wait_ge(silu_ready, n + 1)
                    dve.wait_ge(up_done, n + 1)
                    at_least(dve, h_ready, n - 1 if c >= 1 else n)
                    dve.scalar_tensor_tensor(out=hid[c % 2][0:rows, :], in0=silu[c % 2][0:rows, :],
                                             scalar=N.ffn_factor[0:rows, 1:2], in1=up_ps[c % 2][0:rows, :],
                                             op0=ALU.mult, op1=ALU.mult).then_inc(hid_ready, 1)
                    if is_first(t):
                        if c == 0:
                            dve.wait_ge(down_in, 32)
                            dve.tensor_reduce(wsum[:, :], wd_nat[:, :, :], AX.XY, ALU.add,
                                              apply_absolute_value=True).then_inc(wsum_ready, 1)
                        if c == 1:
                            scale_down()
                        if c == DOWN_FROM - 1:
                            ternary_down()
                        if 0 <= c - DOWN_FROM < OCT:
                            down_block(c - DOWN_FROM)
                    if not is_last(t):
                        if c in (3, 5, 7, 9):
                            i = (c - 3) // 2
                            low(SPAN_TILES * (t + 1) + i, i)
                        if c in (1, 3, 5, 7):
                            i = (c - 1) // 2
                            normalize(SPAN_TILES * (t + 1) + i, i)
                for i in range(SPAN_TILES):
                    m = SPAN_TILES * t + i
                    dve.wait_ge(y_done, m + 1)
                    if not (is_first(t) and i < 2):
                        dve.wait_ge(stored[i % 2], 16 * (2 * t + i // 2))
                    dve.scalar_tensor_tensor(out=result[i % 2][:, :], in0=y_ps[i % 2][:, :], scalar=N.ffn_factor[:, 2:3],
                                             in1=N.acc[:, bass.ds(m, 1), :].rearrange("p a e -> p (a e)"),
                                             op0=ALU.mult, op1=ALU.add).then_inc(result_ready, 1)

            spans(dve, body)

        @block.tensor
        def _(pe):
            def turn_tile(m, i):
                pe.wait_ge(normed_ready, m - SPAN_TILES + 1)
                at_least(pe, lo_ready, m - SPAN_TILES - 1)
                for kt in range(KT):
                    ins = pe.transpose(turn[i % 2][:, kt, :], normed[i][:, kt * P:(kt + 1) * P], N.ident[:, :])
                ins.then_inc(turned, 1)

            def turn_down(d):
                rows = chunk_rows(d)
                pe.wait_ge(down_ready, last_block(d) + 1)
                at_least(pe, down_out, d - 1)
                for kp in range(OCT // 2):
                    ins = pe.transpose(y_ps[d % 2][0:rows, :].bitcast(F16)[:, kp * P:(kp + 1) * P],
                                       down_rows[:, kp, d * P:d * P + rows], F.ident16[:, :])
                ins.then_inc(down_turned, 1)

            def body(t):
                if not is_first(t):
                    pe.wait_ge(lo_ready, SPAN_TILES * t)
                for c in range(HCHUNKS):
                    rows = chunk_rows(c)
                    n = HCHUNKS * t + c
                    for w, ps, free, done in ((0, gate_ps, silu_ready, gate_done), (1, up_ps, hid_ready, up_done)):
                        at_least(pe, free, n - 1 if c >= 1 else n)
                        for k in range(KT):
                            for part in (N.x_hi, N.x_lo):
                                ins = pe.matmul(ps[c % 2][0:rows, :], F.m[w][:, k, c * P:c * P + rows],
                                                part[:, k, bass.ds(t * SPAN, SPAN)],
                                                start=(k == 0 and part is N.x_hi), stop=(k == KT - 1 and part is N.x_lo))
                        ins.then_inc(done, 1)
                    if is_first(t):
                        for d in DOWN_TURNS.get(c, ()):
                            turn_down(d)
                    if not is_last(t) and c in (2, 4, 6, 8):
                        i = (c - 2) // 2
                        turn_tile(SPAN_TILES * (t + 1) + i, i)
                if is_first(t):
                    pe.wait_ge(down_out, HCHUNKS)
                for i in range(SPAN_TILES):
                    m = SPAN_TILES * t + i
                    at_least(pe, result_ready, m - 1)
                    for c in range(HCHUNKS):
                        rows = chunk_rows(c)
                        if i == 0:
                            pe.wait_ge(h_ready, HCHUNKS * t + c + 1)
                        for part in (h_hi, h_lo):
                            ins = pe.matmul(y_ps[i % 2][:, :], part[0:rows, c, i * P:(i + 1) * P], m_down[0:rows, c, :],
                                            start=(c == 0 and part is h_hi), stop=(c == HCHUNKS - 1 and part is h_lo))
                    ins.then_inc(y_done, 1)

            spans(pe, body)


def build(nc, x, ctx_in, pos, mask, wq, wk, wv, wo, w_gate, w_up, w_down, rope_table, out):
    N = Net()
    N.x = x.rearrange("b s e -> (b s) e")
    N.ctx = ctx_in.rearrange("b s e -> (b s) e")
    N.out = out.rearrange("b s e -> (b s) e")
    N.pos, N.mask, N.rope_table = pos, mask, rope_table
    N.wq, N.wk, N.wv, N.wo = wq, wk, wv, wo
    N.w_gate, N.w_up, N.w_down = w_gate, w_up, w_down
    with ExitStack() as ctx:
        N.sems = ctx

        def sb(name, shape, dt):
            return ctx.enter_context(nc.sbuf_tensor(name, shape, dt))

        N.acc = sb("acc", [P, TILES, EMB], F32)
        N.x_hi, N.x_lo = sb("x_hi", [P, KT, TOKENS], F16), sb("x_lo", [P, KT, TOKENS], F16)
        N.c_hi, N.c_lo = sb("c_hi", [P, KT, TOKENS], F16), sb("c_lo", [P, KT, TOKENS], F16)
        N.ident = sb("ident", [P, P], F32)
        N.eps_tile = sb("eps_tile", [P, 1], F32)
        N.stats = sb("stats", [P, TILES, 6], F32)
        N.ffn_factor = sb("ffn_factor", [P, 3], F32)
        N.c_scale, N.c_inv = sb("c_scale", [P, SPANS], F32), sb("c_inv", [P, SPANS], F32)
        N.consts_ready = ctx.enter_context(nc.semaphore("consts_ready"))


        def sem(name):
            return ctx.enter_context(nc.semaphore(name))

        N.ffn = FfnWeights(sb, sem, N)
        with ExitStack() as attention:
            def sba(name, shape, dt):
                return attention.enter_context(nc.sbuf_tensor(name, shape, dt))

            N.cos_t, N.sin_t = sba("cos_t", [P, TOKENS], F32), sba("sin_t", [P, TOKENS], F32)
            N.pred = sba("pred", [P, BATCH, SEQ], U8)
            N.weights = Weights(nc, sba, sem, N)
            N.ffn.place(N.weights)
            prepare(nc, N)
            attend(nc, N)
        feed(nc, N)


_INS = ["x", "ctx_4096", "pos_BxS2", "mask_BxSxS2_ik0", "L0_xattn_Wq", "L0_xattn_Wk", "L0_xattn_Wv", "L0_xattn_Wo",
        "L0_ffn_w_gate", "L0_ffn_w_up", "L0_ffn_w_down"]


def rope_rows():
    import numpy as np
    inv_freq = (np.float32(1.0) / np.float32(THETA) ** (np.arange(0, HEAD_DIM, 2, dtype=np.float32) / np.float32(HEAD_DIM))).astype(np.float32)
    ang = np.arange(MAX_POS, dtype=np.float32)[:, None] * inv_freq[None, :]
    return np.concatenate([np.cos(ang), np.cos(ang), np.sin(ang), -np.sin(ang)], axis=1).astype(np.float32)


def kernel(**inputs):
    import numpy as np
    import concourse.bacc as bacc
    from concourse.bass_utils import run_bass_kernel_spmd

    nc = bacc.Bacc("TRN2", target_bir_lowering=False, num_devices=1)
    arrays, args = {}, []
    for name in _INS:
        a = np.ascontiguousarray(inputs[name])
        arrays[f"in_{name}"] = a
        args.append(nc.dram_tensor(f"in_{name}", a.shape, mybir.dt.from_np(a.dtype), kind="ExternalInput").ap())
    table = rope_rows()
    arrays["rope_table"] = table
    args.append(nc.dram_tensor("rope_table", table.shape, F32, kind="ExternalInput").ap())
    args.append(nc.dram_tensor("out", (BATCH, SEQ, EMB), F32, kind="ExternalOutput").ap())
    build(nc, *args)
    r = run_bass_kernel_spmd(nc, [arrays], core_ids=[0])
    return r.results[0]["out"]
```
